# Optimizing a Trainium2 kernel written in Bass

```python
import numpy as np
import jax
import jax.numpy as jnp

def _softmax(x, axis=-1):
    return jax.nn.softmax(x, axis=axis)

def _gelu(x):
    return jax.nn.gelu(x, approximate=True)

def _silu(x):
    return jax.nn.silu(x)

def _sigmoid(x):
    return jax.nn.sigmoid(x)

def _layernorm(x, axis=-1, eps=1e-05):
    m = jnp.mean(x, axis=axis, keepdims=True)
    v = jnp.var(x, axis=axis, keepdims=True)
    return (x - m) / jnp.sqrt(v + eps)

def _scatter_add(tgt, idx, src, axis=0):
    return tgt.at[idx].add(src)

def _segment_sum(src, seg, n):
    return jax.ops.segment_sum(src, seg, n)
kernel_name = 'mk_flamingo_gated_d4_seqx_r8_c67b0b'

def setup_inputs(seed: int=0):
    np.random.seed(seed)
    _w = jnp.asarray

    def _rec_inputs():
        import jax
        import jax.numpy as jnp
        _rk = jax.random.key(seed)
        x = -0.000125 + 0.9999 * jax.random.normal(jax.random.fold_in(_rk, 1), (64, 64, 128), jnp.float32)
        _lenS = 64 - jax.random.randint(jax.random.fold_in(_rk, 7), (64,), 0, max(1, 64 // 4) + 1, jnp.int32)
        _lenS2 = 64 - jax.random.randint(jax.random.fold_in(_rk, 8), (64,), 0, max(1, 64 // 4) + 1, jnp.int32)
        _ctx_1024P = jax.random.normal(jax.random.fold_in(_rk, 11), (64, 16, 128), jnp.float32)
        _ctx_1024c = jax.random.dirichlet(jax.random.fold_in(_rk, 511), 0.3 * jnp.ones((16,), jnp.float32), (64, 64))
        _ctx_1024t = jnp.einsum('bsk,bkd->bsd', _ctx_1024c, _ctx_1024P)
        _ctx_1024t = _ctx_1024t * jax.lax.rsqrt(jnp.mean(jnp.square(_ctx_1024t)) + 1e-12) * 0.953939
        ctx_1024 = -1.52775e-05 + 0.999936 * (_ctx_1024t + 0.3 * jax.random.normal(jax.random.fold_in(_rk, 611), (64, 64, 128), jnp.float32))
        _g = jax.random.normal(jax.random.fold_in(_rk, 9001), (2, 4), jnp.float32)
        _g = jnp.sign(_g) * jnp.maximum(jnp.abs(_g), 1.0) + (_g == 0) * 1.0
        g_xattn = _g[0]
        g_ffn = _g[1]
        return (x, ctx_1024, g_xattn, g_ffn)
    x, ctx_1024, g_xattn, g_ffn = _rec_inputs()

    def _L0_xattn_setup():
        import jax, jax.numpy as jnp
        import numpy as np
        D_MODEL = 128
        HEAD_SIZE = 128
        CONTEXT_SIZE = 128
        key = jax.random.key(seed)
        kq, kk, kv, kwq, kwk, kwv = jax.random.split(key, 6)
        B, S = (32, 128)
        scale = 1.0 / np.sqrt(D_MODEL)
        return {'query': jax.random.normal(kq, (B, S, D_MODEL), dtype=jnp.float32), 'key': jax.random.normal(kk, (B, S, D_MODEL), dtype=jnp.float32), 'value': jax.random.normal(kv, (B, S, D_MODEL), dtype=jnp.float32), 'w_q': jax.random.normal(kwq, (D_MODEL, HEAD_SIZE), dtype=jnp.float32) * scale, 'w_k': jax.random.normal(kwk, (D_MODEL, HEAD_SIZE), dtype=jnp.float32) * scale, 'w_v': jax.random.normal(kwv, (D_MODEL, HEAD_SIZE), dtype=jnp.float32) * scale, 'mask': 1}
    _L0_xattn_all = _L0_xattn_setup()
    _L0_xattn_in = {k: v for k, v in _L0_xattn_all.items() if k in ('w_q', 'w_k', 'w_v')}
    del _L0_xattn_all

    def _L0_ffn_setup():
        import jax, jax.numpy as jnp
        import numpy as np
        B, S, D_MODEL, D_HIDDEN = (4, 256, 128, 512)

        def act_quant(x):
            scale = 127.0 / jnp.clip(jnp.max(jnp.abs(x), axis=-1, keepdims=True), 1e-05)
            return jnp.clip(jnp.round(x * scale), -128, 127) / scale

        def weight_quant(w):
            scale = 1.0 / jnp.clip(jnp.mean(jnp.abs(w)), 1e-05)
            return jnp.clip(jnp.round(w * scale), -1, 1) / scale

        def bit_linear(x, w):
            xq = x + jax.lax.stop_gradient(act_quant(x) - x)
            wq = w + jax.lax.stop_gradient(weight_quant(w) - w)
            return jnp.einsum('bsd,hd->bsh', xq, wq)

        def depthwise_conv1d(x_bcl, w, b):
            y = jax.lax.conv_general_dilated(x_bcl, w, window_strides=(1,), padding=[(1, 1)], dimension_numbers=('NCH', 'OIH', 'NCH'), feature_group_count=x_bcl.shape[1])
            return y + b[None, :, None]
        key = jax.random.key(seed)
        ks = jax.random.split(key, 5)
        lim1 = 1.0 / np.sqrt(D_MODEL)
        lim2 = 1.0 / np.sqrt(D_HIDDEN)
        limc = 1.0 / np.sqrt(3.0)
        return {'x': jax.random.normal(ks[0], (B, S, D_MODEL), dtype=jnp.float32), 'w1': jax.random.uniform(ks[1], (D_HIDDEN, D_MODEL), jnp.float32, -lim1, lim1), 'conv_w': jax.random.uniform(ks[2], (D_HIDDEN, 1, 3), jnp.float32, -limc, limc), 'conv_b': jax.random.uniform(ks[3], (D_HIDDEN,), jnp.float32, -limc, limc), 'w2': jax.random.uniform(ks[4], (D_MODEL, D_HIDDEN), jnp.float32, -lim2, lim2)}
    _L0_ffn_all = _L0_ffn_setup()
    _L0_ffn_in = {k: v for k, v in _L0_ffn_all.items() if k in ('w1', 'conv_w', 'conv_b', 'w2')}
    del _L0_ffn_all

    def _L1_xattn_setup():
        import jax, jax.numpy as jnp
        import numpy as np
        HEAD_DIM = 64
        key = jax.random.key(seed)
        ks = jax.random.split(key, 6)
        b, q_len, kv_len, emb, h, d = (4, 256, 256, 128, 16, HEAD_DIM)
        scale = 1.0 / np.sqrt(emb)
        return {'inputs_q': jax.random.normal(ks[0], (b, q_len, emb), jnp.float32), 'inputs_kv': jax.random.normal(ks[1], (b, kv_len, emb), jnp.float32), 'Wq': jax.random.normal(ks[2], (emb, h, d), jnp.float32) * scale, 'Wk': jax.random.normal(ks[3], (emb, h, d), jnp.float32) * scale, 'Wv': jax.random.normal(ks[4], (emb, h, d), jnp.float32) * scale, 'Wo': jax.random.normal(ks[5], (h, d, emb), jnp.float32) * scale}
    _L1_xattn_all = _L1_xattn_setup()
    _L1_xattn_in = {k: v for k, v in _L1_xattn_all.items() if k in ('Wq', 'Wk', 'Wv', 'Wo')}
    del _L1_xattn_all

    def _L1_ffn_setup():
        import jax, jax.numpy as jnp
        import numpy as np
        B, S, H, I, E = (2, 512, 128, 64, 8)
        key = jax.random.key(seed)
        ks = jax.random.split(key, 5)
        scale_h = 1.0 / np.sqrt(H)
        scale_i = 1.0 / np.sqrt(I)
        return {'hidden_states': jax.random.normal(ks[0], (B, S, H), dtype=jnp.float32), 'gate_w': jax.random.normal(ks[1], (E, H), dtype=jnp.float32) * scale_h, 'w_gate': jax.random.normal(ks[2], (E, I, H), dtype=jnp.float32) * scale_h, 'w_up': jax.random.normal(ks[3], (E, I, H), dtype=jnp.float32) * scale_h, 'w_down': jax.random.normal(ks[4], (E, H, I), dtype=jnp.float32) * scale_i}
    _L1_ffn_all = _L1_ffn_setup()
    _L1_ffn_in = {k: v for k, v in _L1_ffn_all.items() if k in ('gate_w', 'w_gate', 'w_up', 'w_down')}
    del _L1_ffn_all

    def _L2_xattn_setup():
        import jax, jax.numpy as jnp
        import numpy as np
        B, S, H, NH = (2, 256, 128, 16)
        DK = H // NH
        key = jax.random.key(seed)
        ks = jax.random.split(key, 11)
        sc = 1.0 / np.sqrt(H)
        return {'q': jax.random.normal(ks[0], (B, S, H), jnp.float32), 'v': jax.random.normal(ks[1], (B, S, H), jnp.float32), 'k': jax.random.normal(ks[2], (B, S, H), jnp.float32), 'Wq': jax.random.normal(ks[3], (H, H), jnp.float32) * sc, 'bq': jax.random.normal(ks[4], (H,), jnp.float32) * 0.01, 'Wk': jax.random.normal(ks[5], (H, H), jnp.float32) * sc, 'bk': jax.random.normal(ks[6], (H,), jnp.float32) * 0.01, 'Wv': jax.random.normal(ks[7], (H, H), jnp.float32) * sc, 'bv': jax.random.normal(ks[8], (H,), jnp.float32) * 0.01, 'Wo': jax.random.normal(ks[9], (H, H), jnp.float32) * sc, 'bo': jax.random.normal(ks[10], (H,), jnp.float32) * 0.01}
    _L2_xattn_all = _L2_xattn_setup()
    _L2_xattn_in = {k: v for k, v in _L2_xattn_all.items() if k in ('Wq', 'bq', 'Wk', 'bk', 'Wv', 'bv', 'Wo', 'bo')}
    del _L2_xattn_all

    def _L2_ffn_setup():
        import jax, jax.numpy as jnp
        import numpy as np
        DIM = 128

        def _reference_tuple_inner(x, W_r, W_k, W_v, mu_r, mu_k):
            B, T, C = x.shape
            x_prev = jnp.concatenate([jnp.zeros((B, 1, C), x.dtype), x[:, :-1, :]], axis=1)
            xr = mu_r * x + (1.0 - mu_r) * x_prev
            xk = mu_k * x + (1.0 - mu_k) * x_prev
            r = jax.nn.sigmoid(jnp.einsum('btc,dc->btd', xr, W_r))
            k = jnp.einsum('btc,dc->btd', xk, W_k)
            k_act = jnp.square(jax.nn.relu(k))
            out = r * jnp.einsum('btc,dc->btd', k_act, W_v)
            new_state = x[:, -1, :]
            return (out, new_state)
        key = jax.random.key(seed)
        ks = jax.random.split(key, 6)
        B, T, C = (8, 256, DIM)
        x = jax.random.normal(ks[0], (B, T, C), dtype=jnp.float32)
        s = 1.0 / np.sqrt(C)
        W_r = jax.random.uniform(ks[1], (C, C), jnp.float32, -s, s)
        W_k = jax.random.uniform(ks[2], (C, C), jnp.float32, -s, s)
        W_v = jax.random.uniform(ks[3], (C, C), jnp.float32, -s, s)
        mu_r = jax.random.uniform(ks[4], (C,), jnp.float32)
        mu_k = jax.random.uniform(ks[5], (C,), jnp.float32)
        return {'x': x, 'W_r': W_r, 'W_k': W_k, 'W_v': W_v, 'mu_r': mu_r, 'mu_k': mu_k}
    _L2_ffn_all = _L2_ffn_setup()
    _L2_ffn_in = {k: v for k, v in _L2_ffn_all.items() if k in ('W_r', 'W_k', 'W_v', 'mu_r', 'mu_k')}
    del _L2_ffn_all

    def _L3_xattn_setup():
        import jax, jax.numpy as jnp
        import numpy as np
        EMBED_DIM = 128
        NHEAD = 16
        HEAD_DIM = EMBED_DIM // NHEAD
        BASE = 10000.0

        def rope_tables(seq_len, dim):
            inv_freq = 1.0 / BASE ** (jnp.arange(0, dim, 2, dtype=jnp.float32) / dim)
            t = jnp.arange(seq_len, dtype=jnp.float32)
            freqs = jnp.einsum('i,j->ij', t, inv_freq)
            return (jnp.cos(freqs), jnp.sin(freqs))

        def apply_rope(x, cos, sin):
            x1, x2 = jnp.split(x, 2, axis=-1)
            return jnp.concatenate((x1 * cos - x2 * sin, x1 * sin + x2 * cos), axis=-1)
        key = jax.random.key(seed)
        ks = jax.random.split(key, 7)
        B, S, E = (2, 256, EMBED_DIM)
        scale = 1.0 / np.sqrt(E)
        return {'query': jax.random.normal(ks[0], (B, S, E), dtype=jnp.float32), 'key': jax.random.normal(ks[1], (B, S, E), dtype=jnp.float32), 'value': jax.random.normal(ks[2], (B, S, E), dtype=jnp.float32), 'Wq': jax.random.normal(ks[3], (E, E), dtype=jnp.float32) * scale, 'Wk': jax.random.normal(ks[4], (E, E), dtype=jnp.float32) * scale, 'Wv': jax.random.normal(ks[5], (E, E), dtype=jnp.float32) * scale, 'Wo': jax.random.normal(ks[6], (E, E), dtype=jnp.float32) * scale}
    _L3_xattn_all = _L3_xattn_setup()
    _L3_xattn_in = {k: v for k, v in _L3_xattn_all.items() if k in ('Wq', 'Wk', 'Wv', 'Wo')}
    del _L3_xattn_all

    def _L3_ffn_setup():
        import jax, jax.numpy as jnp
        import numpy as np
        LORA_DIM = 16
        LORA_TOKEN_INDEX = 1
        B, S, D, H = (4, 256, 128, 512)
        key = jax.random.key(seed)
        ks = jax.random.split(key, 6)
        x = jax.random.normal(ks[0], (B, S, D), dtype=jnp.float32)
        W1 = jax.random.normal(ks[1], (H, D), dtype=jnp.float32) * 0.02
        b1 = jnp.zeros((H,), dtype=jnp.float32)
        W2 = jax.random.normal(ks[2], (D, H), dtype=jnp.float32) * 0.02
        b2 = jnp.zeros((D,), dtype=jnp.float32)
        scale = jnp.asarray(0.001, dtype=jnp.float32)
        return {'x': x, 'W1': W1, 'b1': b1, 'W2': W2, 'b2': b2, 'scale': scale}
    _L3_ffn_all = _L3_ffn_setup()
    _L3_ffn_in = {k: v for k, v in _L3_ffn_all.items() if k in ('W1', 'b1', 'W2', 'b2', 'scale')}
    del _L3_ffn_all
    return {'x': x, 'ctx_1024': ctx_1024, 'g_xattn': g_xattn, 'g_ffn': g_ffn, 'L0_xattn_w_q': _L0_xattn_in['w_q'], 'L0_xattn_w_k': _L0_xattn_in['w_k'], 'L0_xattn_w_v': _L0_xattn_in['w_v'], 'L0_ffn_w1': _L0_ffn_in['w1'], 'L0_ffn_conv_w': _L0_ffn_in['conv_w'], 'L0_ffn_conv_b': _L0_ffn_in['conv_b'], 'L0_ffn_w2': _L0_ffn_in['w2'], 'L1_xattn_Wq': _L1_xattn_in['Wq'], 'L1_xattn_Wk': _L1_xattn_in['Wk'], 'L1_xattn_Wv': _L1_xattn_in['Wv'], 'L1_xattn_Wo': _L1_xattn_in['Wo'], 'L1_ffn_gate_w': _L1_ffn_in['gate_w'], 'L1_ffn_w_gate': _L1_ffn_in['w_gate'], 'L1_ffn_w_up': _L1_ffn_in['w_up'], 'L1_ffn_w_down': _L1_ffn_in['w_down'], 'L2_xattn_Wq': _L2_xattn_in['Wq'], 'L2_xattn_bq': _L2_xattn_in['bq'], 'L2_xattn_Wk': _L2_xattn_in['Wk'], 'L2_xattn_bk': _L2_xattn_in['bk'], 'L2_xattn_Wv': _L2_xattn_in['Wv'], 'L2_xattn_bv': _L2_xattn_in['bv'], 'L2_xattn_Wo': _L2_xattn_in['Wo'], 'L2_xattn_bo': _L2_xattn_in['bo'], 'L2_ffn_W_r': _L2_ffn_in['W_r'], 'L2_ffn_W_k': _L2_ffn_in['W_k'], 'L2_ffn_W_v': _L2_ffn_in['W_v'], 'L2_ffn_mu_r': _L2_ffn_in['mu_r'], 'L2_ffn_mu_k': _L2_ffn_in['mu_k'], 'L3_xattn_Wq': _L3_xattn_in['Wq'], 'L3_xattn_Wk': _L3_xattn_in['Wk'], 'L3_xattn_Wv': _L3_xattn_in['Wv'], 'L3_xattn_Wo': _L3_xattn_in['Wo'], 'L3_ffn_W1': _L3_ffn_in['W1'], 'L3_ffn_b1': _L3_ffn_in['b1'], 'L3_ffn_W2': _L3_ffn_in['W2'], 'L3_ffn_b2': _L3_ffn_in['b2'], 'L3_ffn_scale': _L3_ffn_in['scale']}

def reference(x, ctx_1024, g_xattn, g_ffn, L0_xattn_w_q, L0_xattn_w_k, L0_xattn_w_v, L0_ffn_w1, L0_ffn_conv_w, L0_ffn_conv_b, L0_ffn_w2, L1_xattn_Wq, L1_xattn_Wk, L1_xattn_Wv, L1_xattn_Wo, L1_ffn_gate_w, L1_ffn_w_gate, L1_ffn_w_up, L1_ffn_w_down, L2_xattn_Wq, L2_xattn_bq, L2_xattn_Wk, L2_xattn_bk, L2_xattn_Wv, L2_xattn_bv, L2_xattn_Wo, L2_xattn_bo, L2_ffn_W_r, L2_ffn_W_k, L2_ffn_W_v, L2_ffn_mu_r, L2_ffn_mu_k, L3_xattn_Wq, L3_xattn_Wk, L3_xattn_Wv, L3_xattn_Wo, L3_ffn_W1, L3_ffn_b1, L3_ffn_W2, L3_ffn_b2, L3_ffn_scale):
    import jax
    import jax.numpy as jnp

    def _L0_xattn_ref(query, key, value, w_q, w_k, w_v, mask):
        import jax, jax.numpy as jnp
        import numpy as np
        D_MODEL = 128
        HEAD_SIZE = 128
        CONTEXT_SIZE = 128
        q = jnp.einsum('bsd,dh->bsh', query, w_q)
        k = jnp.einsum('bsd,dh->bsh', key, w_k)
        v = jnp.einsum('bsd,dh->bsh', value, w_v)
        scale = 1.0 / np.sqrt(query.shape[-1]).astype(np.float32)
        scores = jnp.einsum('bqh,bkh->bqk', q, k) * scale
        if mask:
            S = scores.shape[1]
            causal = jnp.tril(jnp.ones((S, S), dtype=bool))
            scores = jnp.where(causal, scores, -jnp.inf)
        attn = jax.nn.softmax(scores, axis=-1)
        out = jnp.einsum('bqk,bkh->bqh', attn, v)
        return out

    def _L0_ffn_ref(x, w1, conv_w, conv_b, w2):
        import jax, jax.numpy as jnp
        import numpy as np
        B, S, D_MODEL, D_HIDDEN = (4, 256, 128, 512)

        def act_quant(x):
            scale = 127.0 / jnp.clip(jnp.max(jnp.abs(x), axis=-1, keepdims=True), 1e-05)
            return jnp.clip(jnp.round(x * scale), -128, 127) / scale

        def weight_quant(w):
            scale = 1.0 / jnp.clip(jnp.mean(jnp.abs(w)), 1e-05)
            return jnp.clip(jnp.round(w * scale), -1, 1) / scale

        def bit_linear(x, w):
            xq = x + jax.lax.stop_gradient(act_quant(x) - x)
            wq = w + jax.lax.stop_gradient(weight_quant(w) - w)
            return jnp.einsum('bsd,hd->bsh', xq, wq)

        def depthwise_conv1d(x_bcl, w, b):
            y = jax.lax.conv_general_dilated(x_bcl, w, window_strides=(1,), padding=[(1, 1)], dimension_numbers=('NCH', 'OIH', 'NCH'), feature_group_count=x_bcl.shape[1])
            return y + b[None, :, None]
        h = bit_linear(x, w1)
        h = depthwise_conv1d(h.transpose(0, 2, 1), conv_w, conv_b)
        h = h.transpose(0, 2, 1)
        h = jax.nn.silu(h)
        return bit_linear(h, w2)

    def _L1_xattn_ref(inputs_q, inputs_kv, Wq, Wk, Wv, Wo):
        import jax, jax.numpy as jnp
        import numpy as np
        HEAD_DIM = 64
        depth_scale = jnp.sqrt(jnp.asarray(HEAD_DIM, inputs_q.dtype))
        q = jnp.einsum('bqe,ehd->bqhd', inputs_q, Wq) / depth_scale
        k = jnp.einsum('bke,ehd->bkhd', inputs_kv, Wk)
        v = jnp.einsum('bke,ehd->bkhd', inputs_kv, Wv)
        attn_weights = jnp.einsum('bqhd,bkhd->bhqk', q, k)
        attn_weights = jax.nn.softmax(attn_weights, axis=-1)
        out = jnp.einsum('bhqk,bkhd->bqhd', attn_weights, v)
        return jnp.einsum('bqhd,hde->bqe', out, Wo)

    def _L1_ffn_ref(hidden_states, gate_w, w_gate, w_up, w_down):
        import jax, jax.numpy as jnp
        import numpy as np
        B, S, H, I, E = (2, 512, 128, 64, 8)
        b, s, h = hidden_states.shape
        x = hidden_states.reshape(-1, h)
        logits = x @ gate_w.T
        top_v = jnp.max(logits, axis=-1)
        sel = jnp.argmax(logits, axis=-1)
        rw = jax.nn.sigmoid(top_v)
        out = jnp.zeros_like(x)
        n_exp = gate_w.shape[0]
        for e in range(n_exp):
            mask = (sel == e).astype(x.dtype)
            xs = x * (rw * mask)[:, None]
            g = xs @ w_gate[e].T
            u = xs @ w_up[e].T
            out = out + u * jax.nn.silu(g) @ w_down[e].T
        return out.reshape(b, s, h)

    def _L2_xattn_ref(q, v, k, Wq, bq, Wk, bk, Wv, bv, Wo, bo):
        import jax, jax.numpy as jnp
        import numpy as np
        B, S, H, NH = (2, 256, 128, 16)
        DK = H // NH
        b, s, h = q.shape
        qh = (q @ Wq.T + bq).reshape(b, s, NH, DK).transpose(0, 2, 1, 3)
        kh = (k @ Wk.T + bk).reshape(b, s, NH, DK).transpose(0, 2, 1, 3)
        vh = (v @ Wv.T + bv).reshape(b, s, NH, DK).transpose(0, 2, 1, 3)
        scores = jnp.einsum('bhqd,bhkd->bhqk', qh, kh) / jnp.sqrt(jnp.asarray(DK, qh.dtype))
        probs = jax.nn.softmax(scores, axis=-1)
        ctx = jnp.einsum('bhqk,bhkd->bhqd', probs, vh)
        concat = ctx.transpose(0, 2, 1, 3).reshape(b, s, h)
        return concat @ Wo.T + bo

    def _L2_ffn_ref(x, W_r, W_k, W_v, mu_r, mu_k):
        import jax, jax.numpy as jnp
        import numpy as np
        DIM = 128

        def _reference_tuple_inner(x, W_r, W_k, W_v, mu_r, mu_k):
            B, T, C = x.shape
            x_prev = jnp.concatenate([jnp.zeros((B, 1, C), x.dtype), x[:, :-1, :]], axis=1)
            xr = mu_r * x + (1.0 - mu_r) * x_prev
            xk = mu_k * x + (1.0 - mu_k) * x_prev
            r = jax.nn.sigmoid(jnp.einsum('btc,dc->btd', xr, W_r))
            k = jnp.einsum('btc,dc->btd', xk, W_k)
            k_act = jnp.square(jax.nn.relu(k))
            out = r * jnp.einsum('btc,dc->btd', k_act, W_v)
            new_state = x[:, -1, :]
            return (out, new_state)
        return _reference_tuple_inner(x, W_r, W_k, W_v, mu_r, mu_k)[0]

    def _L3_xattn_ref(query, key, value, Wq, Wk, Wv, Wo):
        import jax, jax.numpy as jnp
        import numpy as np
        EMBED_DIM = 128
        NHEAD = 16
        HEAD_DIM = EMBED_DIM // NHEAD
        BASE = 10000.0

        def rope_tables(seq_len, dim):
            inv_freq = 1.0 / BASE ** (jnp.arange(0, dim, 2, dtype=jnp.float32) / dim)
            t = jnp.arange(seq_len, dtype=jnp.float32)
            freqs = jnp.einsum('i,j->ij', t, inv_freq)
            return (jnp.cos(freqs), jnp.sin(freqs))

        def apply_rope(x, cos, sin):
            x1, x2 = jnp.split(x, 2, axis=-1)
            return jnp.concatenate((x1 * cos - x2 * sin, x1 * sin + x2 * cos), axis=-1)
        B, Sq, E = query.shape
        Skv = key.shape[1]
        H, D = (NHEAD, HEAD_DIM)
        q = (query @ Wq.T).reshape(B, Sq, H, D).transpose(0, 2, 1, 3)
        k = (key @ Wk.T).reshape(B, Skv, H, D).transpose(0, 2, 1, 3)
        v = (value @ Wv.T).reshape(B, Skv, H, D).transpose(0, 2, 1, 3)
        cos, sin = rope_tables(Sq, D)
        q = apply_rope(q, cos, sin)
        k = apply_rope(k, cos, sin)
        scores = jnp.einsum('bhqd,bhkd->bhqk', q, k) / jnp.sqrt(jnp.asarray(D, q.dtype))
        probs = jax.nn.softmax(scores, axis=-1)
        out = jnp.einsum('bhqk,bhkd->bhqd', probs, v)
        out = out.transpose(0, 2, 1, 3).reshape(B, Sq, E)
        return out @ Wo.T

    def _L3_ffn_ref(x, W1, b1, W2, b2, scale):
        import jax, jax.numpy as jnp
        import numpy as np
        LORA_DIM = 16
        LORA_TOKEN_INDEX = 1
        B, S, D, H = (4, 256, 128, 512)
        Bx, Sx, Dx = x.shape
        Hx = W1.shape[0]
        lt = jax.lax.dynamic_slice_in_dim(x, LORA_TOKEN_INDEX, LORA_DIM, axis=1)
        even = lt[:, ::2, :]
        odd = lt[:, 1::2, :]
        m1 = (even[:, :4, :, None] * odd[:, :4, None, :]).reshape(Bx, Hx, Dx)
        m2 = (even[:, 4:, :, None] * odd[:, 4:, None, :]).reshape(Bx, Dx, Hx)
        h = jnp.einsum('bsd,hd->bsh', x, W1) + scale * jnp.einsum('bsd,bhd->bsh', x, m1) + b1
        h = jax.nn.gelu(h, approximate=False)
        out = jnp.einsum('bsh,oh->bso', h, W2) + scale * jnp.einsum('bsh,boh->bso', h, m2) + b2
        return out
    x = x + jnp.tanh(g_xattn[0]) * _L0_xattn_ref(_layernorm(x, axis=-1), ctx_1024, ctx_1024, L0_xattn_w_q, L0_xattn_w_k, L0_xattn_w_v, 1)
    x = x + jnp.tanh(g_ffn[0]) * _L0_ffn_ref(_layernorm(x, axis=-1), L0_ffn_w1, L0_ffn_conv_w, L0_ffn_conv_b, L0_ffn_w2)
    x = x + jnp.tanh(g_xattn[1]) * _L1_xattn_ref(_layernorm(x, axis=-1), ctx_1024, L1_xattn_Wq, L1_xattn_Wk, L1_xattn_Wv, L1_xattn_Wo)
    x = x + jnp.tanh(g_ffn[1]) * _L1_ffn_ref(_layernorm(x, axis=-1), L1_ffn_gate_w, L1_ffn_w_gate, L1_ffn_w_up, L1_ffn_w_down)
    x = x + jnp.tanh(g_xattn[2]) * _L2_xattn_ref(_layernorm(x, axis=-1), ctx_1024, ctx_1024, L2_xattn_Wq, L2_xattn_bq, L2_xattn_Wk, L2_xattn_bk, L2_xattn_Wv, L2_xattn_bv, L2_xattn_Wo, L2_xattn_bo)
    x = x + jnp.tanh(g_ffn[2]) * _L2_ffn_ref(_layernorm(x, axis=-1), L2_ffn_W_r, L2_ffn_W_k, L2_ffn_W_v, L2_ffn_mu_r, L2_ffn_mu_k)
    x = x + jnp.tanh(g_xattn[3]) * _L3_xattn_ref(_layernorm(x, axis=-1), ctx_1024, ctx_1024, L3_xattn_Wq, L3_xattn_Wk, L3_xattn_Wv, L3_xattn_Wo)
    x = x + jnp.tanh(g_ffn[3]) * _L3_ffn_ref(_layernorm(x, axis=-1), L3_ffn_W1, L3_ffn_b1, L3_ffn_W2, L3_ffn_b2, L3_ffn_scale)
    return x

_drawn_inputs = setup_inputs


def setup_inputs(seed=0):
    import zlib

    import numpy as np

    out = dict(_drawn_inputs(seed))
    spreads = {'L3_ffn_b1': (0.0, 0.798), 'L3_ffn_b2': (0.0, 0.1)}
    factors = {'g_ffn': 7.847,
     'L2_xattn_bq': 57.614,
     'L2_xattn_bk': 64.0,
     'L2_xattn_bv': 8.0,
     'L2_xattn_bo': 8.0,
     'L2_ffn_W_r': 5.708,
     'L2_ffn_mu_r': 8.0,
     'L2_ffn_mu_k': 4.09}
    for name, (base, spread) in spreads.items():
        noise = np.random.default_rng([zlib.crc32(name.encode()), seed]).standard_normal(out[name].shape)
        drawn = base * np.exp(spread * noise) if base else spread * noise
        out[name] = jnp.asarray(drawn.astype(out[name].dtype))
    for name, factor in factors.items():
        out[name] = (out[name] * factor).astype(out[name].dtype)
    return out
```

```python
from contextlib import ExitStack

import numpy as np

import concourse.bass as bass
from concourse import mybir

F32 = mybir.dt.float32
BF16 = mybir.dt.bfloat16
ALU = mybir.AluOpType
ACT = mybir.ActivationFunctionType
AX = mybir.AxisListType

P = 128
SEQ = 64
NB = P // SEQ
NT = 32
NH = 16
PAIRS = NH // 2
HID = 512
CH = HID // P
NE = 8
EPS = 1e-5
MAGIC = 12582912.0


def live(s, lag):
    return not isinstance(s, int) or 0 <= s - lag < NT


def exists(t):
    return not isinstance(t, int) or t >= 0


def moved(t, p):
    return t * 8 + (16 - 8 * p)


def run_steps(eng, step, last_lag=4):
    peel = last_lag + 2 + last_lag % 2
    for s in range(peel):
        step(s, s % 2)
    with eng.Fori(peel, NT - 1, 2) as s:
        step(s, 0)
        step(s + 1, 1)
    for s in range(NT, NT + last_lag):
        step(s, s % 2)


def semaphores(nc, c):
    taken = []

    def close():
        nc.clear_and_free_semaphores(taken)
        nc.all_engine_barrier()

    def allocate(name):
        taken.append(nc.alloc_semaphore(name=name))
        return taken[-1]

    c.callback(close)
    return allocate


class Stream:

    def __init__(self, nc, c, name, src, dst, ctx=None):
        self.nc, self.c, self.name, self.src, self.dst, self.ctx_src = nc, c, name, src, dst, ctx
        self.allocate = semaphores(nc, c)
        self.xin = self.two("xin", [P, P])
        self.xres = self.two("xres", [P, P])
        self.xout = self.two("xout", [P, P])
        self.xh = self.two("xh", [P, P])
        self.xT = self.two("xT", [P, P])
        self.bn = self.two("bn", [P, 6])
        self.mv = self.two("mv", [P, 2])
        self.var = self.two("var", [P, 1])
        self.rstd = self.two("rstd", [P, 1])
        self.x_loaded = self.sems("x_loaded")
        self.res_loaded = self.sems("res_loaded")
        self.stored = self.sems("stored")
        if ctx is not None:
            self.ctxT = self.two("ctxT", [P, P])
            self.ctx_loaded = self.sems("ctx_loaded")
            self.ctx_used = None
        self.bn_done = self.sem("bn_done")
        self.bn_waited = self.sem("bn_waited")
        self.mv_done = self.sem("mv_done")
        self.var_done = self.sem("var_done")
        self.rstd_done = self.sem("rstd_done")
        self.xh_done = self.sem("xh_done")
        self.xtr_done = self.sem("xtr_done")
        self.xT_done = self.sem("xT_done")
        self.o_done = self.sem("o_done")
        self.res_done = self.sem("res_done")

    def sem(self, n):
        return self.allocate(f"{self.name}_{n}")

    def sems(self, n):
        return [self.sem(f"{n}{i}") for i in range(2)]

    def sb(self, n, shape, dt=F32):
        return self.c.enter_context(self.nc.sbuf_tensor(f"{self.name}_{n}", shape, dt))

    def two(self, n, shape, dt=F32):
        return [self.sb(f"{n}{i}", shape, dt) for i in range(2)]

    def bank(self, n, dt=F32):
        return self.c.enter_context(
            self.nc.psum_tensor(f"{self.name}_{n}", [P, 512 if dt == F32 else 1024], dt))

    def own_wait(self, eng, t):
        if not isinstance(t, int):
            eng.wait_ge(self.x_loaded[0], 16)

    def load(self, sp, t, p, row):
        self.own_wait(sp, t)
        if exists(t - 2):
            sp.wait_ge(self.xh_done, t - 1)
        sp.dma_start(self.xin[p][:, :], self.src(row)).then_inc(self.x_loaded[p], 16)
        if self.ctx_src is not None:
            self.own_wait(sp, t)
            if exists(t - 2):
                sp.wait_ge(self.ctx_used[0], self.ctx_used[1] * (t - 1))
            sp.dma_start(self.ctxT[p][:, :], self.ctx_src(row)).then_inc(self.ctx_loaded[p], 16)

    def load_res(self, sp, t, p, row):
        self.own_wait(sp, t)
        if exists(t - 2):
            sp.wait_ge(self.res_done, t - 1)
        sp.dma_start(self.xres[p][:, :], self.src(row)).then_inc(self.res_loaded[p], 16)

    def store(self, sp, t, p, row):
        self.own_wait(sp, t)
        sp.wait_ge(self.res_done, t + 1)
        sp.dma_start(self.dst(row), self.xout[p][:, :]).then_inc(self.stored[p], 16)

    def sp_program(self, sp, last_lag=4):
        def step(s, q):
            row = {lag: (s - lag) * P if isinstance(s, int) else sp.snap((s - lag) * P)
                   for lag in (0, last_lag - 2, last_lag)}
            if live(s, 0):
                self.load(sp, s, q, row[0])
            if live(s, last_lag - 2):
                self.load_res(sp, s - (last_lag - 2), (q + last_lag) % 2, row[last_lag - 2])
            if live(s, last_lag):
                self.store(sp, s - last_lag, (q + last_lag) % 2, row[last_lag])

        run_steps(sp, step, last_lag)
        for p in range(2):
            sp.wait_ge(self.stored[p], moved(NT - 2 + p, p))

    def ln_stats(self, dve, t, p):
        nc = self.nc
        dve.wait_ge(self.x_loaded[p], moved(t, p))
        nc.vector.bn_stats(self.bn[p][:, :], self.xin[p][:, :]).then_inc(self.bn_done, 1)
        dve.wait_ge(self.bn_done, t + 1)
        dve.sem_inc(self.bn_waited, 1)
        nc.vector.bn_aggr(self.mv[p][:, :], self.bn[p][:, :]).then_inc(self.mv_done, 1)
        dve.wait_ge(self.mv_done, t + 1)
        if exists(t - 2):
            dve.wait_ge(self.rstd_done, t - 1)
        nc.vector.tensor_scalar_add(self.var[p][:, :], self.mv[p][:, 1:2], EPS).then_inc(self.var_done, 1)

    def ln_pow(self, pool, t, p, minus_half):
        pool.wait_ge(self.var_done, t + 1)
        if exists(t - 2):
            pool.wait_ge(self.xh_done, t - 1)
        self.nc.gpsimd.tensor_tensor(self.rstd[p][:, :], self.var[p][:, :], minus_half[:, :],
                                     ALU.pow).then_inc(self.rstd_done, 1)

    def ln_norm(self, dve, t, p):
        dve.wait_ge(self.rstd_done, t + 1)
        if exists(t - 2):
            dve.wait_ge(self.xtr_done, t - 1)
        self.nc.vector.tensor_scalar(self.xh[p][:, :], self.xin[p][:, :], self.mv[p][:, 0:1],
                                     self.rstd[p][:, :], ALU.subtract, ALU.mult).then_inc(self.xh_done, 1)

    def x_transpose(self, pe, t, p, psX, ident, ready=None, src=None):
        pe.wait_ge(ready or self.xh_done, t + 1)
        if exists(t - 1):
            pe.wait_ge(self.xT_done, t)
        self.nc.tensor.transpose(psX[:, 0:P], (src or self.xh)[p][:, :], ident[:, :]).then_inc(self.xtr_done, 1)

    def x_copy(self, act, t, p, psX, used, per):
        act.wait_ge(self.xtr_done, t + 1)
        if exists(t - 2):
            act.wait_ge(used, per * (t - 1))
        self.nc.scalar.copy(self.xT[p][:, :], psX[:, 0:P]).then_inc(self.xT_done, 1)

    def add_residual(self, dve, t, p, psO, coef):
        dve.wait_ge(self.o_done, t + 1)
        dve.wait_ge(self.res_loaded[p], moved(t, p))
        if exists(t - 2):
            dve.wait_ge(self.stored[p], moved(t - 2, p))
        self.nc.vector.scalar_tensor_tensor(self.xout[p][:, :], psO[:, 0:P], coef, self.xres[p][:, :],
                                            ALU.mult, ALU.add).then_inc(self.res_done, 1)


def prepare(nc, c, w):
    def sb(name, shape, dt=F32):
        return c.enter_context(nc.sbuf_tensor(name, shape, dt))

    keep, loads = {}, []

    def load(stack, name, shape):
        t = stack.enter_context(nc.sbuf_tensor("w_" + name, shape, F32))
        keep[name] = t
        loads.append((t[:], w[name]))
        return t

    ident = load(c, "ident", [P, P])
    for n, shape in (("l0_wv", [P, P]), ("causal", [P, P]),
                     ("l1_gateT", [P, NE]), ("l1_wgT", [P, HID]), ("l1_wuT", [P, HID]),
                     ("l1_wdT", [P, CH, P]), ("desc", [P, NE]),
                     ("l2_wqT", [P, P]), ("l2_wkT", [P, P]), ("l2_wvT2", [P, 2, P]), ("l2_woT", [P, P]),
                     ("l2_bq", [P, 1]), ("l2_bk", [P, 1]), ("l2_bv", [P, 1]), ("l2_bo", [1, P]),
                     ("l2_wrT", [P, P]), ("l2_wkfT", [P, P]), ("l2_wvfT", [P, P]),
                     ("l2_mur", [P, 1]), ("l2_muk", [P, 1]),
                     ("l3_wqT", [P, P]), ("l3_wkT", [P, P]), ("l3_wqrT", [P, P]), ("l3_wkrT", [P, P]),
                     ("l3_wvT2", [P, 2, P]), ("l3_woT", [P, P]), ("rope", [P, 2, 2, P]),
                     ("headmask", [P, 4, SEQ]),
                     ("l3_w1T", [P, HID]), ("l3_w2T", [P, CH, P]), ("l3_b2", [1, P]),
                     ("l3_scale", [P, 1]), ("mask_up", [32, P]), ("mask_down", [P, P]),
                     ("sel_token", [P, 32]), ("sel_up", [32, CH, P]), ("sel_down", [P, CH, 32])):
        load(c, n, shape)
    lora_up = sb("lora_up0", [33, HID]), sb("lora_up1", [33, HID])
    for i in range(2):
        loads.append((lora_up[i][32:33, :], w["l3_b1"]))
    keep["lora_up"] = lora_up

    tg = sb("tanh_gates", [P, 8])
    half_gate = sb("half_gate", [P, 8])
    A0 = sb("A0", [P, P])
    AT = sb("AT", [P, NH, P])
    B = sb("B", [P, 2, PAIRS, P])
    WJ = sb("WJ", [P, 3, HID])
    tern2 = sb("tern2", [P, CH, P], BF16)
    convb3 = sb("convb3", [96, HID], BF16)
    ones_bf = sb("ones_bf", [96, P], BF16)
    ones_row = sb("ones_row", [1, P])
    minus_half = sb("minus_half", [P, 1])
    coef2 = sb("coef2", [P, 1])
    mu = {n: sb("l2f_" + n, [P, P]) for n in ("wr0", "wr1", "wk0", "wk1")}
    keep.update(tg=tg, A0=A0, AT=AT, B=B, WJ=WJ, tern2=tern2, convb3=convb3, ones_bf=ones_bf,
                ones_row=ones_row, minus_half=minus_half, coef2=coef2, half_gate=half_gate, **mu)

    with ExitStack() as pc:
        def tmp(name, shape, dt=F32):
            return pc.enter_context(nc.sbuf_tensor(name, shape, dt))

        sem = semaphores(nc, pc)

        gates = load(pc, "gates", [P, 8])
        l0_wqT, l0_wkT = load(pc, "l0_wqT", [P, P]), load(pc, "l0_wkT", [P, P])
        w1T, w2T = load(pc, "l0_w1T", [P, CH, P]), load(pc, "l0_w2T", [P, CH, P])
        cw, cb = load(pc, "l0_convw", [P, 3, HID]), load(pc, "l0_convb", [1, HID])
        l1_wqT, l1_wkT, l1_wvT, l1_wo = (load(pc, "l1_" + n, [P, PAIRS, P]) for n in ("wqT", "wkT", "wvT", "wo"))
        onesf = tmp("onesf", [P, P])
        asum = tmp("asum", [P, 4])
        small = tmp("small", [P, 12])
        wr = tmp("wrounded", [P, CH, P])
        rowt = tmp("rowt", [1, 4, HID])
        rowb = tmp("rowb", [1, 2, HID], BF16)
        ps = [pc.enter_context(nc.psum_tensor(f"prep_ps{i}", [P, 512], F32)) for i in range(4)]
        loaded, filled, sums_ready, summed, chain, done = (
            sem("prep_" + n) for n in ("loaded", "filled", "sums_ready", "summed", "chain", "done"))
        prod, copied, tanhed = sem("prep_prod"), sem("prep_copied"), sem("prep_tanhed")

        groups = [([(l0_wqT[:, :], l0_wkT[:, :])], A0[:, :].unsqueeze(1), float(P) ** -0.5)]
        for j in range(2):
            for q in range(0, PAIRS, 4):
                r = slice(64 * j, 64 * j + 64)
                part = [(l1_wkT[r, i, :], l1_wqT[r, i, :]) for i in range(q, q + 4)]
                groups.append((part, AT[:, :, :].rearrange("p (a j) b -> p a j b", j=2)[:, q:q + 4, j, :], 0.125))
                part = [(l1_wvT[r, i, :], l1_wo[r, i, :]) for i in range(q, q + 4)]
                groups.append((part, B[:, j, q:q + 4, :], 1.0))

        with nc.Block() as block:
            @block.sync
            def _(sp):
                for dst, src in loads:
                    sp.dma_start(dst, src).then_inc(loaded, 16)

            @block.tensor
            def _(pe):
                pe.wait_ge(loaded, 16 * len(loads))
                for g, (part, _, _) in enumerate(groups):
                    if g >= 3:
                        pe.wait_ge(copied, g - 2)
                    for i, (lhsT, rhs) in enumerate(part):
                        last = nc.tensor.matmul(ps[g % 3][:, i * P:(i + 1) * P], lhsT, rhs, start=True, stop=True)
                    last.then_inc(prod, 1)
                pe.wait_ge(filled, 1)
                pe.wait_ge(sums_ready, 2)
                nc.tensor.matmul(ps[3][:, 0:2], onesf[:, :], asum[:, 0:2], start=True, stop=True).then_inc(summed, 1)

            @block.scalar
            def _(act):
                act.wait_ge(loaded, 16 * len(loads))
                nc.scalar.activation(tg[:, :], gates[:, :], ACT.Tanh).then_inc(tanhed, 1)
                for g, (_, out, scale) in enumerate(groups):
                    act.wait_ge(prod, g + 1)
                    n = out.shape[1]
                    nc.scalar.activation(out, ps[g % 3][:, 0:n * P].rearrange("p (a b) -> p a b", a=n), ACT.Copy,
                                         scale=scale).then_inc(copied, 1)

            @block.vector
            def _(dve):
                links = [0]

                def link(ins):
                    links[0] += 1
                    ins.then_inc(chain, 1)
                    dve.wait_ge(chain, links[0])

                nc.vector.memset(onesf[:, :], 1.0).then_inc(filled, 1)
                nc.vector.memset(ones_bf[:, :], 1.0)
                nc.vector.memset(ones_row[:, :], 1.0)
                nc.vector.memset(minus_half[:, :], -0.5)
                link(nc.vector.memset(convb3[:, :], 0.0))
                dve.wait_ge(loaded, 16 * len(loads))
                for i, wx in enumerate((w1T, w2T)):
                    nc.vector.tensor_reduce(asum[:, i:i + 1], wx[:, :, :], AX.XY, ALU.add,
                                            apply_absolute_value=True).then_inc(sums_ready, 1)
                link(nc.vector.tensor_copy(rowb[:, 0, :], cb[:, :]))
                nc.vector.tensor_copy(convb3[0:1, :], rowb[:, 0, :])
                link(nc.vector.tensor_tensor(rowt[:, 0, :], cb[:, :], rowb[:, 0, :], ALU.subtract))
                link(nc.vector.tensor_copy(rowb[:, 1, :], rowt[:, 0, :]))
                nc.vector.tensor_copy(convb3[32:33, :], rowb[:, 1, :])
                link(nc.vector.tensor_tensor(rowt[:, 1, :], rowt[:, 0, :], rowb[:, 1, :], ALU.subtract))
                nc.vector.tensor_copy(convb3[64:65, :], rowt[:, 1, :])
                dve.wait_ge(summed, 1)
                link(nc.vector.tensor_scalar(small[:, 0:2], ps[3][:, 0:2], 1.0 / (HID * P), 1e-5, ALU.mult, ALU.max))
                link(nc.vector.reciprocal(small[:, 2:4], small[:, 0:2]))
                for i, wx in enumerate((w1T, w2T)):
                    link(nc.vector.tensor_scalar(wr[:, :, :], wx[:, :, :], small[:, 2 + i:3 + i], 1.0, ALU.mult, ALU.min))
                    link(nc.vector.tensor_scalar(wr[:, :, :], wr[:, :, :], -1.0, MAGIC, ALU.max, ALU.add))
                    link(nc.vector.tensor_scalar_add(wr[:, :, :], wr[:, :, :], -MAGIC))
                    if i == 0:
                        wrf = wr[:, :, :].rearrange("p a b -> p (a b)")
                        link(nc.vector.tensor_scalar_mul(wrf, wrf, small[:, 0:1]))
                        for j in range(3):
                            ins = nc.vector.tensor_tensor(WJ[:, j, :], wrf, cw[:, j, :], ALU.mult)
                        link(ins)
                    else:
                        link(nc.vector.tensor_copy(tern2[:, :, :], wr[:, :, :]))
                dve.wait_ge(tanhed, 1)
                nc.vector.tensor_scalar_mul(half_gate[:, :], tg[:, :], 0.5)
                link(nc.vector.tensor_tensor(small[:, 4:5], small[:, 1:2], tg[:, 4:5], ALU.mult))
                link(nc.vector.tensor_scalar_mul(coef2[:, :], small[:, 4:5], 0.5))
                for m, wx, a, b in (("l2_mur", "l2_wrT", "wr0", "wr1"), ("l2_muk", "l2_wkfT", "wk0", "wk1")):
                    link(nc.vector.tensor_scalar(small[:, 6:7], keep[m][:, :], -1.0, 1.0, ALU.mult, ALU.add))
                    nc.vector.tensor_scalar_mul(mu[a][:, :], keep[wx][:, :], keep[m][:, :])
                    link(nc.vector.tensor_scalar_mul(mu[b][:, :], keep[wx][:, :], small[:, 6:7]))
                link(nc.vector.tensor_scalar_mul(keep["l2_bq"][:, :], keep["l2_bq"][:, :], 8.0 ** -0.5))
                link(nc.vector.tensor_scalar_mul(keep["mask_up"][:, :], keep["mask_up"][:, :], keep["l3_scale"][0:32, :]))
                link(nc.vector.tensor_scalar_mul(keep["mask_down"][:, :], keep["mask_down"][:, :], keep["l3_scale"][:, :]))
    return keep


def load_gate(k, i):
    return k["tg"][:, i:i + 1]


def layer0_attention(nc, k, src, dst, ctx):
    with ExitStack() as c:
        S = Stream(nc, c, "a0", src, dst, ctx)
        qT, V, E, PT = (S.two(n, [P, P]) for n in ("qT", "V", "E", "PT"))
        nmax, ssum, rinv, coef = (S.two(n, [P, 1]) for n in ("nmax", "ssum", "rinv", "coef"))
        psX, psQ, psV, psS, psPT, psO = (S.bank(n) for n in ("psX", "psQ", "psV", "psS", "psPT", "psO"))
        q_done, q_copied, v_done, v_copied, s_done, masked, max_done, exp_done, rinv_done, coef_done, \
            ptr_done, pt_copied = (S.sem(n) for n in (
                "q_done", "q_copied", "v_done", "v_copied", "s_done", "masked", "max_done", "exp_done",
                "rinv_done", "coef_done", "ptr_done", "pt_copied"))
        S.ctx_used = s_done, 1
        block = c.enter_context(nc.Block())

        @block.sync
        def _(sp):
            S.sp_program(sp)

        @block.gpsimd
        def _(pool):
            def step(s, q):
                if live(s, 1):
                    S.ln_pow(pool, s - 1, 1 - q, k["minus_half"])

            run_steps(pool, step)

        @block.tensor
        def _(pe):
            def scores(t, p):
                pe.wait_ge(S.xT_done, t + 1)
                pe.wait_ge(S.ctx_loaded[p], moved(t, p))
                if exists(t - 1):
                    pe.wait_ge(q_copied, t)
                nc.tensor.matmul(psQ[:, 0:P], k["A0"][:, :], S.xT[p][:, :], start=True, stop=True).then_inc(q_done, 1)
                if exists(t - 1):
                    pe.wait_ge(v_copied, t)
                nc.tensor.matmul(psV[:, 0:P], S.ctxT[p][:, :], k["l0_wv"][:, :], start=True, stop=True)\
                    .then_inc(v_done, 1)
                pe.wait_ge(q_copied, t + 1)
                if exists(t - 1):
                    pe.wait_ge(masked, t)
                nc.tensor.matmul(psS[:, 0:P], qT[p][:, :], S.ctxT[p][:, :], start=True, stop=True).then_inc(s_done, 1)

            def values(t, p):
                pe.wait_ge(exp_done, t + 1)
                if exists(t - 1):
                    pe.wait_ge(pt_copied, t)
                nc.tensor.transpose(psPT[:, 0:P], E[p][:, :], k["ident"][:, :]).then_inc(ptr_done, 1)
                pe.wait_ge(pt_copied, t + 1)
                pe.wait_ge(v_copied, t + 1)
                if exists(t - 1):
                    pe.wait_ge(S.res_done, t)
                nc.tensor.matmul(psO[:, 0:P], PT[p][:, :], V[p][:, :], start=True, stop=True).then_inc(S.o_done, 1)

            def step(s, q):
                if live(s, 2):
                    scores(s - 2, q)
                if live(s, 1):
                    S.x_transpose(pe, s - 1, 1 - q, psX, k["ident"])
                if live(s, 3):
                    values(s - 3, 1 - q)

            run_steps(pe, step)

        @block.scalar
        def _(act):
            def step(s, q):
                if live(s, 2):
                    t, p = s - 2, q
                    act.wait_ge(q_done, t + 1)
                    if exists(t - 2):
                        act.wait_ge(s_done, t - 1)
                    nc.scalar.copy(qT[p][:, :], psQ[:, 0:P]).then_inc(q_copied, 1)
                    act.wait_ge(v_done, t + 1)
                    if exists(t - 2):
                        act.wait_ge(S.o_done, t - 1)
                    nc.scalar.copy(V[p][:, :], psV[:, 0:P]).then_inc(v_copied, 1)
                if live(s, 1):
                    S.x_copy(act, s - 1, 1 - q, psX, q_done, 1)
                if live(s, 3):
                    t, p = s - 3, 1 - q
                    act.wait_ge(ptr_done, t + 1)
                    if exists(t - 2):
                        act.wait_ge(S.o_done, t - 1)
                    nc.scalar.copy(PT[p][:, :], psPT[:, 0:P]).then_inc(pt_copied, 1)
                if live(s, 2):
                    t, p = s - 2, q
                    act.wait_ge(max_done, t + 1)
                    if exists(t - 2):
                        act.wait_ge(rinv_done, t - 1)
                    nc.scalar.activation(E[p][:, :], E[p][:, :], ACT.Exp, bias=nmax[p][:, :],
                                         accum_out=ssum[p][:, :]).then_inc(exp_done, 1)

            run_steps(act, step)

        @block.vector
        def _(dve):
            def step(s, q):
                if live(s, 1):
                    S.ln_stats(dve, s - 1, 1 - q)
                if live(s, 2):
                    t, p = s - 2, q
                    dve.wait_ge(s_done, t + 1)
                    if exists(t - 2):
                        dve.wait_ge(ptr_done, t - 1)
                    nc.vector.tensor_tensor(E[p][:, :], psS[:, 0:P], k["causal"][:, :], ALU.add).then_inc(masked, 1)
                    dve.wait_ge(masked, t + 1)
                    if exists(t - 2):
                        dve.wait_ge(exp_done, t - 1)
                    nc.vector.tensor_reduce(nmax[p][:, :], E[p][:, :], AX.X, ALU.max, negate=True)\
                        .then_inc(max_done, 1)
                if live(s, 1):
                    S.ln_norm(dve, s - 1, 1 - q)
                if live(s, 2):
                    t, p = s - 2, q
                    dve.wait_ge(exp_done, t + 1)
                    if exists(t - 2):
                        dve.wait_ge(coef_done, t - 1)
                    nc.vector.reciprocal(rinv[p][:, :], ssum[p][:, :]).then_inc(rinv_done, 1)
                    dve.wait_ge(rinv_done, t + 1)
                    if exists(t - 2):
                        dve.wait_ge(S.res_done, t - 1)
                    nc.vector.tensor_scalar_mul(coef[p][:, :], rinv[p][:, :], load_gate(k, 0)).then_inc(coef_done, 1)
                if live(s, 3):
                    dve.wait_ge(coef_done, s - 2)
                    S.add_residual(dve, s - 3, 1 - q, psO, coef[1 - q][:, :])

            run_steps(dve, step)


def layer0_ffn(nc, k, src, dst):
    PADDED = SEQ + 2
    with ExitStack() as c:
        S = Stream(nc, c, "f0", src, dst)
        xpad = S.two("xpad", [P, NB, PADDED])
        xq, xd = S.two("xq", [P, P]), S.two("xd", [P, P])
        amax, step1, inv1, amax2, step2, inv2, coef = (
            S.two(n, [P, 1]) for n in ("amax", "step1", "inv1", "amax2", "step2", "inv2", "coef"))
        th, g, gm = (S.two(n, [P, HID]) for n in ("th", "g", "gm"))
        q2 = S.two("q2", [P, HID], BF16)
        q2T = S.two("q2T", [P, HID], BF16)
        identb = S.sb("identb", [P, P], BF16)
        psX, psO = S.bank("psX"), S.bank("psO")
        psH = [S.bank(f"psH{i}") for i in range(2)]
        psT = S.bank("psT", BF16)
        xT_used = S.sem("xT_used")
        ready, amax_done, step_done, inv_done, round_done, xd_done, h_done, th_done, g_done, amax2_done, \
            step2_done, inv2_done, gm_done, q2_done, coef_done, qtr_done, qT_done = (S.sem(n) for n in (
                "ready", "amax_done", "step_done", "inv_done", "round_done", "xd_done", "h_done", "th_done",
                "g_done", "amax2_done", "step2_done", "inv2_done", "gm_done", "q2_done", "coef_done",
                "qtr_done", "qT_done"))
        block = c.enter_context(nc.Block())

        @block.sync
        def _(sp):
            S.sp_program(sp)

        @block.gpsimd
        def _(pool):
            nc.gpsimd.tensor_copy(identb[:, :], k["ident"][:, :]).then_inc(ready, 1)
            for p in range(2):
                nc.gpsimd.memset(xpad[p][:, :, :], 0.0).then_inc(ready, 1)

            def step(s, q):
                if live(s, 1):
                    S.ln_pow(pool, s - 1, 1 - q, k["minus_half"])

            run_steps(pool, step)

        @block.tensor
        def _(pe):
            def hidden(t, p):
                pe.wait_ge(S.xT_done, t + 1)
                if exists(t - 2):
                    pe.wait_ge(g_done, t - 1)
                for j in range(3):
                    for b in range(NB):
                        last = nc.tensor.matmul(psH[p][64 * b:64 * b + 64, :], xpad[p][:, b, j:j + SEQ],
                                                k["WJ"][:, j, :], start=(j == 0), stop=False)
                last.then_inc(xT_used, 1)
                for b in range(NB):
                    last = nc.tensor.matmul(psH[p][64 * b:64 * b + 64, :], k["ones_bf"][:, 0:64], k["convb3"][:, :],
                                            start=False, stop=True)
                last.then_inc(h_done, 1)

            def down(t, p):
                pe.wait_ge(q2_done, t + 1)
                if exists(t - 1):
                    pe.wait_ge(qT_done, t)
                for i in range(CH):
                    last = nc.tensor.transpose(psT[:, i * P:(i + 1) * P], q2[p][:, i * P:(i + 1) * P], identb[:, :])
                last.then_inc(qtr_done, 1)
                pe.wait_ge(qT_done, t + 1)
                if exists(t - 1):
                    pe.wait_ge(S.res_done, t)
                for i in range(CH):
                    last = nc.tensor.matmul(psO[:, 0:P], q2T[p][:, i * P:(i + 1) * P], k["tern2"][:, i, :],
                                            start=(i == 0), stop=(i == CH - 1))
                last.then_inc(S.o_done, 1)

            pe.wait_ge(ready, 3)

            def step(s, q):
                if live(s, 2):
                    hidden(s - 2, q)
                if live(s, 1):
                    S.x_transpose(pe, s - 1, 1 - q, psX, k["ident"], ready=xd_done, src=xd)
                if live(s, 3):
                    down(s - 3, 1 - q)

            run_steps(pe, step)

        @block.scalar
        def _(act):
            act.wait_ge(ready, 3)

            def step(s, q):
                if live(s, 1):
                    t, p = s - 1, 1 - q
                    act.wait_ge(S.xtr_done, t + 1)
                    if exists(t - 2):
                        act.wait_ge(xT_used, t - 1)
                    nc.scalar.copy(xpad[p][:, :, 1:1 + SEQ], psX[:, 0:P].rearrange("p (b s) -> p b s", b=NB))\
                        .then_inc(S.xT_done, 1)
                if live(s, 2):
                    t, p = s - 2, q
                    act.wait_ge(h_done, t + 1)
                    if exists(t - 2):
                        act.wait_ge(g_done, t - 1)
                    nc.scalar.activation(th[p][:, :], psH[p][:, :], ACT.Tanh, scale=0.5).then_inc(th_done, 1)
                if live(s, 3):
                    t, p = s - 3, 1 - q
                    act.wait_ge(qtr_done, t + 1)
                    if exists(t - 2):
                        act.wait_ge(S.o_done, t - 1)
                    nc.scalar.copy(q2T[p][:, :], psT[:, 0:HID]).then_inc(qT_done, 1)

            run_steps(act, step)

        @block.vector
        def _(dve):
            def quantise_input(t, p):
                S.ln_norm(dve, t, p)
                dve.wait_ge(S.xh_done, t + 1)
                nc.vector.tensor_reduce(amax[p][:, :], S.xh[p][:, :], AX.X, ALU.max, apply_absolute_value=True)\
                    .then_inc(amax_done, 1)
                dve.wait_ge(amax_done, t + 1)
                nc.vector.tensor_scalar(step1[p][:, :], amax[p][:, :], 1e-5, 1.0 / 127.0, ALU.max, ALU.mult)\
                    .then_inc(step_done, 1)
                dve.wait_ge(step_done, t + 1)
                nc.vector.reciprocal(inv1[p][:, :], step1[p][:, :]).then_inc(inv_done, 1)
                dve.wait_ge(inv_done, t + 1)
                nc.vector.tensor_scalar(xq[p][:, :], S.xh[p][:, :], inv1[p][:, :], MAGIC, ALU.mult, ALU.add)\
                    .then_inc(round_done, 1)
                dve.wait_ge(round_done, t + 1)
                if exists(t - 2):
                    dve.wait_ge(S.xtr_done, t - 1)
                nc.vector.tensor_scalar(xd[p][:, :], xq[p][:, :], MAGIC, step1[p][:, :], ALU.subtract, ALU.mult)\
                    .then_inc(xd_done, 1)

            def quantise_hidden(t, p):
                dve.wait_ge(th_done, t + 1)
                nc.vector.scalar_tensor_tensor(g[p][:, :], th[p][:, :], 1.0, psH[p][:, :], ALU.add, ALU.mult)\
                    .then_inc(g_done, 1)
                dve.wait_ge(g_done, t + 1)
                nc.vector.tensor_reduce(amax2[p][:, :], g[p][:, :], AX.X, ALU.max, apply_absolute_value=True)\
                    .then_inc(amax2_done, 1)
                dve.wait_ge(amax2_done, t + 1)
                nc.vector.tensor_scalar(step2[p][:, :], amax2[p][:, :], 2e-5, 1.0 / 127.0, ALU.max, ALU.mult)\
                    .then_inc(step2_done, 1)
                dve.wait_ge(step2_done, t + 1)
                nc.vector.reciprocal(inv2[p][:, :], step2[p][:, :]).then_inc(inv2_done, 1)
                if exists(t - 2):
                    dve.wait_ge(S.res_done, t - 1)
                nc.vector.tensor_scalar_mul(coef[p][:, :], step2[p][:, :], k["coef2"][:, :]).then_inc(coef_done, 1)
                dve.wait_ge(inv2_done, t + 1)
                nc.vector.tensor_scalar(gm[p][:, :], g[p][:, :], inv2[p][:, :], MAGIC, ALU.mult, ALU.add)\
                    .then_inc(gm_done, 1)
                dve.wait_ge(gm_done, t + 1)
                if exists(t - 2):
                    dve.wait_ge(qtr_done, t - 1)
                nc.vector.tensor_scalar_add(q2[p][:, :], gm[p][:, :], -MAGIC).then_inc(q2_done, 1)

            def step(s, q):
                if live(s, 1):
                    S.ln_stats(dve, s - 1, 1 - q)
                if live(s, 3):
                    dve.wait_ge(coef_done, s - 2)
                if live(s, 1):
                    quantise_input(s - 1, 1 - q)
                if live(s, 2):
                    quantise_hidden(s - 2, q)
                if live(s, 3):
                    S.add_residual(dve, s - 3, 1 - q, psO, coef[1 - q][:, :])

            run_steps(dve, step)


def softmax_max_sub(dve, nc, nmax, E, psS, t, p, s_done, max_done, sub_done, e_used):
    for hf in range(2):
        sv = psS[hf][:, :].rearrange("p (h k) -> p h k", k=SEQ)
        dve.wait_ge(s_done, 2 * t + hf + 1)
        if hf == 0:
            if exists(t - 2):
                dve.wait_ge(sub_done, 2 * t - 2)
        nc.vector.tensor_reduce(nmax[p][:, 8 * hf:8 * hf + 8], sv, AX.X, ALU.max).then_inc(max_done, 1)
        dve.wait_ge(max_done, 2 * t + hf + 1)
        if hf == 0:
            if exists(t - 2):
                dve.wait_ge(e_used, 2 * t - 2)
        nc.vector.tensor_tensor(E[p][:, hf, :].rearrange("p (h k) -> p h k", k=SEQ), sv,
                                nmax[p][:, 8 * hf:8 * hf + 8].unsqueeze(2).broadcast_to([P, 8, SEQ]),
                                ALU.subtract).then_inc(sub_done, 1)


def layer1_attention(nc, k, src, dst, ctx):
    with ExitStack() as c:
        S = Stream(nc, c, "a1", src, dst, ctx)
        T = S.two("T", [P, NB, NH, SEQ])
        U = S.two("U", [P, NB, PAIRS, P])
        E = S.two("E", [P, 2, 512])
        PT = S.two("PT", [P, PAIRS, P])
        rmax, ssum, rinv = (S.two(n, [P, NH]) for n in ("rmax", "ssum", "rinv"))
        psM = [S.bank(f"psM{i}") for i in range(2)]
        psS = [S.bank(f"psS{i}") for i in range(2)]
        psT = [S.bank(f"psT{i}") for i in range(2)]
        psX, psO = S.bank("psX"), S.bank("psO")
        proj_done, proj_copied, s_done, max_done, sub_done, exp_done, sum_done, rinv_done, p_done, \
            ptr_done, pt_copied = (S.sem(n) for n in (
                "proj_done", "proj_copied", "s_done", "max_done", "sub_done", "exp_done", "sum_done",
                "rinv_done", "p_done", "ptr_done", "pt_copied"))
        S.ctx_used = proj_done, 8
        block = c.enter_context(nc.Block())

        @block.sync
        def _(sp):
            S.sp_program(sp)

        @block.gpsimd
        def _(pool):
            def step(s, q):
                if live(s, 1):
                    S.ln_pow(pool, s - 1, 1 - q, k["minus_half"])
                if live(s, 2):
                    t, p = s - 2, q
                    for hf in range(2):
                        pool.wait_ge(rinv_done, 2 * t + hf + 1)
                        ev = E[p][:, hf, :].rearrange("p (h k) -> p h k", k=SEQ)
                        nc.gpsimd.tensor_tensor(
                            ev, ev, rinv[p][:, 8 * hf:8 * hf + 8].unsqueeze(2).broadcast_to([P, 8, SEQ]),
                            ALU.mult).then_inc(p_done, 1)

            run_steps(pool, step)

        @block.tensor
        def _(pe):
            def project(t, p):
                pe.wait_ge(S.xT_done, t + 1)
                pe.wait_ge(S.ctx_loaded[p], moved(t, p))
                for i in range(4):
                    if i < 2:
                        if exists(t - 1):
                            pe.wait_ge(proj_copied, 8 * t + i - 1)
                    else:
                        pe.wait_ge(proj_copied, 8 * t + i - 1)
                    for h in range(4):
                        last = nc.tensor.matmul(psM[i % 2][:, h * P:(h + 1) * P], k["AT"][:, 4 * i + h, :],
                                                S.ctxT[p][:, :], start=True, stop=True)
                    last.then_inc(proj_done, 1)
                for i in range(4):
                    pe.wait_ge(proj_copied, 8 * t + i + 3)
                    b, q4 = i // 2, 4 * (i % 2)
                    for j in range(2):
                        last = nc.tensor.matmul(psM[i % 2][64 * j:64 * j + 64, :], S.ctxT[p][:, 64 * b:64 * b + 64],
                                                k["B"][:, j, q4:q4 + 4, :], start=True, stop=True)
                    last.then_inc(proj_done, 1)
                last_use = last
                return last_use

            def scores(t, p):
                for hf in range(2):
                    pe.wait_ge(proj_copied, 8 * t + 4)
                    if exists(t - 1):
                        pe.wait_ge(sub_done, 2 * t + hf - 1)
                    for b in range(NB):
                        last = nc.tensor.matmul(psS[hf][64 * b:64 * b + 64, :], S.xT[p][:, 64 * b:64 * b + 64],
                                                T[p][:, b, 8 * hf:8 * hf + 8, :], start=True, stop=True)
                    last.then_inc(s_done, 1)

            def values(t, p):
                for hf in range(2):
                    pe.wait_ge(p_done, 2 * t + hf + 1)
                    if exists(t - 1):
                        pe.wait_ge(pt_copied, 2 * t + hf - 1)
                    for i in range(4):
                        last = nc.tensor.transpose(psT[hf][:, i * P:(i + 1) * P], E[p][:, hf, i * P:(i + 1) * P],
                                                   k["ident"][:, :])
                    last.then_inc(ptr_done, 1)
                if exists(t - 1):
                    pe.wait_ge(S.res_done, t)
                for i in range(PAIRS):
                    if i % 4 == 0:
                        pe.wait_ge(pt_copied, 2 * t + i // 4 + 1)
                    for b in range(NB):
                        last = nc.tensor.matmul(psO[64 * b:64 * b + 64, 0:P], PT[p][:, i, 64 * b:64 * b + 64],
                                                U[p][:, b, i, :], start=(i == 0), stop=(i == PAIRS - 1))
                last.then_inc(S.o_done, 1)

            def step(s, q):
                if live(s, 2):
                    project(s - 2, q)
                    scores(s - 2, q)
                if live(s, 1):
                    S.x_transpose(pe, s - 1, 1 - q, psX, k["ident"])
                if live(s, 3):
                    values(s - 3, 1 - q)

            run_steps(pe, step)

        @block.scalar
        def _(act):
            def step(s, q):
                if live(s, 2):
                    t, p = s - 2, q
                    if exists(t - 2):
                        act.wait_ge(s_done, 2 * t - 2)
                    for i in range(4):
                        act.wait_ge(proj_done, 8 * t + i + 1)
                        nc.scalar.copy(T[p][:, :, 4 * i:4 * i + 4, :].rearrange("p b h k -> p h b k"),
                                       psM[i % 2][:, :].rearrange("p (h b k) -> p h b k", h=4, b=NB))\
                            .then_inc(proj_copied, 1)
                    if exists(t - 2):
                        act.wait_ge(S.o_done, t - 1)
                    for i in range(4):
                        act.wait_ge(proj_done, 8 * t + i + 5)
                        b, q4 = i // 2, 4 * (i % 2)
                        nc.scalar.copy(U[p][:, b, q4:q4 + 4, :].rearrange("p a b -> p (a b)"), psM[i % 2][:, :])\
                            .then_inc(proj_copied, 1)
                if live(s, 1):
                    S.x_copy(act, s - 1, 1 - q, psX, s_done, 2)
                if live(s, 3):
                    t, p = s - 3, 1 - q
                    if exists(t - 2):
                        act.wait_ge(S.o_done, t - 1)
                    for hf in range(2):
                        act.wait_ge(ptr_done, 2 * t + hf + 1)
                        nc.scalar.copy(PT[p][:, 4 * hf:4 * hf + 4, :].rearrange("p a b -> p (a b)"), psT[hf][:, :])\
                            .then_inc(pt_copied, 1)
                if live(s, 2):
                    t, p = s - 2, q
                    for hf in range(2):
                        act.wait_ge(sub_done, 2 * t + hf + 1)
                        nc.scalar.activation(E[p][:, hf, :], E[p][:, hf, :], ACT.Exp).then_inc(exp_done, 1)

            run_steps(act, step)

        @block.vector
        def _(dve):
            def step(s, q):
                if live(s, 1):
                    S.ln_stats(dve, s - 1, 1 - q)
                if live(s, 2):
                    softmax_max_sub(dve, nc, rmax, E, psS, s - 2, q, s_done, max_done, sub_done, ptr_done)
                if live(s, 1):
                    S.ln_norm(dve, s - 1, 1 - q)
                if live(s, 2):
                    t, p = s - 2, q
                    for hf in range(2):
                        h8 = slice(8 * hf, 8 * hf + 8)
                        dve.wait_ge(exp_done, 2 * t + hf + 1)
                        if hf == 0:
                            if exists(t - 2):
                                dve.wait_ge(rinv_done, 2 * t - 2)
                        nc.vector.tensor_reduce(ssum[p][:, h8], E[p][:, hf, :].rearrange("p (h k) -> p h k", k=SEQ),
                                                AX.X, ALU.add).then_inc(sum_done, 1)
                        dve.wait_ge(sum_done, 2 * t + hf + 1)
                        if hf == 0:
                            if exists(t - 2):
                                dve.wait_ge(p_done, 2 * t - 2)
                        nc.vector.reciprocal(rinv[p][:, h8], ssum[p][:, h8]).then_inc(rinv_done, 1)
                if live(s, 3):
                    S.add_residual(dve, s - 3, 1 - q, psO, load_gate(k, 1))

            run_steps(dve, step)


def layer1_ffn(nc, k, src, dst):
    with ExitStack() as c:
        S = Stream(nc, c, "f1", src, dst)
        top, topw, th_top, rw, coef = (S.two(n, [P, 1]) for n in ("top", "topw", "th_top", "rw", "coef"))
        ranks, pick, share = (S.two(n, [P, NE]) for n in ("ranks", "pick", "share"))
        G, TH, A, Hd = (S.two(n, [P, HID]) for n in ("G", "TH", "A", "Hd"))
        HT = S.two("HT", [P, HID])
        psX, psL, psG, psT, psO = (S.bank(n) for n in ("psX", "psL", "psG", "psT", "psO"))
        psU = [S.bank(f"psU{i}") for i in range(2)]
        l_done, g_done, u_done, top_done, ranks_done, topw_done, pick_done, thtop_done, rw_done, share_done, \
            G_done, TH_done, A_done, H_done, coef_done, htr_done, hT_done = (S.sem(n) for n in (
                "l_done", "g_done", "u_done", "top_done", "ranks_done", "topw_done", "pick_done", "thtop_done",
                "rw_done", "share_done", "G_done", "TH_done", "A_done", "H_done", "coef_done", "htr_done",
                "hT_done"))
        block = c.enter_context(nc.Block())

        @block.sync
        def _(sp):
            S.sp_program(sp)

        @block.gpsimd
        def _(pool):
            def step(s, q):
                if live(s, 1):
                    S.ln_pow(pool, s - 1, 1 - q, k["minus_half"])

            run_steps(pool, step)

        @block.tensor
        def _(pe):
            def up(t, p):
                pe.wait_ge(S.xT_done, t + 1)
                if exists(t - 1):
                    pe.wait_ge(ranks_done, t)
                if exists(t - 1):
                    pe.wait_ge(thtop_done, t)
                nc.tensor.matmul(psL[:, 0:NE], S.xT[p][:, :], k["l1_gateT"][:, :], start=True, stop=True)\
                    .then_inc(l_done, 1)
                if exists(t - 1):
                    pe.wait_ge(G_done, t)
                nc.tensor.matmul(psG[:, :], S.xT[p][:, :], k["l1_wgT"][:, :], start=True, stop=True)\
                    .then_inc(g_done, 1)
                if exists(t - 2):
                    pe.wait_ge(H_done, t - 1)
                nc.tensor.matmul(psU[p][:, :], S.xT[p][:, :], k["l1_wuT"][:, :], start=True, stop=True)\
                    .then_inc(u_done, 1)

            def down(t, p):
                pe.wait_ge(H_done, t + 1)
                if exists(t - 1):
                    pe.wait_ge(hT_done, t)
                for i in range(CH):
                    last = nc.tensor.transpose(psT[:, i * P:(i + 1) * P], Hd[p][:, i * P:(i + 1) * P], k["ident"][:, :])
                last.then_inc(htr_done, 1)
                pe.wait_ge(hT_done, t + 1)
                if exists(t - 1):
                    pe.wait_ge(S.res_done, t)
                for i in range(CH):
                    last = nc.tensor.matmul(psO[:, 0:P], HT[p][:, i * P:(i + 1) * P], k["l1_wdT"][:, i, :],
                                            start=(i == 0), stop=(i == CH - 1))
                last.then_inc(S.o_done, 1)

            def step(s, q):
                if live(s, 2):
                    up(s - 2, q)
                if live(s, 1):
                    S.x_transpose(pe, s - 1, 1 - q, psX, k["ident"])
                if live(s, 3):
                    down(s - 3, 1 - q)

            run_steps(pe, step)

        @block.scalar
        def _(act):
            def step(s, q):
                if live(s, 2):
                    t, p = s - 2, q
                    act.wait_ge(top_done, t + 1)
                    if exists(t - 2):
                        act.wait_ge(rw_done, t - 1)
                    nc.scalar.activation(th_top[p][:, :], top[p][:, :], ACT.Tanh, scale=0.5).then_inc(thtop_done, 1)
                    act.wait_ge(G_done, t + 1)
                    if exists(t - 2):
                        act.wait_ge(A_done, t - 1)
                    nc.scalar.activation(TH[p][:, :], G[p][:, :], ACT.Tanh, scale=0.5).then_inc(TH_done, 1)
                if live(s, 1):
                    t, p = s - 1, 1 - q
                    act.wait_ge(S.xtr_done, t + 1)
                    if exists(t - 2):
                        act.wait_ge(u_done, t - 1)
                    nc.scalar.copy(S.xT[p][:, :], psX[:, 0:P]).then_inc(S.xT_done, 1)
                if live(s, 3):
                    t, p = s - 3, 1 - q
                    act.wait_ge(htr_done, t + 1)
                    if exists(t - 2):
                        act.wait_ge(S.o_done, t - 1)
                    nc.scalar.copy(HT[p][:, :], psT[:, :]).then_inc(hT_done, 1)

            run_steps(act, step)

        @block.vector
        def _(dve):
            def route(t, p):
                dve.wait_ge(l_done, t + 1)
                if exists(t - 2):
                    dve.wait_ge(thtop_done, t - 1)
                if exists(t - 2):
                    dve.wait_ge(ranks_done, t - 1)
                nc.vector.tensor_reduce(top[p][:, :], psL[:, 0:NE], AX.X, ALU.max).then_inc(top_done, 1)
                dve.wait_ge(top_done, t + 1)
                nc.vector.scalar_tensor_tensor(ranks[p][:, :], psL[:, 0:NE], top[p][:, :], k["desc"][:, :],
                                               ALU.is_equal, ALU.mult).then_inc(ranks_done, 1)
                dve.wait_ge(ranks_done, t + 1)
                nc.vector.tensor_reduce(topw[p][:, :], ranks[p][:, :], AX.X, ALU.max).then_inc(topw_done, 1)
                dve.wait_ge(thtop_done, t + 1)
                nc.vector.tensor_scalar(rw[p][:, :], th_top[p][:, :], 1.0, 0.5, ALU.add, ALU.mult).then_inc(rw_done, 1)
                dve.wait_ge(topw_done, t + 1)
                nc.vector.tensor_scalar(pick[p][:, :], ranks[p][:, :], topw[p][:, :], None, ALU.is_equal)\
                    .then_inc(pick_done, 1)
                dve.wait_ge(rw_done, t + 1)
                dve.wait_ge(pick_done, t + 1)
                nc.vector.tensor_scalar_mul(share[p][:, :], pick[p][:, :], rw[p][:, :]).then_inc(share_done, 1)
                if exists(t - 2):
                    dve.wait_ge(S.res_done, t - 1)
                nc.vector.tensor_scalar(coef[p][:, :], rw[p][:, :], load_gate(k, 5), 0.5, ALU.mult, ALU.mult)\
                    .then_inc(coef_done, 1)

            def gated(t, p):
                dve.wait_ge(g_done, t + 1)
                dve.wait_ge(share_done, t + 1)
                if exists(t - 2):
                    dve.wait_ge(TH_done, t - 1)
                if exists(t - 2):
                    dve.wait_ge(A_done, t - 1)
                nc.vector.tensor_tensor(G[p][:, :].rearrange("p (e i) -> p e i", e=NE),
                                        psG[:, :].rearrange("p (e i) -> p e i", e=NE),
                                        share[p][:, :].unsqueeze(2).broadcast_to([P, NE, HID // NE]),
                                        ALU.mult).then_inc(G_done, 1)

            def gated2(t, p):
                dve.wait_ge(TH_done, t + 1)
                if exists(t - 2):
                    dve.wait_ge(H_done, t - 1)
                nc.vector.scalar_tensor_tensor(A[p][:, :], TH[p][:, :], 1.0, G[p][:, :], ALU.add, ALU.mult)\
                    .then_inc(A_done, 1)
                dve.wait_ge(A_done, t + 1)
                dve.wait_ge(u_done, t + 1)
                if exists(t - 2):
                    dve.wait_ge(htr_done, t - 1)
                nc.vector.tensor_tensor(Hd[p][:, :], psU[p][:, :], A[p][:, :], ALU.mult).then_inc(H_done, 1)

            def step(s, q):
                if live(s, 1):
                    S.ln_stats(dve, s - 1, 1 - q)
                if live(s, 2):
                    route(s - 2, q)
                    gated(s - 2, q)
                if live(s, 1):
                    S.ln_norm(dve, s - 1, 1 - q)
                if live(s, 2):
                    gated2(s - 2, q)
                if live(s, 3):
                    dve.wait_ge(coef_done, s - 2)
                    S.add_residual(dve, s - 3, 1 - q, psO, coef[1 - q][:, :])

            run_steps(dve, step)


def small_head_attention(nc, k, name, src, dst, ctx, w, rotary, gate):
    LAG = 6
    with ExitStack() as c:
        S = Stream(nc, c, name, src, dst, ctx)
        QK = S.two("QK", [P, 2, P])
        Kb = S.two("Kb", [P, NB, NH, SEQ])
        V = S.two("V", [P, NB, NH, 9])
        E = S.two("E", [P, 2, 512])
        PT = S.two("PT", [P, PAIRS, P])
        on, oT = S.two("on", [P, P]), S.two("oT", [P, P])
        rmax, rinv = S.two("rmax", [P, NH]), S.two("rinv", [P, NH])
        rc, rs = S.two("rc", [P, 2, P]), S.two("rs", [P, 2, P])
        psX, psQK, psV, psO = S.bank("psX"), S.bank("psQK"), S.bank("psV"), S.bank("psO")
        psS = [S.bank(f"psS{i}") for i in range(2)]
        psT = [S.bank(f"psT{i}") for i in range(2)]
        o9 = psO[:, P:P + 9 * NH].rearrange("p (h e) -> p h e", e=9)
        ready, qk_done, qk_ready, v_done, v_copied, kb_dve, kb_pool, rc_done, rs_done, s_done, max_done, sub_done, \
            exp_done, ptr_done, pt_copied, pv_done, rinv_done, on_done, otr_done, oT_done = (S.sem(n) for n in (
                "ready", "qk_done", "qk_ready", "v_done", "v_copied", "kb_dve", "kb_pool", "rc_done", "rs_done",
                "s_done", "max_done", "sub_done", "exp_done", "ptr_done", "pt_copied", "pv_done", "rinv_done",
                "on_done", "otr_done", "oT_done"))
        QK_PER = 1 if rotary else 2
        S.ctx_used = v_done, 1
        block = c.enter_context(nc.Block())

        def spread_keys(eng, vec, groups, t, p, sem):
            eng.wait_ge(qk_ready, QK_PER * (t + 1))
            if exists(t - 2):
                eng.wait_ge(s_done, 2 * t - 2)
            for g in groups:
                r = slice(32 * g, 32 * g + 32)
                kv = QK[p][r, 1, :].rearrange("p (b k) -> p b k", b=NB)
                last = vec.tensor_tensor(
                    Kb[p][r, :, 4 * g:4 * g + 4, :], kv.unsqueeze(2).broadcast_to([32, NB, 4, SEQ]),
                    k["headmask"][r, :, :].unsqueeze(1).broadcast_to([32, NB, 4, SEQ]), ALU.mult)
                last.then_inc(sem, 1)
                if sem is kb_pool:
                    eng.wait_ge(sem, 2 * t + g - groups[0] + 1)

        @block.sync
        def _(sp):
            S.sp_program(sp, LAG)

        @block.gpsimd
        def _(pool):
            for p in range(2):
                nc.gpsimd.memset(Kb[p][:, :, :, :], 0.0).then_inc(ready, 1)
                for j in range(2):
                    r = slice(64 * j, 64 * j + 64)
                    pool.wait_ge(ready, 5 * p + 2 * j + 1)
                    nc.gpsimd.memset(V[p][r, :, j::2, 8:9], 1.0).then_inc(ready, 1)
                    pool.wait_ge(ready, 5 * p + 2 * j + 2)
                    nc.gpsimd.memset(V[p][r, :, 1 - j::2, 8:9], 0.0).then_inc(ready, 1)
                pool.wait_ge(ready, 5 * p + 5)

            def step(s, q):
                if live(s, 1):
                    S.ln_pow(pool, s - 1, 1 - q, k["minus_half"])
                if live(s, 2):
                    if live(s, 1):
                        pool.wait_ge(S.rstd_done, s)
                    spread_keys(pool, nc.gpsimd, (2, 3), s - 2, q, kb_pool)

            run_steps(pool, step, LAG)

        @block.tensor
        def _(pe):
            pe.wait_ge(ready, 10)

            def project(t, p):
                pe.wait_ge(S.xT_done, t + 1)
                pe.wait_ge(S.ctx_loaded[p], moved(t, p))
                if exists(t - 1):
                    pe.wait_ge(qk_ready, QK_PER * t)
                nc.tensor.matmul(psQK[:, 0:P], k[w + "wqT"][:, :], S.xT[p][:, :], start=True, stop=True)
                if rotary:
                    nc.tensor.matmul(psQK[:, 2 * P:3 * P], k[w + "wqrT"][:, :], S.xT[p][:, :], start=True, stop=True)
                    nc.tensor.matmul(psQK[:, 3 * P:4 * P], k[w + "wkrT"][:, :], S.ctxT[p][:, :], start=True, stop=True)
                nc.tensor.matmul(psQK[:, P:2 * P], k[w + "wkT"][:, :], S.ctxT[p][:, :], start=True, stop=True)\
                    .then_inc(qk_done, 1)
                if exists(t - 1):
                    pe.wait_ge(v_copied, t)
                for b in range(NB):
                    for j in range(2):
                        last = nc.tensor.matmul(psV[64 * j:64 * j + 64, b * P:(b + 1) * P],
                                                S.ctxT[p][:, 64 * b:64 * b + 64], k[w + "wvT2"][:, j, :],
                                                start=True, stop=True)
                last.then_inc(v_done, 1)

            def scores(t, p):
                pe.wait_ge(kb_dve, 2 * t + 2)
                pe.wait_ge(kb_pool, 2 * t + 2)
                for hf in range(2):
                    if exists(t - 1):
                        pe.wait_ge(sub_done, 2 * t + hf - 1)
                    for b in range(NB):
                        last = nc.tensor.matmul(psS[hf][64 * b:64 * b + 64, :], QK[p][:, 0, 64 * b:64 * b + 64],
                                                Kb[p][:, b, 8 * hf:8 * hf + 8, :], start=True, stop=True)
                    last.then_inc(s_done, 1)

            def values(t, p):
                for hf in range(2):
                    pe.wait_ge(exp_done, 2 * t + hf + 1)
                    if exists(t - 1):
                        pe.wait_ge(pt_copied, 2 * t + hf - 1)
                    for i in range(4):
                        last = nc.tensor.transpose(psT[hf][:, i * P:(i + 1) * P], E[p][:, hf, i * P:(i + 1) * P],
                                                   k["ident"][:, :])
                    last.then_inc(ptr_done, 1)
                pe.wait_ge(v_copied, t + 1)
                if exists(t - 1):
                    pe.wait_ge(on_done, t)
                if exists(t - 1):
                    pe.wait_ge(S.res_done, t)
                for i in range(PAIRS):
                    if i % 4 == 0:
                        pe.wait_ge(pt_copied, 2 * t + i // 4 + 1)
                    for b in range(NB):
                        last = nc.tensor.matmul(o9[64 * b:64 * b + 64, 2 * i:2 * i + 2, :],
                                                PT[p][:, i, 64 * b:64 * b + 64], V[p][:, b, 2 * i:2 * i + 2, :],
                                                start=True, stop=True)
                last.then_inc(pv_done, 1)

            def out_transpose(t, p):
                pe.wait_ge(on_done, t + 1)
                last_normed = min(t + 3, NT - 1) if isinstance(t, int) else t + 3
                pe.wait_ge(S.xT_done, last_normed + 1)
                nc.tensor.transpose(psX[:, P:2 * P], on[p][:, :], k["ident"][:, :]).then_inc(otr_done, 1)

            def out_project(t, p):
                pe.wait_ge(oT_done, t + 1)
                last = nc.tensor.matmul(psO[:, 0:P], oT[p][:, :], k[w + "woT"][:, :], start=True, stop=rotary)
                if not rotary:
                    last = nc.tensor.matmul(psO[:, 0:P], k["ones_row"][:, :], k[w + "bo"][:, :], start=False, stop=True)
                last.then_inc(S.o_done, 1)

            def step(s, q):
                if live(s, 2):
                    project(s - 2, q)
                if live(s, 5):
                    out_transpose(s - 5, 1 - q)
                if live(s, 3):
                    scores(s - 3, 1 - q)
                if live(s, 5):
                    out_project(s - 5, 1 - q)
                if live(s, 1):
                    if exists(s - 5):
                        pe.wait_ge(oT_done, s - 4)
                    S.x_transpose(pe, s - 1, 1 - q, psX, k["ident"])
                if live(s, 4):
                    values(s - 4, q)

            run_steps(pe, step, LAG)

        @block.scalar
        def _(act):
            act.wait_ge(ready, 10)

            def step(s, q):
                if live(s, 2) and not rotary:
                    t, p = s - 2, q
                    act.wait_ge(qk_done, t + 1)
                    if exists(t - 2):
                        act.wait_ge(s_done, 2 * t - 2)
                    if exists(t - 2):
                        act.wait_ge(kb_dve, 2 * t - 2)
                    if exists(t - 2):
                        act.wait_ge(kb_pool, 2 * t - 2)
                    nc.scalar.activation(QK[p][:, 0, :], psQK[:, 0:P], ACT.Identity, bias=k[w + "bq"][:, :],
                                         scale=8.0 ** -0.5).then_inc(qk_ready, 1)
                    nc.scalar.activation(QK[p][:, 1, :], psQK[:, P:2 * P], ACT.Identity, bias=k[w + "bk"][:, :])\
                        .then_inc(qk_ready, 1)
                if live(s, 5):
                    t, p = s - 5, 1 - q
                    act.wait_ge(otr_done, t + 1)
                    if exists(t - 2):
                        act.wait_ge(S.o_done, t - 1)
                    if rotary:
                        nc.scalar.copy(oT[p][:, :], psX[:, P:2 * P]).then_inc(oT_done, 1)
                    else:
                        nc.scalar.activation(oT[p][:, :], psX[:, P:2 * P], ACT.Identity, bias=k[w + "bv"][:, :])\
                            .then_inc(oT_done, 1)
                if live(s, 1):
                    t, p = s - 1, 1 - q
                    act.wait_ge(S.xtr_done, t + 1)
                    if exists(t - 2):
                        act.wait_ge(qk_done, t - 1)
                    nc.scalar.copy(S.xT[p][:, :], psX[:, 0:P]).then_inc(S.xT_done, 1)
                if live(s, 4):
                    t, p = s - 4, q
                    if exists(t - 2):
                        act.wait_ge(pv_done, t - 1)
                    for hf in range(2):
                        act.wait_ge(ptr_done, 2 * t + hf + 1)
                        nc.scalar.copy(PT[p][:, 4 * hf:4 * hf + 4, :].rearrange("p a b -> p (a b)"), psT[hf][:, :])\
                            .then_inc(pt_copied, 1)
                if live(s, 3):
                    t, p = s - 3, 1 - q
                    for hf in range(2):
                        act.wait_ge(sub_done, 2 * t + hf + 1)
                        nc.scalar.activation(E[p][:, hf, :], E[p][:, hf, :], ACT.Exp).then_inc(exp_done, 1)
                if live(s, 2):
                    t, p = s - 2, q
                    act.wait_ge(v_done, t + 1)
                    if exists(t - 2):
                        act.wait_ge(pv_done, t - 1)
                    nc.scalar.copy(V[p][:, :, :, 0:8], psV[:, 0:2 * P].rearrange("p (b h e) -> p b h e", b=NB, e=8))\
                        .then_inc(v_copied, 1)

            run_steps(act, step, LAG)

        @block.vector
        def _(dve):
            dve.wait_ge(ready, 10)

            def rotate(t, p):
                qk = psQK[:, 0:2 * P].rearrange("p (a s) -> p a s", a=2)
                qk_swapped = psQK[:, 2 * P:4 * P].rearrange("p (a s) -> p a s", a=2)
                dve.wait_ge(qk_done, t + 1)
                if exists(t - 2):
                    dve.wait_ge(qk_ready, t - 1)
                nc.vector.tensor_tensor(rc[p][:, :, :], qk, k["rope"][:, 0, :, :], ALU.mult).then_inc(rc_done, 1)
                nc.vector.tensor_tensor(rs[p][:, :, :], qk_swapped, k["rope"][:, 1, :, :], ALU.mult).then_inc(rs_done, 1)
                dve.wait_ge(rc_done, t + 1)
                dve.wait_ge(rs_done, t + 1)
                if exists(t - 2):
                    dve.wait_ge(s_done, 2 * t - 2)
                if exists(t - 2):
                    dve.wait_ge(kb_dve, 2 * t - 2)
                if exists(t - 2):
                    dve.wait_ge(kb_pool, 2 * t - 2)
                nc.vector.tensor_tensor(QK[p][:, :, :], rc[p][:, :, :], rs[p][:, :, :], ALU.add).then_inc(qk_ready, 1)

            def step(s, q):
                if live(s, 1):
                    S.ln_stats(dve, s - 1, 1 - q)
                if live(s, 2):
                    if rotary:
                        rotate(s - 2, q)
                    spread_keys(dve, nc.vector, (0, 1), s - 2, q, kb_dve)
                if live(s, 1):
                    S.ln_norm(dve, s - 1, 1 - q)
                if live(s, 3):
                    softmax_max_sub(dve, nc, rmax, E, psS, s - 3, 1 - q, s_done, max_done, sub_done, ptr_done)
                if live(s, 5):
                    S.add_residual(dve, s - 5, 1 - q, psO, load_gate(k, gate))
                if live(s, 4):
                    t, p = s - 4, q
                    dve.wait_ge(pv_done, t + 1)
                    if exists(t - 2):
                        dve.wait_ge(on_done, t - 1)
                    nc.vector.reciprocal(rinv[p][:, :].unsqueeze(2), o9[:, :, 8:9]).then_inc(rinv_done, 1)
                    dve.wait_ge(rinv_done, t + 1)
                    if exists(t - 2):
                        dve.wait_ge(otr_done, t - 1)
                    nc.vector.tensor_tensor(on[p][:, :].rearrange("p (h e) -> p h e", e=8), o9[:, :, 0:8],
                                            rinv[p][:, :].unsqueeze(2).broadcast_to([P, NH, 8]), ALU.mult)\
                        .then_inc(on_done, 1)

            run_steps(dve, step, LAG)


def layer2_ffn(nc, k, src, dst):
    with ExitStack() as c:
        S = Stream(nc, c, "f2", src, dst)
        xpad = S.two("xpad", [P, NB, SEQ + 1])
        thr, kr, k2, mixed = (S.two(n, [P, P]) for n in ("thr", "kr", "k2", "mixed"))
        psX, psR, psK, psO = (S.bank(n) for n in ("psX", "psR", "psK", "psO"))
        ready, r_done, k_done, thr_done, kr_done, k2_done, mixed_done = (S.sem(n) for n in (
            "ready", "r_done", "k_done", "thr_done", "kr_done", "k2_done", "mixed_done"))
        block = c.enter_context(nc.Block())

        @block.sync
        def _(sp):
            S.sp_program(sp)

        @block.gpsimd
        def _(pool):
            for p in range(2):
                nc.gpsimd.memset(xpad[p][:, :, :], 0.0).then_inc(ready, 1)

            def step(s, q):
                if live(s, 1):
                    S.ln_pow(pool, s - 1, 1 - q, k["minus_half"])

            run_steps(pool, step)

        @block.tensor
        def _(pe):
            pe.wait_ge(ready, 2)

            def hidden(t, p):
                now, before = xpad[p][:, :, 1:1 + SEQ], xpad[p][:, :, 0:SEQ]
                pe.wait_ge(S.xT_done, t + 1)
                if exists(t - 1):
                    pe.wait_ge(thr_done, t)
                for x, wx, first in ((now, "wr0", True), (before, "wr1", False)):
                    for b in range(NB):
                        last = nc.tensor.matmul(psR[64 * b:64 * b + 64, 0:P], x[:, b, :], k[wx][:, :],
                                                start=first, stop=not first)
                last.then_inc(r_done, 1)
                if exists(t - 1):
                    pe.wait_ge(kr_done, t)
                psk = psK[:, 0:P].rearrange("p (b s) -> p b s", b=NB)
                nc.tensor.matmul(psk, k["wk0"][:, :], now, start=True, stop=False)
                nc.tensor.matmul(psk, k["wk1"][:, :], before, start=False, stop=True).then_inc(k_done, 1)

            def step(s, q):
                if live(s, 2):
                    hidden(s - 2, q)
                if live(s, 1):
                    S.x_transpose(pe, s - 1, 1 - q, psX, k["ident"])
                if live(s, 3):
                    t, p = s - 3, 1 - q
                    pe.wait_ge(k2_done, t + 1)
                    if exists(t - 1):
                        pe.wait_ge(mixed_done, t)
                    nc.tensor.matmul(psO[:, 0:P], k2[p][:, :], k["l2_wvfT"][:, :], start=True, stop=True)\
                        .then_inc(S.o_done, 1)

            run_steps(pe, step)

        @block.scalar
        def _(act):
            act.wait_ge(ready, 2)

            def step(s, q):
                if live(s, 2):
                    t, p = s - 2, q
                    act.wait_ge(r_done, t + 1)
                    if exists(t - 2):
                        act.wait_ge(mixed_done, t - 1)
                    nc.scalar.activation(thr[p][:, :], psR[:, 0:P], ACT.Tanh, scale=0.5).then_inc(thr_done, 1)
                    act.wait_ge(k_done, t + 1)
                    if exists(t - 2):
                        act.wait_ge(k2_done, t - 1)
                    nc.scalar.activation(kr[p][:, :], psK[:, 0:P], ACT.Relu).then_inc(kr_done, 1)
                if live(s, 1):
                    t, p = s - 1, 1 - q
                    act.wait_ge(S.xtr_done, t + 1)
                    if exists(t - 2):
                        act.wait_ge(k_done, t - 1)
                    nc.scalar.copy(xpad[p][:, :, 1:1 + SEQ], psX[:, 0:P].rearrange("p (b s) -> p b s", b=NB))\
                        .then_inc(S.xT_done, 1)

            run_steps(act, step)

        @block.vector
        def _(dve):
            def step(s, q):
                if live(s, 1):
                    S.ln_stats(dve, s - 1, 1 - q)
                if live(s, 2):
                    t, p = s - 2, q
                    dve.wait_ge(kr_done, t + 1)
                    if exists(t - 2):
                        dve.wait_ge(S.o_done, t - 1)
                    nc.vector.tensor_tensor(k2[p][:, :], kr[p][:, :], kr[p][:, :], ALU.mult).then_inc(k2_done, 1)
                if live(s, 1):
                    S.ln_norm(dve, s - 1, 1 - q)
                if live(s, 3):
                    t, p = s - 3, 1 - q
                    dve.wait_ge(S.o_done, t + 1)
                    dve.wait_ge(thr_done, t + 1)
                    if exists(t - 2):
                        dve.wait_ge(S.res_done, t - 1)
                    nc.vector.scalar_tensor_tensor(mixed[p][:, :], thr[p][:, :], 1.0, psO[:, 0:P], ALU.add, ALU.mult)\
                        .then_inc(mixed_done, 1)
                    dve.wait_ge(mixed_done, t + 1)
                    S.add_residual(dve, t, p, mixed[p], k["half_gate"][:, 6:7])

            run_steps(dve, step)


def layer3_ffn(nc, k, src, dst):
    with ExitStack() as c:
        S = Stream(nc, c, "f3", src, dst)
        lead = S.two("lead", [P, 32])
        t1 = S.two("t1", [33, P])
        t2 = S.two("t2", [P, P])
        down_rows = S.two("down_rows", [P, P])
        Hd = S.two("Hd", [P, HID])
        psX, psA, psB, psH, psD, psO = (S.bank(n) for n in ("psX", "psA", "psB", "psH", "psD", "psO"))
        ready, ab_done, t1_done, up_done, rows_done, h_done, gelu_done, d_done, t2_done, copied = (S.sem(n) for n in (
            "ready", "ab_done", "t1_done", "up_done", "rows_done", "h_done", "gelu_done", "d_done", "t2_done", "copied"))
        block = c.enter_context(nc.Block())

        @block.sync
        def _(sp):
            S.sp_program(sp)

        @block.gpsimd
        def _(pool):
            for p in range(2):
                nc.gpsimd.memset(t1[p][32:33, :], 1.0).then_inc(ready, 1)
            pool.wait_ge(ready, 2)

            def step(s, q):
                if live(s, 1):
                    S.ln_pow(pool, s - 1, 1 - q, k["minus_half"])

            run_steps(pool, step)

        @block.tensor
        def _(pe):
            pe.wait_ge(ready, 2)

            def rank(t, p):
                pe.wait_ge(S.xT_done, t + 1)
                pe.wait_ge(copied, t + 1)
                if exists(t - 1):
                    pe.wait_ge(t1_done, t)
                if exists(t - 1):
                    pe.wait_ge(up_done, t)
                if exists(t - 1):
                    pe.wait_ge(rows_done, t)
                nc.tensor.matmul(psA[0:32, 0:P], lead[p][:, :], S.xT[p][:, :], start=True, stop=True)
                nc.tensor.matmul(psA[0:32, P:2 * P], k["sel_token"][:, :], S.xh[p][:, :], start=True, stop=True)
                xs = S.xh[p][:, :].rearrange("p (r j) -> p j r", j=CH)
                for j in range(CH):
                    last = nc.tensor.matmul(psB[32 * j:32 * j + 32, 0:32], k["sel_token"][:, :], xs[:, j, :],
                                            start=True, stop=True)
                last.then_inc(ab_done, 1)

            def hidden(t, p):
                pe.wait_ge(t1_done, t + 1)
                pe.wait_ge(up_done, t + 1)
                if exists(t - 1):
                    pe.wait_ge(gelu_done, t)
                for i in range(CH):
                    nc.tensor.matmul(psH[:, i * P:(i + 1) * P], k["l3_w1T"][:, i * P:(i + 1) * P], S.xT[p][:, :],
                                     start=True, stop=False)
                    last = nc.tensor.matmul(psH[:, i * P:(i + 1) * P], k["lora_up"][p][:, i * P:(i + 1) * P],
                                            t1[p][:, :], start=False, stop=True)
                last.then_inc(h_done, 1)

            def down(t, p):
                pe.wait_ge(gelu_done, t + 1)
                if exists(t - 1):
                    pe.wait_ge(t2_done, t)
                for j in range(CH):
                    last = nc.tensor.matmul(psD[32 * j:32 * j + 32, 0:P], lead[p][:, :], Hd[p][:, j * P:(j + 1) * P],
                                            start=True, stop=True)
                last.then_inc(d_done, 1)
                if exists(t - 1):
                    pe.wait_ge(S.res_done, t)
                for i in range(CH):
                    nc.tensor.matmul(psO[:, 0:P], Hd[p][:, i * P:(i + 1) * P], k["l3_w2T"][:, i, :],
                                     start=(i == 0), stop=False)
                nc.tensor.matmul(psO[:, 0:P], k["ones_row"][:, :], k["l3_b2"][:, :], start=False, stop=False)
                pe.wait_ge(t2_done, t + 1)
                pe.wait_ge(rows_done, t + 1)
                nc.tensor.matmul(psO[:, 0:P], t2[p][:, :], down_rows[p][:, :], start=False, stop=True)\
                    .then_inc(S.o_done, 1)

            def step(s, q):
                if live(s, 2):
                    rank(s - 2, q)
                if live(s, 3):
                    down(s - 3, 1 - q)
                if live(s, 2):
                    hidden(s - 2, q)
                if live(s, 1):
                    S.x_transpose(pe, s - 1, 1 - q, psX, k["ident"])

            run_steps(pe, step)

        @block.scalar
        def _(act):
            def step(s, q):
                if live(s, 2):
                    t, p = s - 2, q
                    act.wait_ge(h_done, t + 1)
                    if exists(t - 2):
                        act.wait_ge(S.o_done, t - 1)
                    nc.scalar.activation(Hd[p][:, :], psH[:, :], ACT.Gelu).then_inc(gelu_done, 1)
                if live(s, 1):
                    t, p = s - 1, 1 - q
                    act.wait_ge(S.xtr_done, t + 1)
                    if exists(t - 2):
                        act.wait_ge(d_done, t - 1)
                    if exists(t - 2):
                        act.wait_ge(h_done, t - 1)
                    nc.scalar.copy(S.xT[p][:, :], psX[:, 0:P]).then_inc(copied, 1)
                    nc.scalar.copy(lead[p][:, :].rearrange("p (b s) -> p b s", b=NB),
                                   psX[:, 0:P].rearrange("p (b s) -> p b s", b=NB)[:, :, 1:17])\
                        .then_inc(S.xT_done, 1)

            run_steps(act, step)

        @block.vector
        def _(dve):
            def step(s, q):
                if live(s, 2):
                    t, p = s - 2, q
                    dve.wait_ge(ab_done, t + 1)
                    if exists(t - 2):
                        dve.wait_ge(h_done, t - 1)
                    nc.vector.tensor_tensor(t1[p][0:32, :], psA[0:32, 0:P], k["mask_up"][:, :], ALU.mult)\
                        .then_inc(t1_done, 1)
                    nc.vector.tensor_tensor(
                        k["lora_up"][p][0:32, :].rearrange("p (i c) -> p i c", i=CH),
                        psA[0:32, P:2 * P].unsqueeze(1).broadcast_to([32, CH, P]), k["sel_up"][:, :, :], ALU.mult)\
                        .then_inc(up_done, 1)
                    if exists(t - 2):
                        dve.wait_ge(S.o_done, t - 1)
                    nc.vector.tensor_tensor(
                        down_rows[p][:, :].rearrange("p (i r) -> p i r", i=CH),
                        psB[:, 0:32].unsqueeze(1).broadcast_to([P, CH, 32]), k["sel_down"][:, :, :], ALU.mult)\
                        .then_inc(rows_done, 1)
                if live(s, 1):
                    S.ln_stats(dve, s - 1, 1 - q)
                if live(s, 3):
                    t, p = s - 3, 1 - q
                    dve.wait_ge(d_done, t + 1)
                    if exists(t - 2):
                        dve.wait_ge(S.o_done, t - 1)
                    nc.vector.tensor_tensor(t2[p][:, :], psD[:, 0:P], k["mask_down"][:, :], ALU.mult)\
                        .then_inc(t2_done, 1)
                if live(s, 1):
                    if exists(s - 3):
                        dve.wait_ge(ab_done, s - 2)
                    S.ln_norm(dve, s - 1, 1 - q)
                if live(s, 3):
                    S.add_residual(dve, s - 3, 1 - q, psO, load_gate(k, 7))

            run_steps(dve, step)


def build(nc, w, out):
    with ExitStack() as c:
        X = c.enter_context(nc.sbuf_tensor("residual", [P, NT * P], F32))
        k = prepare(nc, c, w)

        def x_tile(row):
            return w["x"][bass.ds(row, P), :]

        def resident(row):
            return X[:, bass.ds(row, P)]

        def ctx_tile(row):
            return w["ctxT"][:, bass.ds(row, P)]

        def out_tile(row):
            return out[bass.ds(row, P), :]

        layer0_attention(nc, k, x_tile, resident, ctx_tile)
        layer0_ffn(nc, k, resident, resident)
        layer1_attention(nc, k, resident, resident, ctx_tile)
        layer1_ffn(nc, k, resident, resident)
        small_head_attention(nc, k, "a2", resident, resident, ctx_tile, "l2_", False, 2)
        layer2_ffn(nc, k, resident, resident)
        small_head_attention(nc, k, "a3", resident, resident, ctx_tile, "l3_", True, 3)
        layer3_ffn(nc, k, resident, out_tile)


def shape_constants():
    c = {}
    tok, seq = np.arange(P), np.arange(P) // SEQ
    c["ident"] = np.eye(P, dtype=np.float32)
    seen = (seq[:, None] == seq[None, :]) & (tok[None, :] <= tok[:, None])
    c["causal"] = np.where(seen, 0.0, -1e30).astype(np.float32)
    c["desc"] = np.broadcast_to(np.arange(NE, 0, -1, dtype=np.float32), (P, NE)).copy()
    row = np.arange(P)
    c["headmask"] = np.broadcast_to(((row // 8) % 4)[:, None, None] == np.arange(4)[None, :, None],
                                    (P, 4, SEQ)).astype(np.float32)
    inv = (1.0 / 10000.0 ** (np.arange(0, 8, 2, dtype=np.float32) / 8)).astype(np.float32)
    angle = (tok % SEQ).astype(np.float32)[None, :] * inv[row % 4][:, None]
    sign = np.where(row % 8 < 4, -1.0, 1.0)[:, None]
    cos, sin = np.cos(angle), np.sin(angle) * sign
    q = 8.0 ** -0.5
    c["rope"] = np.stack([np.stack([cos * q, cos], 1), np.stack([sin * q, sin], 1)], 1).astype(np.float32)
    b32, n32 = np.arange(32) // 16, np.arange(32) % 16
    c["mask_up"] = ((b32[:, None] == seq[None, :]) & (n32 % 2 == 1)[:, None] & (n32 < 8)[:, None]).astype(np.float32)
    down = (b32[:, None] == seq[None, :]) & (n32 % 2 == 1)[:, None] & (n32 > 8)[:, None]
    c["mask_down"] = np.tile(down, (4, 1)).astype(np.float32)
    c["sel_token"] = (tok[:, None] == (SEQ * b32 + n32)[None, :]).astype(np.float32)
    i = np.arange(CH)
    c["sel_up"] = np.broadcast_to((n32[:, None] == 2 * i + 1)[:, :, None], (32, CH, P)).astype(np.float32)
    c["sel_down"] = np.broadcast_to(np.tile(n32[:, None] == 2 * i + 9, (4, 1))[:, :, None], (P, CH, 32))\
        .astype(np.float32)
    return c


def lay_out(v):
    def t(a):
        return np.ascontiguousarray(np.asarray(a).T)

    def rows(a):
        a = np.asarray(a)
        return np.ascontiguousarray(a.reshape(-1, P, a.shape[-1]).transpose(1, 0, 2))

    def parity(a):
        a = t(a).reshape(P, PAIRS, 2, 8)
        z = np.zeros((P, 2, PAIRS, 2, 8), a.dtype)
        for j in range(2):
            z[:, j, :, j, :] = a[:, :, j, :]
        return z.reshape(P, 2, P)

    swap = np.arange(P) ^ 4
    d = shape_constants()
    d["x"] = np.asarray(v["x"]).reshape(NT * P, P)
    d["ctxT"] = t(np.asarray(v["ctx_1024"]).reshape(NT * P, P))
    g = np.concatenate([np.asarray(v["g_xattn"]), np.asarray(v["g_ffn"])])
    d["gates"] = np.broadcast_to(g, (P, 8)).copy()
    d["l0_wqT"], d["l0_wkT"], d["l0_wv"] = t(v["L0_xattn_w_q"]), t(v["L0_xattn_w_k"]), np.asarray(v["L0_xattn_w_v"])
    d["l0_w1T"] = t(v["L0_ffn_w1"]).reshape(P, CH, P)
    d["l0_convw"] = np.broadcast_to(t(np.asarray(v["L0_ffn_conv_w"])[:, 0, :]), (P, 3, HID)).copy()
    d["l0_convb"] = np.asarray(v["L0_ffn_conv_b"]).reshape(1, HID)
    d["l0_w2T"] = rows(t(v["L0_ffn_w2"]))
    for n in "qkv":
        d[f"l1_w{n}T"] = rows(t(np.asarray(v[f"L1_xattn_W{n}"]).reshape(P, -1)))
    d["l1_wo"] = rows(np.asarray(v["L1_xattn_Wo"]).reshape(-1, P))
    d["l1_gateT"] = t(v["L1_ffn_gate_w"])
    d["l1_wgT"] = t(np.asarray(v["L1_ffn_w_gate"]).reshape(HID, P))
    d["l1_wuT"] = t(np.asarray(v["L1_ffn_w_up"]).reshape(HID, P))
    d["l1_wdT"] = rows(np.asarray(v["L1_ffn_w_down"]).transpose(0, 2, 1).reshape(HID, P))
    for n in ("2", "3"):
        a = f"L{n}_xattn_W"
        d[f"l{n}_wqT"], d[f"l{n}_wkT"], d[f"l{n}_woT"] = t(v[a + "q"]), t(v[a + "k"]), t(v[a + "o"])
        d[f"l{n}_wvT2"] = parity(v[a + "v"])
    d["l3_wqrT"], d["l3_wkrT"] = t(np.asarray(v["L3_xattn_Wq"])[swap]), t(np.asarray(v["L3_xattn_Wk"])[swap])
    for n in "qkv":
        d["l2_b" + n] = np.asarray(v["L2_xattn_b" + n]).reshape(P, 1)
    d["l2_bo"] = np.asarray(v["L2_xattn_bo"]).reshape(1, P)
    d["l2_wrT"], d["l2_wkfT"], d["l2_wvfT"] = t(v["L2_ffn_W_r"]), t(v["L2_ffn_W_k"]), t(v["L2_ffn_W_v"])
    d["l2_mur"], d["l2_muk"] = np.asarray(v["L2_ffn_mu_r"]).reshape(P, 1), np.asarray(v["L2_ffn_mu_k"]).reshape(P, 1)
    d["l3_w1T"], d["l3_w2T"] = t(v["L3_ffn_W1"]), rows(t(v["L3_ffn_W2"]))
    d["l3_b1"], d["l3_b2"] = np.asarray(v["L3_ffn_b1"]).reshape(1, HID), np.asarray(v["L3_ffn_b2"]).reshape(1, P)
    d["l3_scale"] = np.broadcast_to(np.asarray(v["L3_ffn_scale"]).reshape(1, 1), (P, 1)).copy()
    return {n: np.ascontiguousarray(a) for n, a in d.items()}


def kernel(**inputs):
    import concourse.bacc as bacc
    from concourse.bass_utils import run_bass_kernel_spmd

    nc = bacc.Bacc("TRN2", target_bir_lowering=False, num_devices=1)
    arrays, w = {}, {}
    for name, a in lay_out(inputs).items():
        arrays[f"in_{name}"] = a
        w[name] = nc.dram_tensor(f"in_{name}", a.shape, mybir.dt.from_np(a.dtype), kind="ExternalInput").ap()
    out = nc.dram_tensor("out_x", (NT * P, P), F32, kind="ExternalOutput").ap()
    build(nc, w, out)
    r = run_bass_kernel_spmd(nc, [arrays], core_ids=[0])
    return r.results[0]["out_x"].reshape(NT * P // SEQ, SEQ, P)
```

```python
from contextlib import ExitStack

import numpy as np

import concourse.bass as bass
from concourse import mybir

F32 = mybir.dt.float32
BF16 = mybir.dt.bfloat16
ALU = mybir.AluOpType
ACT = mybir.ActivationFunctionType
AX = mybir.AxisListType

P = 128
SEQ = 64
NB = P // SEQ
NT = 32
NH = 16
PAIRS = NH // 2
HID = 512
CH = HID // P
NE = 8
EPS = 1e-5
MAGIC = 12582912.0


def live(s, lag):
    return not isinstance(s, int) or 0 <= s - lag < NT


def exists(t):
    return not isinstance(t, int) or t >= 0


def moved(t, p):
    return t * 8 + (16 - 8 * p)


def run_steps(eng, step, last_lag=5):
    peel = last_lag + 2 + last_lag % 2
    for s in range(peel):
        step(s, s % 2)
    with eng.Fori(peel, NT - 1, 2) as s:
        step(s, 0)
        step(s + 1, 1)
    for s in range(NT, NT + last_lag):
        step(s, s % 2)


def semaphores(nc, c):
    taken = []

    def close():
        nc.clear_and_free_semaphores(taken)
        nc.all_engine_barrier()

    def allocate(name):
        taken.append(nc.alloc_semaphore(name=name))
        return taken[-1]

    c.callback(close)
    return allocate


class Stream:

    def __init__(self, nc, c, name, src, dst, ctx=None):
        self.nc, self.c, self.name, self.src, self.dst, self.ctx_src = nc, c, name, src, dst, ctx
        self.allocate = semaphores(nc, c)
        self.xin = self.two("xin", [P, P])
        self.xres = self.two("xres", [P, P])
        self.xout = self.two("xout", [P, P])
        self.xh = self.two("xh", [P, P])
        self.xT = self.two("xT", [P, P])
        self.bn = self.two("bn", [P, 6])
        self.mv = self.two("mv", [P, 2])
        self.var = self.two("var", [P, 1])
        self.rstd = self.two("rstd", [P, 1])
        self.x_loaded = self.sems("x_loaded")
        self.res_loaded = self.sems("res_loaded")
        self.stored = self.sems("stored")
        if ctx is not None:
            self.ctxT = self.two("ctxT", [P, P])
            self.ctx_loaded = self.sems("ctx_loaded")
            self.ctx_used = None
        self.bn_done = self.sem("bn_done")
        self.bn_waited = self.sem("bn_waited")
        self.mv_done = self.sem("mv_done")
        self.var_done = self.sem("var_done")
        self.rstd_done = self.sem("rstd_done")
        self.xh_done = self.sem("xh_done")
        self.xtr_done = self.sem("xtr_done")
        self.xT_done = self.sem("xT_done")
        self.o_done = self.sem("o_done")
        self.res_done = self.sem("res_done")

    def sem(self, n):
        return self.allocate(f"{self.name}_{n}")

    def sems(self, n):
        return [self.sem(f"{n}{i}") for i in range(2)]

    def sb(self, n, shape, dt=F32):
        return self.c.enter_context(self.nc.sbuf_tensor(f"{self.name}_{n}", shape, dt))

    def two(self, n, shape, dt=F32):
        return [self.sb(f"{n}{i}", shape, dt) for i in range(2)]

    def bank(self, n, dt=F32):
        return self.c.enter_context(
            self.nc.psum_tensor(f"{self.name}_{n}", [P, 512 if dt == F32 else 1024], dt))

    def own_wait(self, eng, t):
        if not isinstance(t, int):
            eng.wait_ge(self.x_loaded[0], 16)

    def load(self, sp, t, p, row):
        self.own_wait(sp, t)
        if exists(t - 2):
            sp.wait_ge(self.xh_done, t - 1)
        sp.dma_start(self.xin[p][:, :], self.src(row)).then_inc(self.x_loaded[p], 16)

    def load_ctx(self, sp, t, p, row):
        self.own_wait(sp, t)
        if exists(t - 2):
            sp.wait_ge(self.ctx_used[0], self.ctx_used[1] * (t - 1))
        sp.dma_start(self.ctxT[p][:, :], self.ctx_src(row)).then_inc(self.ctx_loaded[p], 16)

    def load_res(self, sp, t, p, row):
        self.own_wait(sp, t)
        if exists(t - 2):
            sp.wait_ge(self.res_done, t - 1)
        sp.dma_start(self.xres[p][:, :], self.src(row)).then_inc(self.res_loaded[p], 16)

    def store(self, sp, t, p, row):
        self.own_wait(sp, t)
        sp.wait_ge(self.res_done, t + 1)
        sp.dma_start(self.dst(row), self.xout[p][:, :]).then_inc(self.stored[p], 16)

    def sp_program(self, sp, last_lag=5, ctx_lag=1):
        def step(s, q):
            row = {lag: (s - lag) * P if isinstance(s, int) else sp.snap((s - lag) * P)
                   for lag in {0, ctx_lag, last_lag - 2, last_lag}}
            if live(s, 0):
                self.load(sp, s, q, row[0])
            if self.ctx_src is not None:
                if live(s, ctx_lag):
                    self.load_ctx(sp, s - ctx_lag, (q + ctx_lag) % 2, row[ctx_lag])
            if live(s, last_lag - 2):
                self.load_res(sp, s - (last_lag - 2), (q + last_lag) % 2, row[last_lag - 2])
            if live(s, last_lag):
                self.store(sp, s - last_lag, (q + last_lag) % 2, row[last_lag])

        run_steps(sp, step, last_lag)
        for p in range(2):
            sp.wait_ge(self.stored[p], moved(NT - 2 + p, p))

    def ln_stats(self, dve, t, p):
        self.bn_first(dve, t, p)
        self.bn_second(dve, t, p)
        self.bn_third(dve, t, p)

    def bn_first(self, dve, t, p):
        dve.wait_ge(self.x_loaded[p], moved(t, p))
        self.nc.vector.bn_stats(self.bn[p][:, :], self.xin[p][:, :]).then_inc(self.bn_done, 1)

    def bn_second(self, dve, t, p):
        dve.wait_ge(self.bn_done, t + 1)
        dve.sem_inc(self.bn_waited, 1)
        self.nc.vector.bn_aggr(self.mv[p][:, :], self.bn[p][:, :]).then_inc(self.mv_done, 1)

    def bn_third(self, dve, t, p):
        dve.wait_ge(self.mv_done, t + 1)
        if exists(t - 2):
            dve.wait_ge(self.rstd_done, t - 1)
        self.nc.vector.tensor_scalar_add(self.var[p][:, :], self.mv[p][:, 1:2], EPS).then_inc(self.var_done, 1)

    def ln_pow(self, pool, t, p, minus_half):
        pool.wait_ge(self.var_done, t + 1)
        if exists(t - 2):
            pool.wait_ge(self.xh_done, t - 1)
        self.nc.gpsimd.tensor_tensor(self.rstd[p][:, :], self.var[p][:, :], minus_half[:, :],
                                     ALU.pow).then_inc(self.rstd_done, 1)

    def ln_norm(self, dve, t, p):
        dve.wait_ge(self.rstd_done, t + 1)
        if exists(t - 2):
            dve.wait_ge(self.xtr_done, t - 1)
        self.nc.vector.tensor_scalar(self.xh[p][:, :], self.xin[p][:, :], self.mv[p][:, 0:1],
                                     self.rstd[p][:, :], ALU.subtract, ALU.mult).then_inc(self.xh_done, 1)

    def x_transpose(self, pe, t, p, psX, ident, ready=None, src=None):
        pe.wait_ge(ready or self.xh_done, t + 1)
        if exists(t - 1):
            pe.wait_ge(self.xT_done, t)
        self.nc.tensor.transpose(psX[:, 0:P], (src or self.xh)[p][:, :], ident[:, :]).then_inc(self.xtr_done, 1)

    def x_copy(self, act, t, p, psX, used, per):
        act.wait_ge(self.xtr_done, t + 1)
        if exists(t - 2):
            act.wait_ge(used, per * (t - 1))
        self.nc.scalar.copy(self.xT[p][:, :], psX[:, 0:P]).then_inc(self.xT_done, 1)

    def add_residual(self, dve, t, p, psO, coef):
        dve.wait_ge(self.o_done, t + 1)
        dve.wait_ge(self.res_loaded[p], moved(t, p))
        if exists(t - 2):
            dve.wait_ge(self.stored[p], moved(t - 2, p))
        self.nc.vector.scalar_tensor_tensor(self.xout[p][:, :], psO[:, 0:P], coef, self.xres[p][:, :],
                                            ALU.mult, ALU.add).then_inc(self.res_done, 1)


def prepare(nc, c, w):
    def sb(name, shape, dt=F32):
        return c.enter_context(nc.sbuf_tensor(name, shape, dt))

    keep, loads = {}, []

    def load(stack, name, shape):
        t = stack.enter_context(nc.sbuf_tensor("w_" + name, shape, F32))
        keep[name] = t
        loads.append((t[:], w[name]))
        return t

    ident = load(c, "ident", [P, P])
    for n, shape in (("l0_wv", [P, P]), ("causal", [P, P]),
                     ("l1_gateT", [P, NE]), ("l1_wgT", [P, HID]), ("l1_wuT", [P, HID]),
                     ("l1_wdT", [P, CH, P]), ("desc", [P, NE]),
                     ("l2_wqT", [P, P]), ("l2_wkT", [P, P]), ("l2_wvT2", [P, 2, P]), ("l2_woT", [P, P]),
                     ("l2_bq", [P, 1]), ("l2_bk", [P, 1]), ("l2_bv", [P, 1]), 
                     ("l2_wrT", [P, P]), ("l2_wkfT", [P, P]), ("l2_wvfT", [P, P]),
                     ("l2_mur", [P, 1]), ("l2_muk", [P, 1]),
                     ("l3_wqT", [P, P]), ("l3_wkT", [P, P]), ("l3_wqrT", [P, P]), ("l3_wkrT", [P, P]),
                     ("l3_wvT2", [P, 2, P]), ("l3_woT", [P, P]), ("rope", [P, 2, 2, P]),
                     ("jmask", [P, 4]),
                     ("l3_w1T", [P, HID]), ("l3_w2T", [P, CH, P]),
                     ("l3_scale", [P, 1]), ("mask_up", [32, P]), ("mask_down", [P, P]),
                     ("sel_token", [P, 32]), ("sel_up", [32, CH, P]), ("sel_down", [P, CH, 32])):
        load(c, n, shape)
    lora_up = sb("lora_up0", [P, HID]), sb("lora_up1", [P, HID])
    for i in range(2):
        loads.append((lora_up[i][32:P, :], w["l3_b1"]))
    keep["lora_up"] = lora_up

    tg = sb("tanh_gates", [P, 8])
    half_gate = sb("half_gate", [P, 8])
    A0 = sb("A0", [P, P])
    AT = sb("AT", [P, NH, P])
    B = sb("B", [P, 2, PAIRS, P])
    WJ = sb("WJ", [P, 3, HID])
    tern2 = sb("tern2", [P, CH, P], BF16)
    bias3 = sb("bias3", [P, HID + 2 * P], BF16)
    ones_bf = sb("ones_bf", [P, P], BF16)
    minus_half = sb("minus_half", [P, 1])
    coef2 = sb("coef2", [P, 1])
    mu = {n: sb("l2f_" + n, [P, P]) for n in ("wr0", "wr1", "wk0", "wk1")}
    keep.update(tg=tg, A0=A0, AT=AT, B=B, WJ=WJ, tern2=tern2, bias3=bias3, ones_bf=ones_bf,
                minus_half=minus_half, coef2=coef2, half_gate=half_gate, **mu)

    with ExitStack() as pc:
        def tmp(name, shape, dt=F32):
            return pc.enter_context(nc.sbuf_tensor(name, shape, dt))

        sem = semaphores(nc, pc)

        gates = load(pc, "gates", [P, 8])
        l0_wqT, l0_wkT = load(pc, "l0_wqT", [P, P]), load(pc, "l0_wkT", [P, P])
        w1T, w2T = load(pc, "l0_w1T", [P, CH, P]), load(pc, "l0_w2T", [P, CH, P])
        cw, cb = load(pc, "l0_convw", [P, 3, HID]), load(pc, "row_biases", [1, HID + 2 * P])
        l1_wqT, l1_wkT, l1_wvT, l1_wo = (load(pc, "l1_" + n, [P, PAIRS, P]) for n in ("wqT", "wkT", "wvT", "wo"))
        onesf = tmp("onesf", [P, P])
        asum = tmp("asum", [P, 4])
        small = tmp("small", [P, 12])
        wr = tmp("wrounded", [P, CH, P])
        rowt = tmp("rowt", [1, 2, HID + 2 * P])
        rowb = tmp("rowb", [1, 2, HID + 2 * P], BF16)
        ps = [pc.enter_context(nc.psum_tensor(f"prep_ps{i}", [P, 512], F32)) for i in range(4)]
        loaded, filled, sums_ready, summed, chain, done = (
            sem("prep_" + n) for n in ("loaded", "filled", "sums_ready", "summed", "chain", "done"))
        prod, copied, tanhed = sem("prep_prod"), sem("prep_copied"), sem("prep_tanhed")

        groups = [([(l0_wqT[:, :], l0_wkT[:, :])], A0[:, :].unsqueeze(1), float(P) ** -0.5)]
        for j in range(2):
            for q in range(0, PAIRS, 4):
                r = slice(64 * j, 64 * j + 64)
                part = [(l1_wkT[r, i, :], l1_wqT[r, i, :]) for i in range(q, q + 4)]
                groups.append((part, AT[:, :, :].rearrange("p (a j) b -> p a j b", j=2)[:, q:q + 4, j, :], 0.125))
                part = [(l1_wvT[r, i, :], l1_wo[r, i, :]) for i in range(q, q + 4)]
                groups.append((part, B[:, j, q:q + 4, :], 1.0))

        with nc.Block() as block:
            @block.sync
            def _(sp):
                for dst, src in loads:
                    sp.dma_start(dst, src).then_inc(loaded, 16)

            @block.tensor
            def _(pe):
                pe.wait_ge(loaded, 16 * len(loads))
                for g, (part, _, _) in enumerate(groups):
                    if g >= 3:
                        pe.wait_ge(copied, g - 2)
                    for i, (lhsT, rhs) in enumerate(part):
                        last = nc.tensor.matmul(ps[g % 3][:, i * P:(i + 1) * P], lhsT, rhs, start=True, stop=True)
                    last.then_inc(prod, 1)
                pe.wait_ge(filled, 1)
                pe.wait_ge(sums_ready, 2)
                nc.tensor.matmul(ps[3][:, 0:2], onesf[:, :], asum[:, 0:2], start=True, stop=True).then_inc(summed, 1)

            @block.scalar
            def _(act):
                act.wait_ge(loaded, 16 * len(loads))
                nc.scalar.activation(tg[:, :], gates[:, :], ACT.Tanh).then_inc(tanhed, 1)
                for g, (_, out, scale) in enumerate(groups):
                    act.wait_ge(prod, g + 1)
                    n = out.shape[1]
                    nc.scalar.activation(out, ps[g % 3][:, 0:n * P].rearrange("p (a b) -> p a b", a=n), ACT.Copy,
                                         scale=scale).then_inc(copied, 1)

            @block.vector
            def _(dve):
                links = [0]

                def link(ins):
                    links[0] += 1
                    ins.then_inc(chain, 1)
                    dve.wait_ge(chain, links[0])

                nc.vector.memset(onesf[:, :], 1.0).then_inc(filled, 1)
                nc.vector.memset(ones_bf[:, :], 1.0)
                nc.vector.memset(minus_half[:, :], -0.5)
                link(nc.vector.memset(bias3[:, :], 0.0))
                dve.wait_ge(loaded, 16 * len(loads))
                for i, wx in enumerate((w1T, w2T)):
                    nc.vector.tensor_reduce(asum[:, i:i + 1], wx[:, :, :], AX.XY, ALU.add,
                                            apply_absolute_value=True).then_inc(sums_ready, 1)
                link(nc.vector.tensor_copy(rowb[:, 0, :], cb[:, :]))
                nc.vector.tensor_copy(bias3[0:1, :], rowb[:, 0, :])
                link(nc.vector.tensor_tensor(rowt[:, 0, :], cb[:, :], rowb[:, 0, :], ALU.subtract))
                link(nc.vector.tensor_copy(rowb[:, 1, :], rowt[:, 0, :]))
                nc.vector.tensor_copy(bias3[32:33, :], rowb[:, 1, :])
                link(nc.vector.tensor_tensor(rowt[:, 1, :], rowt[:, 0, :], rowb[:, 1, :], ALU.subtract))
                nc.vector.tensor_copy(bias3[64:65, :], rowt[:, 1, :])
                dve.wait_ge(summed, 1)
                link(nc.vector.tensor_scalar(small[:, 0:2], ps[3][:, 0:2], 1.0 / (HID * P), 1e-5, ALU.mult, ALU.max))
                link(nc.vector.reciprocal(small[:, 2:4], small[:, 0:2]))
                for i, wx in enumerate((w1T, w2T)):
                    link(nc.vector.tensor_scalar(wr[:, :, :], wx[:, :, :], small[:, 2 + i:3 + i], 1.0, ALU.mult, ALU.min))
                    link(nc.vector.tensor_scalar(wr[:, :, :], wr[:, :, :], -1.0, MAGIC, ALU.max, ALU.add))
                    link(nc.vector.tensor_scalar_add(wr[:, :, :], wr[:, :, :], -MAGIC))
                    if i == 0:
                        wrf = wr[:, :, :].rearrange("p a b -> p (a b)")
                        link(nc.vector.tensor_scalar_mul(wrf, wrf, small[:, 0:1]))
                        for j in range(3):
                            ins = nc.vector.tensor_tensor(WJ[:, j, :], wrf, cw[:, j, :], ALU.mult)
                        link(ins)
                    else:
                        link(nc.vector.tensor_copy(tern2[:, :, :], wr[:, :, :]))
                dve.wait_ge(tanhed, 1)
                nc.vector.tensor_scalar_mul(half_gate[:, :], tg[:, :], 0.5)
                link(nc.vector.tensor_tensor(small[:, 4:5], small[:, 1:2], tg[:, 4:5], ALU.mult))
                link(nc.vector.tensor_scalar_mul(coef2[:, :], small[:, 4:5], 0.5))
                for m, wx, a, b in (("l2_mur", "l2_wrT", "wr0", "wr1"), ("l2_muk", "l2_wkfT", "wk0", "wk1")):
                    link(nc.vector.tensor_scalar(small[:, 6:7], keep[m][:, :], -1.0, 1.0, ALU.mult, ALU.add))
                    nc.vector.tensor_scalar_mul(mu[a][:, :], keep[wx][:, :], keep[m][:, :])
                    link(nc.vector.tensor_scalar_mul(mu[b][:, :], keep[wx][:, :], small[:, 6:7]))
                link(nc.vector.tensor_scalar_mul(keep["l2_bq"][:, :], keep["l2_bq"][:, :], 8.0 ** -0.5))
                link(nc.vector.tensor_scalar_mul(keep["mask_up"][:, :], keep["mask_up"][:, :], keep["l3_scale"][0:32, :]))
                link(nc.vector.tensor_scalar_mul(keep["mask_down"][:, :], keep["mask_down"][:, :], keep["l3_scale"][:, :]))
    return keep


def load_gate(k, i):
    return k["tg"][:, i:i + 1]


def layer0_attention(nc, k, src, dst, ctx):
    LAG = 6
    with ExitStack() as c:
        S = Stream(nc, c, "a0", src, dst, ctx)
        qT, V, E, PT = (S.two(n, [P, P]) for n in ("qT", "V", "E", "PT"))
        nmax, ssum, rinv, coef = (S.two(n, [P, 1]) for n in ("nmax", "ssum", "rinv", "coef"))
        psX, psQ, psV, psS, psPT, psO = (S.bank(n) for n in ("psX", "psQ", "psV", "psS", "psPT", "psO"))
        q_done, q_copied, v_done, v_copied, s_done, masked, max_done, exp_done, rinv_done, coef_done, \
            ptr_done, pt_copied = (S.sem(n) for n in (
                "q_done", "q_copied", "v_done", "v_copied", "s_done", "masked", "max_done", "exp_done",
                "rinv_done", "coef_done", "ptr_done", "pt_copied"))
        S.ctx_used = s_done, 1
        block = c.enter_context(nc.Block())

        @block.sync
        def _(sp):
            S.sp_program(sp, LAG, ctx_lag=2)

        @block.gpsimd
        def _(pool):
            def step(s, q):
                if live(s, 1):
                    S.ln_pow(pool, s - 1, 1 - q, k["minus_half"])

            run_steps(pool, step, LAG)

        @block.tensor
        def _(pe):
            def project_q(t, p):
                pe.wait_ge(S.xT_done, t + 1)
                if exists(t - 1):
                    pe.wait_ge(q_copied, t)
                nc.tensor.matmul(psQ[:, 0:P], k["A0"][:, :], S.xT[p][:, :], start=True, stop=True).then_inc(q_done, 1)

            def project_v(t, p):
                pe.wait_ge(S.ctx_loaded[p], moved(t, p))
                if exists(t - 1):
                    pe.wait_ge(v_copied, t)
                nc.tensor.matmul(psV[:, 0:P], S.ctxT[p][:, :], k["l0_wv"][:, :], start=True, stop=True)\
                    .then_inc(v_done, 1)

            def scores(t, p):
                pe.wait_ge(q_copied, t + 1)
                if exists(t - 1):
                    pe.wait_ge(masked, t)
                nc.tensor.matmul(psS[:, 0:P], qT[p][:, :], S.ctxT[p][:, :], start=True, stop=True).then_inc(s_done, 1)

            def transpose_p(t, p):
                pe.wait_ge(exp_done, t + 1)
                if exists(t - 1):
                    pe.wait_ge(pt_copied, t)
                nc.tensor.transpose(psPT[:, 0:P], E[p][:, :], k["ident"][:, :]).then_inc(ptr_done, 1)

            def values(t, p):
                pe.wait_ge(pt_copied, t + 1)
                pe.wait_ge(v_copied, t + 1)
                if exists(t - 1):
                    pe.wait_ge(S.res_done, t)
                nc.tensor.matmul(psO[:, 0:P], PT[p][:, :], V[p][:, :], start=True, stop=True).then_inc(S.o_done, 1)

            def step(s, q):
                if live(s, 4):
                    scores(s - 4, q)
                if live(s, 5):
                    transpose_p(s - 5, 1 - q)
                if live(s, 3):
                    project_q(s - 3, 1 - q)
                if live(s, 2):
                    S.x_transpose(pe, s - 2, q, psX, k["ident"])
                if live(s, 5):
                    values(s - 5, 1 - q)
                if live(s, 3):
                    project_v(s - 3, 1 - q)

            run_steps(pe, step, LAG)

        @block.scalar
        def _(act):
            def step(s, q):
                if live(s, 5):
                    t, p = s - 5, 1 - q
                    act.wait_ge(ptr_done, t + 1)
                    if exists(t - 2):
                        act.wait_ge(S.o_done, t - 1)
                    nc.scalar.copy(PT[p][:, :], psPT[:, 0:P]).then_inc(pt_copied, 1)
                if live(s, 3):
                    t, p = s - 3, 1 - q
                    act.wait_ge(q_done, t + 1)
                    if exists(t - 2):
                        act.wait_ge(s_done, t - 1)
                    nc.scalar.copy(qT[p][:, :], psQ[:, 0:P]).then_inc(q_copied, 1)
                if live(s, 2):
                    S.x_copy(act, s - 2, q, psX, q_done, 1)
                if live(s, 4):
                    t, p = s - 4, q
                    act.wait_ge(max_done, t + 1)
                    if exists(t - 2):
                        act.wait_ge(rinv_done, t - 1)
                    nc.scalar.activation(E[p][:, :], E[p][:, :], ACT.Exp, bias=nmax[p][:, :],
                                         accum_out=ssum[p][:, :]).then_inc(exp_done, 1)
                if live(s, 3):
                    t, p = s - 3, 1 - q
                    act.wait_ge(v_done, t + 1)
                    if exists(t - 2):
                        act.wait_ge(S.o_done, t - 1)
                    nc.scalar.copy(V[p][:, :], psV[:, 0:P]).then_inc(v_copied, 1)

            run_steps(act, step, LAG)

        @block.vector
        def _(dve):
            def step(s, q):
                if live(s, 5):
                    t, p = s - 5, 1 - q
                    dve.wait_ge(exp_done, t + 1)
                    if exists(t - 2):
                        dve.wait_ge(coef_done, t - 1)
                    nc.vector.reciprocal(rinv[p][:, :], ssum[p][:, :]).then_inc(rinv_done, 1)
                if live(s, 2):
                    S.ln_norm(dve, s - 2, q)
                if live(s, 5):
                    t, p = s - 5, 1 - q
                    dve.wait_ge(rinv_done, t + 1)
                    if exists(t - 2):
                        dve.wait_ge(S.res_done, t - 1)
                    nc.vector.tensor_scalar_mul(coef[p][:, :], rinv[p][:, :], load_gate(k, 0)).then_inc(coef_done, 1)
                if live(s, 4):
                    t, p = s - 4, q
                    dve.wait_ge(s_done, t + 1)
                    if exists(t - 2):
                        dve.wait_ge(ptr_done, t - 1)
                    nc.vector.tensor_tensor(E[p][:, :], psS[:, 0:P], k["causal"][:, :], ALU.add).then_inc(masked, 1)
                if live(s, 1):
                    S.bn_first(dve, s - 1, 1 - q)
                if live(s, 4):
                    t, p = s - 4, q
                    dve.wait_ge(masked, t + 1)
                    if exists(t - 2):
                        dve.wait_ge(exp_done, t - 1)
                    nc.vector.tensor_reduce(nmax[p][:, :], E[p][:, :], AX.X, ALU.max, negate=True)\
                        .then_inc(max_done, 1)
                if live(s, 1):
                    S.bn_second(dve, s - 1, 1 - q)
                if live(s, 5):
                    dve.wait_ge(coef_done, s - 4)
                    S.add_residual(dve, s - 5, 1 - q, psO, coef[1 - q][:, :])
                if live(s, 1):
                    S.bn_third(dve, s - 1, 1 - q)

            run_steps(dve, step, LAG)


def layer0_ffn(nc, k, src, dst):
    PADDED = SEQ + 2
    LAG = 7
    with ExitStack() as c:
        S = Stream(nc, c, "f0", src, dst)
        xpad = S.two("xpad", [P, NB, PADDED])
        xq, xd = S.two("xq", [P, P]), S.two("xd", [P, P])
        amax, step1, inv1, amax2, step2, inv2, coef = (
            S.two(n, [P, 1]) for n in ("amax", "step1", "inv1", "amax2", "step2", "inv2", "coef"))
        th, g, gm = (S.two(n, [P, HID]) for n in ("th", "g", "gm"))
        q2 = S.two("q2", [P, HID], BF16)
        q2T = S.two("q2T", [P, HID], BF16)
        magic = S.sb("magic", [P, 1])
        identb = S.sb("identb", [P, P], BF16)
        psX, psO = S.bank("psX"), S.bank("psO")
        psH = [S.bank(f"psH{i}") for i in range(2)]
        psT = S.bank("psT", BF16)
        xT_used = S.sem("xT_used")
        ready, amax_done, step_done, inv_done, round_done, xd_done, h_done, th_done, g_done, amax2_done, \
            step2_done, inv2_done, gm_done, q2_done, coef_done, qtr_done, qT_done = (S.sem(n) for n in (
                "ready", "amax_done", "step_done", "inv_done", "round_done", "xd_done", "h_done", "th_done",
                "g_done", "amax2_done", "step2_done", "inv2_done", "gm_done", "q2_done", "coef_done",
                "qtr_done", "qT_done"))
        block = c.enter_context(nc.Block())

        @block.sync
        def _(sp):
            S.sp_program(sp, LAG)

        @block.gpsimd
        def _(pool):
            nc.gpsimd.tensor_copy(identb[:, :], k["ident"][:, :]).then_inc(ready, 1)
            nc.gpsimd.memset(magic[:, :], MAGIC).then_inc(ready, 1)
            for p in range(2):
                nc.gpsimd.memset(xpad[p][:, :, :], 0.0).then_inc(ready, 1)

            def step(s, q):
                if live(s, 1):
                    S.ln_pow(pool, s - 1, 1 - q, k["minus_half"])

            run_steps(pool, step, LAG)

        @block.tensor
        def _(pe):
            def hidden(t, p):
                pe.wait_ge(S.xT_done, t + 1)
                if exists(t - 2):
                    pe.wait_ge(g_done, t - 1)
                for j in range(3):
                    for b in range(NB):
                        last = nc.tensor.matmul(psH[p][64 * b:64 * b + 64, :], xpad[p][:, b, j:j + SEQ],
                                                k["WJ"][:, j, :], start=(j == 0), stop=False)
                last.then_inc(xT_used, 1)
                for b in range(NB):
                    last = nc.tensor.matmul(psH[p][64 * b:64 * b + 64, :], k["ones_bf"][:, 0:64], k["bias3"][:, 0:HID],
                                            start=False, stop=True)
                last.then_inc(h_done, 1)

            def transpose_q(t, p):
                pe.wait_ge(q2_done, t + 1)
                if exists(t - 1):
                    pe.wait_ge(qT_done, t)
                for i in range(CH):
                    last = nc.tensor.transpose(psT[:, i * P:(i + 1) * P], q2[p][:, i * P:(i + 1) * P], identb[:, :])
                last.then_inc(qtr_done, 1)

            def down(t, p):
                pe.wait_ge(qT_done, t + 1)
                if exists(t - 1):
                    pe.wait_ge(S.res_done, t)
                for i in range(CH):
                    last = nc.tensor.matmul(psO[:, 0:P], q2T[p][:, i * P:(i + 1) * P], k["tern2"][:, i, :],
                                            start=(i == 0), stop=(i == CH - 1))
                last.then_inc(S.o_done, 1)

            pe.wait_ge(ready, 4)

            def step(s, q):
                if live(s, 6):
                    down(s - 6, q)
                if live(s, 3):
                    hidden(s - 3, 1 - q)
                if live(s, 2):
                    S.x_transpose(pe, s - 2, q, psX, k["ident"], ready=xd_done, src=xd)
                if live(s, 5):
                    transpose_q(s - 5, 1 - q)

            run_steps(pe, step, LAG)

        @block.scalar
        def _(act):
            act.wait_ge(ready, 4)

            def step(s, q):
                if live(s, 4):
                    t, p = s - 4, q
                    act.wait_ge(inv2_done, t + 1)
                    if exists(t - 2):
                        act.wait_ge(q2_done, t - 1)
                    nc.scalar.activation(gm[p][:, :], g[p][:, :], ACT.Identity, bias=magic[:, :],
                                         scale=inv2[p][:, :]).then_inc(gm_done, 1)
                if live(s, 3):
                    t, p = s - 3, 1 - q
                    act.wait_ge(h_done, t + 1)
                    if exists(t - 2):
                        act.wait_ge(g_done, t - 1)
                    nc.scalar.activation(th[p][:, :], psH[p][:, :], ACT.Tanh, scale=0.5).then_inc(th_done, 1)
                if live(s, 2):
                    t, p = s - 2, q
                    act.wait_ge(S.xtr_done, t + 1)
                    if exists(t - 2):
                        act.wait_ge(xT_used, t - 1)
                    nc.scalar.copy(xpad[p][:, :, 1:1 + SEQ], psX[:, 0:P].rearrange("p (b s) -> p b s", b=NB))\
                        .then_inc(S.xT_done, 1)
                if live(s, 5):
                    t, p = s - 5, 1 - q
                    act.wait_ge(qtr_done, t + 1)
                    if exists(t - 2):
                        act.wait_ge(S.o_done, t - 1)
                    nc.scalar.copy(q2T[p][:, :], psT[:, 0:HID]).then_inc(qT_done, 1)

            run_steps(act, step, LAG)

        @block.vector
        def _(dve):
            def step(s, q):
                ti, pi = s - 2, q
                tt, ph = s - 4, q
                if live(s, 5):
                    t, p = s - 5, 1 - q
                    dve.wait_ge(gm_done, t + 1)
                    if exists(t - 2):
                        dve.wait_ge(qtr_done, t - 1)
                    nc.vector.tensor_scalar_add(q2[p][:, :], gm[p][:, :], -MAGIC).then_inc(q2_done, 1)
                if live(s, 2):
                    S.ln_norm(dve, ti, pi)
                if live(s, 4):
                    dve.wait_ge(th_done, tt + 1)
                    if exists(tt - 2):
                        dve.wait_ge(gm_done, tt - 1)
                    nc.vector.scalar_tensor_tensor(g[ph][:, :], th[ph][:, :], 1.0, psH[ph][:, :], ALU.add, ALU.mult)\
                        .then_inc(g_done, 1)
                if live(s, 2):
                    dve.wait_ge(S.xh_done, ti + 1)
                    nc.vector.tensor_reduce(amax[pi][:, :], S.xh[pi][:, :], AX.X, ALU.max,
                                            apply_absolute_value=True).then_inc(amax_done, 1)
                if live(s, 4):
                    dve.wait_ge(g_done, tt + 1)
                    nc.vector.tensor_reduce(amax2[ph][:, :], g[ph][:, :], AX.X, ALU.max,
                                            apply_absolute_value=True).then_inc(amax2_done, 1)
                if live(s, 2):
                    dve.wait_ge(amax_done, ti + 1)
                    nc.vector.tensor_scalar(step1[pi][:, :], amax[pi][:, :], 1e-5, 1.0 / 127.0, ALU.max, ALU.mult)\
                        .then_inc(step_done, 1)
                if live(s, 4):
                    dve.wait_ge(amax2_done, tt + 1)
                    nc.vector.tensor_scalar(step2[ph][:, :], amax2[ph][:, :], 2e-5, 1.0 / 127.0, ALU.max, ALU.mult)\
                        .then_inc(step2_done, 1)
                if live(s, 2):
                    dve.wait_ge(step_done, ti + 1)
                    nc.vector.reciprocal(inv1[pi][:, :], step1[pi][:, :]).then_inc(inv_done, 1)
                if live(s, 4):
                    dve.wait_ge(step2_done, tt + 1)
                    nc.vector.reciprocal(inv2[ph][:, :], step2[ph][:, :]).then_inc(inv2_done, 1)
                if live(s, 2):
                    dve.wait_ge(inv_done, ti + 1)
                    nc.vector.tensor_scalar(xq[pi][:, :], S.xh[pi][:, :], inv1[pi][:, :], MAGIC, ALU.mult, ALU.add)\
                        .then_inc(round_done, 1)
                if live(s, 1):
                    S.bn_first(dve, s - 1, 1 - q)
                if live(s, 2):
                    dve.wait_ge(round_done, ti + 1)
                    if exists(ti - 2):
                        dve.wait_ge(S.xtr_done, ti - 1)
                    nc.vector.tensor_scalar(xd[pi][:, :], xq[pi][:, :], MAGIC, step1[pi][:, :],
                                            ALU.subtract, ALU.mult).then_inc(xd_done, 1)
                if live(s, 1):
                    S.bn_second(dve, s - 1, 1 - q)
                if live(s, 6):
                    dve.wait_ge(coef_done, s - 5)
                    S.add_residual(dve, s - 6, q, psO, coef[q][:, :])
                if live(s, 1):
                    S.bn_third(dve, s - 1, 1 - q)
                if live(s, 4):
                    if exists(tt - 2):
                        dve.wait_ge(S.res_done, tt - 1)
                    nc.vector.tensor_scalar_mul(coef[ph][:, :], step2[ph][:, :], k["coef2"][:, :])\
                        .then_inc(coef_done, 1)

            run_steps(dve, step, LAG)


def softmax_max_sub(dve, nc, nmax, E, psS, t, p, s_done, max_done, sub_done, e_used):
    for hf in range(2):
        sv = psS[hf][:, :].rearrange("p (h k) -> p h k", k=SEQ)
        dve.wait_ge(s_done, 2 * t + hf + 1)
        if hf == 0:
            if exists(t - 2):
                dve.wait_ge(sub_done, 2 * t - 2)
        nc.vector.tensor_reduce(nmax[p][:, 8 * hf:8 * hf + 8], sv, AX.X, ALU.max).then_inc(max_done, 1)
        dve.wait_ge(max_done, 2 * t + hf + 1)
        if hf == 0:
            if exists(t - 2):
                dve.wait_ge(e_used, 2 * t - 2)
        nc.vector.tensor_tensor(E[p][:, hf, :].rearrange("p (h k) -> p h k", k=SEQ), sv,
                                nmax[p][:, 8 * hf:8 * hf + 8].unsqueeze(2).broadcast_to([P, 8, SEQ]),
                                ALU.subtract).then_inc(sub_done, 1)


def layer1_attention(nc, k, src, dst, ctx):
    with ExitStack() as c:
        S = Stream(nc, c, "a1", src, dst, ctx)
        T = S.two("T", [P, NB, NH, SEQ])
        U = S.two("U", [P, NB, PAIRS, P])
        E = S.two("E", [P, 2, 512])
        PT = S.two("PT", [P, PAIRS, P])
        rmax, ssum, rinv = (S.two(n, [P, NH]) for n in ("rmax", "ssum", "rinv"))
        psM = [S.bank(f"psM{i}") for i in range(2)]
        psS = [S.bank(f"psS{i}") for i in range(2)]
        psT = [S.bank(f"psT{i}") for i in range(2)]
        psX, psO = S.bank("psX"), S.bank("psO")
        proj_done, proj_copied, s_done, max_done, sub_done, exp_done, sum_done, rinv_done, p_done, \
            ptr_done, pt_copied = (S.sem(n) for n in (
                "proj_done", "proj_copied", "s_done", "max_done", "sub_done", "exp_done", "sum_done",
                "rinv_done", "p_done", "ptr_done", "pt_copied"))
        S.ctx_used = proj_done, 8
        block = c.enter_context(nc.Block())

        @block.sync
        def _(sp):
            S.sp_program(sp)

        @block.gpsimd
        def _(pool):
            def step(s, q):
                if live(s, 1):
                    S.ln_pow(pool, s - 1, 1 - q, k["minus_half"])
                if live(s, 3):
                    t, p = s - 3, 1 - q
                    for hf in range(2):
                        pool.wait_ge(rinv_done, 2 * t + hf + 1)
                        ev = E[p][:, hf, :].rearrange("p (h k) -> p h k", k=SEQ)
                        nc.gpsimd.tensor_tensor(
                            ev, ev, rinv[p][:, 8 * hf:8 * hf + 8].unsqueeze(2).broadcast_to([P, 8, SEQ]),
                            ALU.mult).then_inc(p_done, 1)

            run_steps(pool, step)

        @block.tensor
        def _(pe):
            def project(t, p):
                pe.wait_ge(S.xT_done, t + 1)
                pe.wait_ge(S.ctx_loaded[p], moved(t, p))
                for i in range(4):
                    if i < 2:
                        if exists(t - 1):
                            pe.wait_ge(proj_copied, 8 * t + i - 1)
                    else:
                        pe.wait_ge(proj_copied, 8 * t + i - 1)
                    for h in range(4):
                        last = nc.tensor.matmul(psM[i % 2][:, h * P:(h + 1) * P], k["AT"][:, 4 * i + h, :],
                                                S.ctxT[p][:, :], start=True, stop=True)
                    last.then_inc(proj_done, 1)
                for i in range(4):
                    pe.wait_ge(proj_copied, 8 * t + i + 3)
                    b, q4 = i // 2, 4 * (i % 2)
                    for j in range(2):
                        last = nc.tensor.matmul(psM[i % 2][64 * j:64 * j + 64, :], S.ctxT[p][:, 64 * b:64 * b + 64],
                                                k["B"][:, j, q4:q4 + 4, :], start=True, stop=True)
                    last.then_inc(proj_done, 1)
                last_use = last
                return last_use

            def scores(t, p):
                for hf in range(2):
                    pe.wait_ge(proj_copied, 8 * t + 4)
                    if exists(t - 1):
                        pe.wait_ge(sub_done, 2 * t + hf - 1)
                    for b in range(NB):
                        last = nc.tensor.matmul(psS[hf][64 * b:64 * b + 64, :], S.xT[p][:, 64 * b:64 * b + 64],
                                                T[p][:, b, 8 * hf:8 * hf + 8, :], start=True, stop=True)
                    last.then_inc(s_done, 1)

            def values(t, p):
                for hf in range(2):
                    pe.wait_ge(p_done, 2 * t + hf + 1)
                    if exists(t - 1):
                        pe.wait_ge(pt_copied, 2 * t + hf - 1)
                    for i in range(4):
                        last = nc.tensor.transpose(psT[hf][:, i * P:(i + 1) * P], E[p][:, hf, i * P:(i + 1) * P],
                                                   k["ident"][:, :])
                    last.then_inc(ptr_done, 1)
                if exists(t - 1):
                    pe.wait_ge(S.res_done, t)
                for i in range(PAIRS):
                    if i % 4 == 0:
                        pe.wait_ge(pt_copied, 2 * t + i // 4 + 1)
                    for b in range(NB):
                        last = nc.tensor.matmul(psO[64 * b:64 * b + 64, 0:P], PT[p][:, i, 64 * b:64 * b + 64],
                                                U[p][:, b, i, :], start=(i == 0), stop=(i == PAIRS - 1))
                last.then_inc(S.o_done, 1)

            def step(s, q):
                if live(s, 3):
                    project(s - 3, 1 - q)
                    scores(s - 3, 1 - q)
                if live(s, 2):
                    S.x_transpose(pe, s - 2, q, psX, k["ident"])
                if live(s, 4):
                    values(s - 4, q)

            run_steps(pe, step)

        @block.scalar
        def _(act):
            def step(s, q):
                if live(s, 3):
                    t, p = s - 3, 1 - q
                    if exists(t - 2):
                        act.wait_ge(s_done, 2 * t - 2)
                    for i in range(4):
                        act.wait_ge(proj_done, 8 * t + i + 1)
                        nc.scalar.copy(T[p][:, :, 4 * i:4 * i + 4, :].rearrange("p b h k -> p h b k"),
                                       psM[i % 2][:, :].rearrange("p (h b k) -> p h b k", h=4, b=NB))\
                            .then_inc(proj_copied, 1)
                    if exists(t - 2):
                        act.wait_ge(S.o_done, t - 1)
                    for i in range(4):
                        act.wait_ge(proj_done, 8 * t + i + 5)
                        b, q4 = i // 2, 4 * (i % 2)
                        nc.scalar.copy(U[p][:, b, q4:q4 + 4, :].rearrange("p a b -> p (a b)"), psM[i % 2][:, :])\
                            .then_inc(proj_copied, 1)
                if live(s, 2):
                    S.x_copy(act, s - 2, q, psX, s_done, 2)
                if live(s, 4):
                    t, p = s - 4, q
                    if exists(t - 2):
                        act.wait_ge(S.o_done, t - 1)
                    for hf in range(2):
                        act.wait_ge(ptr_done, 2 * t + hf + 1)
                        nc.scalar.copy(PT[p][:, 4 * hf:4 * hf + 4, :].rearrange("p a b -> p (a b)"), psT[hf][:, :])\
                            .then_inc(pt_copied, 1)
                if live(s, 3):
                    t, p = s - 3, 1 - q
                    for hf in range(2):
                        act.wait_ge(sub_done, 2 * t + hf + 1)
                        nc.scalar.activation(E[p][:, hf, :], E[p][:, hf, :], ACT.Exp).then_inc(exp_done, 1)

            run_steps(act, step)

        @block.vector
        def _(dve):
            def step(s, q):
                if live(s, 2):
                    S.ln_norm(dve, s - 2, q)
                if live(s, 1):
                    S.ln_stats(dve, s - 1, 1 - q)
                if live(s, 3):
                    softmax_max_sub(dve, nc, rmax, E, psS, s - 3, 1 - q, s_done, max_done, sub_done, ptr_done)
                    t, p = s - 3, 1 - q
                    for hf in range(2):
                        h8 = slice(8 * hf, 8 * hf + 8)
                        dve.wait_ge(exp_done, 2 * t + hf + 1)
                        if hf == 0:
                            if exists(t - 2):
                                dve.wait_ge(rinv_done, 2 * t - 2)
                        nc.vector.tensor_reduce(ssum[p][:, h8], E[p][:, hf, :].rearrange("p (h k) -> p h k", k=SEQ),
                                                AX.X, ALU.add).then_inc(sum_done, 1)
                        dve.wait_ge(sum_done, 2 * t + hf + 1)
                        if hf == 0:
                            if exists(t - 2):
                                dve.wait_ge(p_done, 2 * t - 2)
                        nc.vector.reciprocal(rinv[p][:, h8], ssum[p][:, h8]).then_inc(rinv_done, 1)
                if live(s, 4):
                    S.add_residual(dve, s - 4, q, psO, load_gate(k, 1))

            run_steps(dve, step)


def layer1_ffn(nc, k, src, dst):
    LAG = 8
    with ExitStack() as c:
        S = Stream(nc, c, "f1", src, dst)
        top, topw, th_top, rwh, coef = (S.two(n, [P, 1]) for n in ("top", "topw", "th_top", "rwh", "coef"))
        ranks, pick = (S.two(n, [P, NE]) for n in ("ranks", "pick"))
        TH, A, Hd = (S.two(n, [P, HID]) for n in ("TH", "A", "Hd"))
        HT = S.two("HT", [P, HID])
        gate2 = S.sb("gate2", [P, 1])
        psX, psL, psT, psO = (S.bank(n) for n in ("psX", "psL", "psT", "psO"))
        psG = [S.bank(f"psG{i}") for i in range(2)]
        psU = [S.bank(f"psU{i}") for i in range(2)]
        ready, l_done, g_done, u_done, top_done, ranks_done, topw_done, pick_done, thtop_done, rwh_done, \
            TH_done, A_done, H_done, picked, coef_done, htr_done, hT_done = (S.sem(n) for n in (
                "ready", "l_done", "g_done", "u_done", "top_done", "ranks_done", "topw_done", "pick_done",
                "thtop_done", "rwh_done", "TH_done", "A_done", "H_done", "picked", "coef_done", "htr_done",
                "hT_done"))
        block = c.enter_context(nc.Block())

        @block.sync
        def _(sp):
            S.sp_program(sp, LAG)

        @block.gpsimd
        def _(pool):
            def step(s, q):
                if live(s, 1):
                    S.ln_pow(pool, s - 1, 1 - q, k["minus_half"])
                if live(s, 5):
                    t, p = s - 5, 1 - q
                    pool.wait_ge(H_done, t + 1)
                    pool.wait_ge(pick_done, t + 1)
                    hv = Hd[p][:, :].rearrange("p (e i) -> p e i", e=NE)
                    nc.gpsimd.tensor_tensor(hv, hv, pick[p][:, :].unsqueeze(2).broadcast_to([P, NE, HID // NE]),
                                            ALU.mult).then_inc(picked, 1)

            run_steps(pool, step, LAG)

        @block.tensor
        def _(pe):
            def up(t, p):
                pe.wait_ge(S.xT_done, t + 1)
                if exists(t - 2):
                    pe.wait_ge(A_done, t - 1)
                nc.tensor.matmul(psG[p][:, :], S.xT[p][:, :], k["l1_wgT"][:, :], start=True, stop=True)\
                    .then_inc(g_done, 1)
                if exists(t - 2):
                    pe.wait_ge(H_done, t - 1)
                nc.tensor.matmul(psU[p][:, :], S.xT[p][:, :], k["l1_wuT"][:, :], start=True, stop=True)\
                    .then_inc(u_done, 1)
                if exists(t - 1):
                    pe.wait_ge(ranks_done, t)
                nc.tensor.matmul(psL[:, 0:NE], S.xT[p][:, :], k["l1_gateT"][:, :], start=True, stop=True)\
                    .then_inc(l_done, 1)

            def transpose_h(t, p):
                pe.wait_ge(picked, t + 1)
                if exists(t - 1):
                    pe.wait_ge(hT_done, t)
                for i in range(CH):
                    last = nc.tensor.transpose(psT[:, i * P:(i + 1) * P], Hd[p][:, i * P:(i + 1) * P], k["ident"][:, :])
                last.then_inc(htr_done, 1)

            def down(t, p):
                pe.wait_ge(hT_done, t + 1)
                if exists(t - 1):
                    pe.wait_ge(S.res_done, t)
                for i in range(CH):
                    last = nc.tensor.matmul(psO[:, 0:P], HT[p][:, i * P:(i + 1) * P], k["l1_wdT"][:, i, :],
                                            start=(i == 0), stop=(i == CH - 1))
                last.then_inc(S.o_done, 1)

            def step(s, q):
                if live(s, 7):
                    down(s - 7, 1 - q)
                if live(s, 6):
                    transpose_h(s - 6, q)
                if live(s, 2):
                    S.x_transpose(pe, s - 2, q, psX, k["ident"])
                if live(s, 3):
                    up(s - 3, 1 - q)

            run_steps(pe, step, LAG)

        @block.scalar
        def _(act):
            def step(s, q):
                if live(s, 6):
                    t, p = s - 6, q
                    act.wait_ge(htr_done, t + 1)
                    if exists(t - 2):
                        act.wait_ge(S.o_done, t - 1)
                    nc.scalar.copy(HT[p][:, :], psT[:, :]).then_inc(hT_done, 1)
                if live(s, 2):
                    S.x_copy(act, s - 2, q, psX, l_done, 1)
                if live(s, 4):
                    t, p = s - 4, q
                    act.wait_ge(top_done, t + 1)
                    if exists(t - 2):
                        act.wait_ge(rwh_done, t - 1)
                    nc.scalar.activation(th_top[p][:, :], top[p][:, :], ACT.Tanh, scale=0.5).then_inc(thtop_done, 1)
                    act.wait_ge(rwh_done, t + 1)
                    act.wait_ge(g_done, t + 1)
                    if exists(t - 2):
                        act.wait_ge(A_done, t - 1)
                    nc.scalar.activation(TH[p][:, :], psG[p][:, :], ACT.Tanh, scale=rwh[p][:, :]).then_inc(TH_done, 1)

            run_steps(act, step, LAG)

        @block.vector
        def _(dve):
            nc.vector.tensor_scalar_mul(gate2[:, :], load_gate(k, 5), 2.0).then_inc(ready, 1)
            dve.wait_ge(ready, 1)

            def step(s, q):
                t4, p4 = s - 4, q
                t5, p5 = s - 5, 1 - q
                if live(s, 5):
                    dve.wait_ge(TH_done, t5 + 1)
                    if exists(t5 - 2):
                        dve.wait_ge(H_done, t5 - 1)
                    nc.vector.scalar_tensor_tensor(A[p5][:, :], TH[p5][:, :], 1.0, psG[p5][:, :], ALU.add, ALU.mult)\
                        .then_inc(A_done, 1)
                if live(s, 4):
                    dve.wait_ge(l_done, t4 + 1)
                    if exists(t4 - 2):
                        dve.wait_ge(thtop_done, t4 - 1)
                    if exists(t4 - 2):
                        dve.wait_ge(ranks_done, t4 - 1)
                    nc.vector.tensor_reduce(top[p4][:, :], psL[:, 0:NE], AX.X, ALU.max).then_inc(top_done, 1)
                if live(s, 5):
                    dve.wait_ge(A_done, t5 + 1)
                    dve.wait_ge(u_done, t5 + 1)
                    if exists(t5 - 2):
                        dve.wait_ge(htr_done, t5 - 1)
                    nc.vector.tensor_tensor(Hd[p5][:, :], psU[p5][:, :], A[p5][:, :], ALU.mult).then_inc(H_done, 1)
                if live(s, 4):
                    dve.wait_ge(top_done, t4 + 1)
                    nc.vector.scalar_tensor_tensor(ranks[p4][:, :], psL[:, 0:NE], top[p4][:, :], k["desc"][:, :],
                                                   ALU.is_equal, ALU.mult).then_inc(ranks_done, 1)
                if live(s, 2):
                    S.ln_norm(dve, s - 2, q)
                if live(s, 4):
                    dve.wait_ge(thtop_done, t4 + 1)
                    if exists(t4 - 2):
                        dve.wait_ge(TH_done, t4 - 1)
                    if exists(t4 - 2):
                        dve.wait_ge(coef_done, t4 - 1)
                    nc.vector.tensor_scalar(rwh[p4][:, :], th_top[p4][:, :], 1.0, 0.25, ALU.add, ALU.mult)\
                        .then_inc(rwh_done, 1)
                    dve.wait_ge(ranks_done, t4 + 1)
                    nc.vector.tensor_reduce(topw[p4][:, :], ranks[p4][:, :], AX.X, ALU.max).then_inc(topw_done, 1)
                if live(s, 1):
                    S.bn_first(dve, s - 1, 1 - q)
                if live(s, 4):
                    dve.wait_ge(topw_done, t4 + 1)
                    if exists(t4 - 2):
                        dve.wait_ge(picked, t4 - 1)
                    nc.vector.tensor_scalar(pick[p4][:, :], ranks[p4][:, :], topw[p4][:, :], None, ALU.is_equal)\
                        .then_inc(pick_done, 1)
                if live(s, 1):
                    S.bn_second(dve, s - 1, 1 - q)
                if live(s, 7):
                    dve.wait_ge(coef_done, s - 6)
                    S.add_residual(dve, s - 7, 1 - q, psO, coef[1 - q][:, :])
                if live(s, 1):
                    S.bn_third(dve, s - 1, 1 - q)
                if live(s, 5):
                    dve.wait_ge(rwh_done, t5 + 1)
                    if exists(t5 - 2):
                        dve.wait_ge(S.res_done, t5 - 1)
                    nc.vector.tensor_scalar(coef[p5][:, :], rwh[p5][:, :], rwh[p5][:, :], gate2[:, :],
                                            ALU.mult, ALU.mult).then_inc(coef_done, 1)

            run_steps(dve, step, LAG)


def small_head_attention(nc, k, name, src, dst, ctx, w, rotary, gate):
    LAG = 8
    G = NH // 4
    with ExitStack() as c:
        S = Stream(nc, c, name, src, dst, ctx)
        QK = S.two("QK", [P, 2, P] if rotary else [P, 1, P])
        Qj = S.two("Qj", [P, 4, P])
        Kg = S.two("Kg", [P, NB, G, SEQ])
        V = S.two("V", [P, NB, NH, 9])
        E = S.two("E", [P, 2, 512])
        PT = S.two("PT", [P, PAIRS, P])
        on, oT = S.two("on", [P, P]), S.two("oT", [P, P])
        rmax, rinv = S.two("rmax", [P, NH]), S.two("rinv", [P, NH])
        if rotary:
            rc, rs = S.two("rc", [P, 2, P]), S.two("rs", [P, 2, P])
        psX, psQK, psV, psO = S.bank("psX"), S.bank("psQK"), S.bank("psV"), S.bank("psO")
        psS = [S.bank(f"psS{i}") for i in range(2)]
        psT = [S.bank(f"psT{i}") for i in range(2)]
        o9 = psO[:, P:P + 9 * NH].rearrange("p (h e) -> p h e", e=9)
        ready, qk_done, qk_ready, qj_ready, kg_ready, v_done, v_copied, rc_done, rs_done, s_done, max_done, \
            sub_done, exp_done, ptr_done, pt_copied, pv_done, rinv_done, on_done, otr_done, oT_done = (
                S.sem(n) for n in (
                    "ready", "qk_done", "qk_ready", "qj_ready", "kg_ready", "v_done", "v_copied", "rc_done",
                    "rs_done", "s_done", "max_done", "sub_done", "exp_done", "ptr_done", "pt_copied", "pv_done",
                    "rinv_done", "on_done", "otr_done", "oT_done"))
        S.ctx_used = v_done, 1
        block = c.enter_context(nc.Block())

        @block.sync
        def _(sp):
            S.sp_program(sp, LAG)

        @block.gpsimd
        def _(pool):
            for p in range(2):
                nc.gpsimd.memset(Kg[p][:, :, :, :], 0.0).then_inc(ready, 1)
                for j in range(2):
                    r = slice(64 * j, 64 * j + 64)
                    pool.wait_ge(ready, 5 * p + 2 * j + 1)
                    nc.gpsimd.memset(V[p][r, :, j::2, 8:9], 1.0).then_inc(ready, 1)
                    pool.wait_ge(ready, 5 * p + 2 * j + 2)
                    nc.gpsimd.memset(V[p][r, :, 1 - j::2, 8:9], 0.0).then_inc(ready, 1)
                pool.wait_ge(ready, 5 * p + 5)

            def step(s, q):
                if live(s, 3):
                    t, p = s - 3, 1 - q
                    pool.wait_ge(qk_ready, t + 1)
                    if exists(t - 2):
                        pool.wait_ge(s_done, 2 * t - 2)
                    nc.gpsimd.tensor_tensor(Qj[p][:, :, :], QK[p][:, 0:1, :].broadcast_to([P, 4, P]),
                                            k["jmask"][:, :].unsqueeze(2).broadcast_to([P, 4, P]), ALU.mult)\
                        .then_inc(qj_ready, 1)
                if live(s, 1):
                    S.ln_pow(pool, s - 1, 1 - q, k["minus_half"])

            run_steps(pool, step, LAG)

        @block.tensor
        def _(pe):
            pe.wait_ge(ready, 10)

            def project_qk(t, p):
                pe.wait_ge(S.xT_done, t + 1)
                pe.wait_ge(S.ctx_loaded[p], moved(t, p))
                if exists(t - 1):
                    pe.wait_ge(qk_ready, t)
                if not rotary:
                    if exists(t - 1):
                        pe.wait_ge(kg_ready, G * t)
                nc.tensor.matmul(psQK[:, 0:P], k[w + "wqT"][:, :], S.xT[p][:, :], start=True, stop=True)
                if rotary:
                    nc.tensor.matmul(psQK[:, 2 * P:3 * P], k[w + "wqrT"][:, :], S.xT[p][:, :], start=True, stop=True)
                    nc.tensor.matmul(psQK[:, 3 * P:4 * P], k[w + "wkrT"][:, :], S.ctxT[p][:, :], start=True, stop=True)
                nc.tensor.matmul(psQK[:, P:2 * P], k[w + "wkT"][:, :], S.ctxT[p][:, :], start=True, stop=True)\
                    .then_inc(qk_done, 1)

            def project_v(t, p):
                if exists(t - 1):
                    pe.wait_ge(v_copied, t)
                for b in range(NB):
                    for j in range(2):
                        last = nc.tensor.matmul(psV[64 * j:64 * j + 64, b * P:(b + 1) * P],
                                                S.ctxT[p][:, 64 * b:64 * b + 64], k[w + "wvT2"][:, j, :],
                                                start=True, stop=True)
                last.then_inc(v_done, 1)

            def scores(t, p):
                pe.wait_ge(kg_ready, G * t + G)
                pe.wait_ge(qj_ready, t + 1)
                for hf in range(2):
                    if exists(t - 1):
                        pe.wait_ge(sub_done, 2 * t + hf - 1)
                    sv = psS[hf][:, :].rearrange("p (g j k) -> p g j k", g=G, j=2)
                    for j in range(2):
                        for b in range(NB):
                            last = nc.tensor.matmul(sv[64 * b:64 * b + 64, :, j, :],
                                                    Qj[p][:, 2 * hf + j, 64 * b:64 * b + 64],
                                                    Kg[p][:, b, :, :], start=True, stop=True)
                    last.then_inc(s_done, 1)

            def transpose_p(t, p):
                for hf in range(2):
                    pe.wait_ge(exp_done, 2 * t + hf + 1)
                    if exists(t - 1):
                        pe.wait_ge(pt_copied, 2 * t + hf - 1)
                    for i in range(4):
                        last = nc.tensor.transpose(psT[hf][:, i * P:(i + 1) * P], E[p][:, hf, i * P:(i + 1) * P],
                                                   k["ident"][:, :])
                    last.then_inc(ptr_done, 1)

            def values(t, p):
                pe.wait_ge(v_copied, t + 1)
                if exists(t - 1):
                    pe.wait_ge(on_done, t)
                if exists(t - 2):
                    pe.wait_ge(S.res_done, t - 1)
                for hf in range(2):
                    pe.wait_ge(pt_copied, 2 * t + hf + 1)
                    for g in range(G):
                        h = 4 * g + 2 * hf
                        for b in range(NB):
                            last = nc.tensor.matmul(o9[64 * b:64 * b + 64, h:h + 2, :],
                                                    PT[p][:, G * hf + g, 64 * b:64 * b + 64], V[p][:, b, h:h + 2, :],
                                                    start=True, stop=True)
                last.then_inc(pv_done, 1)

            def out_transpose(t, p):
                pe.wait_ge(on_done, t + 1)
                if exists(t - 1):
                    pe.wait_ge(oT_done, t)
                last_normed = min(t + 3, NT - 1) if isinstance(t, int) else t + 3
                pe.wait_ge(S.xT_done, last_normed + 1)
                nc.tensor.transpose(psX[:, P:2 * P], on[p][:, :], k["ident"][:, :]).then_inc(otr_done, 1)

            def out_project(t, p):
                pe.wait_ge(oT_done, t + 1)
                if exists(t - 1):
                    pe.wait_ge(S.res_done, t)
                last = nc.tensor.matmul(psO[:, 0:P], oT[p][:, :], k[w + "woT"][:, :], start=True, stop=rotary)
                if not rotary:
                    last = nc.tensor.matmul(psO[:, 0:P], k["ones_bf"][:, :], k["bias3"][:, HID:HID + P],
                                            start=False, stop=True)
                last.then_inc(S.o_done, 1)

            def step(s, q):
                if live(s, 3):
                    project_qk(s - 3, 1 - q)
                if live(s, 4):
                    scores(s - 4, q)
                if live(s, 5):
                    transpose_p(s - 5, 1 - q)
                if live(s, 6):
                    out_transpose(s - 6, q)
                if live(s, 2):
                    S.x_transpose(pe, s - 2, q, psX, k["ident"])
                if live(s, 3):
                    project_v(s - 3, 1 - q)
                if live(s, 5):
                    values(s - 5, 1 - q)
                if live(s, 6):
                    out_project(s - 6, q)

            run_steps(pe, step, LAG)

        @block.scalar
        def _(act):
            act.wait_ge(ready, 10)

            def step(s, q):
                if live(s, 3):
                    t, p = s - 3, 1 - q
                    if rotary:
                        act.wait_ge(qk_ready, t + 1)
                    else:
                        act.wait_ge(qk_done, t + 1)
                        if exists(t - 2):
                            act.wait_ge(qj_ready, t - 1)
                        nc.scalar.activation(QK[p][:, 0, :], psQK[:, 0:P], ACT.Identity, bias=k[w + "bq"][:, :],
                                             scale=8.0 ** -0.5).then_inc(qk_ready, 1)
                    if exists(t - 2):
                        act.wait_ge(s_done, 2 * t - 2)
                    for g in range(G):
                        r = slice(32 * g, 32 * g + 32)
                        if rotary:
                            nc.scalar.copy(Kg[p][r, :, g, :], QK[p][r, 1, :].rearrange("p (b k) -> p b k", b=NB))\
                                .then_inc(kg_ready, 1)
                        else:
                            nc.scalar.activation(Kg[p][r, :, g, :],
                                                 psQK[r, P:2 * P].rearrange("p (b k) -> p b k", b=NB),
                                                 ACT.Identity, bias=k[w + "bk"][r, :]).then_inc(kg_ready, 1)
                if live(s, 5):
                    t, p = s - 5, 1 - q
                    if exists(t - 2):
                        act.wait_ge(pv_done, t - 1)
                    for hf in range(2):
                        act.wait_ge(ptr_done, 2 * t + hf + 1)
                        nc.scalar.copy(PT[p][:, 4 * hf:4 * hf + 4, :].rearrange("p a b -> p (a b)"), psT[hf][:, :])\
                            .then_inc(pt_copied, 1)
                if live(s, 6):
                    t, p = s - 6, q
                    act.wait_ge(otr_done, t + 1)
                    if live(s, 2):
                        act.wait_ge(S.xtr_done, s - 1)
                    if exists(t - 2):
                        act.wait_ge(S.o_done, t - 1)
                    if rotary:
                        nc.scalar.copy(oT[p][:, :], psX[:, P:2 * P]).then_inc(oT_done, 1)
                    else:
                        nc.scalar.activation(oT[p][:, :], psX[:, P:2 * P], ACT.Identity, bias=k[w + "bv"][:, :])\
                            .then_inc(oT_done, 1)
                if live(s, 2):
                    t, p = s - 2, q
                    act.wait_ge(S.xtr_done, t + 1)
                    if exists(t - 2):
                        act.wait_ge(qk_done, t - 1)
                    nc.scalar.copy(S.xT[p][:, :], psX[:, 0:P]).then_inc(S.xT_done, 1)
                if live(s, 4):
                    t, p = s - 4, q
                    act.wait_ge(sub_done, 2 * t + 1)
                    nc.scalar.activation(E[p][:, 0, :], E[p][:, 0, :], ACT.Exp).then_inc(exp_done, 1)
                    act.wait_ge(sub_done, 2 * t + 2)
                    nc.scalar.activation(E[p][:, 1, :], E[p][:, 1, :], ACT.Exp).then_inc(exp_done, 1)
                if live(s, 3):
                    t, p = s - 3, 1 - q
                    act.wait_ge(v_done, t + 1)
                    if exists(t - 2):
                        act.wait_ge(pv_done, t - 1)
                    nc.scalar.copy(V[p][:, :, :, 0:8], psV[:, 0:2 * P].rearrange("p (b h e) -> p b h e", b=NB, e=8))\
                        .then_inc(v_copied, 1)

            run_steps(act, step, LAG)

        @block.vector
        def _(dve):
            dve.wait_ge(ready, 10)

            def rotate(t, p):
                qk = psQK[:, 0:2 * P].rearrange("p (a s) -> p a s", a=2)
                qk_swapped = psQK[:, 2 * P:4 * P].rearrange("p (a s) -> p a s", a=2)
                dve.wait_ge(qk_done, t + 1)
                if exists(t - 2):
                    dve.wait_ge(qk_ready, t - 1)
                nc.vector.tensor_tensor(rc[p][:, :, :], qk, k["rope"][:, 0, :, :], ALU.mult).then_inc(rc_done, 1)
                nc.vector.tensor_tensor(rs[p][:, :, :], qk_swapped, k["rope"][:, 1, :, :], ALU.mult).then_inc(rs_done, 1)
                dve.wait_ge(rc_done, t + 1)
                dve.wait_ge(rs_done, t + 1)
                if exists(t - 2):
                    dve.wait_ge(qj_ready, t - 1)
                if exists(t - 2):
                    dve.wait_ge(kg_ready, G * (t - 1))
                nc.vector.tensor_tensor(QK[p][:, :, :], rc[p][:, :, :], rs[p][:, :, :], ALU.add).then_inc(qk_ready, 1)

            def step(s, q):
                if live(s, 7):
                    S.add_residual(dve, s - 7, 1 - q, psO, load_gate(k, gate))
                t, p = s - 6, q
                if live(s, 6):
                    dve.wait_ge(pv_done, t + 1)
                    if exists(t - 2):
                        dve.wait_ge(on_done, t - 1)
                    nc.vector.reciprocal(rinv[p][:, :].unsqueeze(2), o9[:, :, 8:9]).then_inc(rinv_done, 1)
                if live(s, 2):
                    S.ln_norm(dve, s - 2, q)
                if live(s, 6):
                    dve.wait_ge(rinv_done, t + 1)
                    if exists(t - 2):
                        dve.wait_ge(otr_done, t - 1)
                    nc.vector.tensor_tensor(on[p][:, :].rearrange("p (h e) -> p h e", e=8), o9[:, :, 0:8],
                                            rinv[p][:, :].unsqueeze(2).broadcast_to([P, NH, 8]), ALU.mult)\
                        .then_inc(on_done, 1)
                if live(s, 1):
                    S.bn_first(dve, s - 1, 1 - q)
                if live(s, 3) and rotary:
                    rotate(s - 3, 1 - q)
                if live(s, 1):
                    S.bn_second(dve, s - 1, 1 - q)
                if live(s, 4):
                    softmax_max_sub(dve, nc, rmax, E, psS, s - 4, q, s_done, max_done, sub_done, ptr_done)
                if live(s, 1):
                    S.bn_third(dve, s - 1, 1 - q)

            run_steps(dve, step, LAG)


def layer2_ffn(nc, k, src, dst):
    LAG = 6
    with ExitStack() as c:
        S = Stream(nc, c, "f2", src, dst)
        xpad = S.two("xpad", [P, NB, SEQ + 1])
        thr, kr, k2, mixed = (S.two(n, [P, P]) for n in ("thr", "kr", "k2", "mixed"))
        psX, psR, psK, psO = (S.bank(n) for n in ("psX", "psR", "psK", "psO"))
        ready, r_done, k_done, thr_done, kr_done, k2_done, mixed_done = (S.sem(n) for n in (
            "ready", "r_done", "k_done", "thr_done", "kr_done", "k2_done", "mixed_done"))
        block = c.enter_context(nc.Block())

        @block.sync
        def _(sp):
            S.sp_program(sp, LAG)

        @block.gpsimd
        def _(pool):
            for p in range(2):
                nc.gpsimd.memset(xpad[p][:, :, :], 0.0).then_inc(ready, 1)

            def step(s, q):
                if live(s, 1):
                    S.ln_pow(pool, s - 1, 1 - q, k["minus_half"])

            run_steps(pool, step, LAG)

        @block.tensor
        def _(pe):
            pe.wait_ge(ready, 2)

            def hidden(t, p):
                now, before = xpad[p][:, :, 1:1 + SEQ], xpad[p][:, :, 0:SEQ]
                pe.wait_ge(S.xT_done, t + 1)
                if exists(t - 1):
                    pe.wait_ge(thr_done, t)
                for x, wx, first in ((now, "wr0", True), (before, "wr1", False)):
                    for b in range(NB):
                        last = nc.tensor.matmul(psR[64 * b:64 * b + 64, 0:P], x[:, b, :], k[wx][:, :],
                                                start=first, stop=not first)
                last.then_inc(r_done, 1)
                if exists(t - 1):
                    pe.wait_ge(kr_done, t)
                psk = psK[:, 0:P].rearrange("p (b s) -> p b s", b=NB)
                nc.tensor.matmul(psk, k["wk0"][:, :], now, start=True, stop=False)
                nc.tensor.matmul(psk, k["wk1"][:, :], before, start=False, stop=True).then_inc(k_done, 1)

            def step(s, q):
                if live(s, 5):
                    t, p = s - 5, 1 - q
                    pe.wait_ge(k2_done, t + 1)
                    if exists(t - 1):
                        pe.wait_ge(mixed_done, t)
                    nc.tensor.matmul(psO[:, 0:P], k2[p][:, :], k["l2_wvfT"][:, :], start=True, stop=True)\
                        .then_inc(S.o_done, 1)
                if live(s, 3):
                    hidden(s - 3, 1 - q)
                if live(s, 2):
                    S.x_transpose(pe, s - 2, q, psX, k["ident"])

            run_steps(pe, step, LAG)

        @block.scalar
        def _(act):
            act.wait_ge(ready, 2)

            def step(s, q):
                if live(s, 3):
                    t, p = s - 3, 1 - q
                    act.wait_ge(r_done, t + 1)
                    if exists(t - 2):
                        act.wait_ge(mixed_done, t - 1)
                    nc.scalar.activation(thr[p][:, :], psR[:, 0:P], ACT.Tanh, scale=0.5).then_inc(thr_done, 1)
                if live(s, 2):
                    t, p = s - 2, q
                    act.wait_ge(S.xtr_done, t + 1)
                    if exists(t - 2):
                        act.wait_ge(k_done, t - 1)
                    nc.scalar.copy(xpad[p][:, :, 1:1 + SEQ], psX[:, 0:P].rearrange("p (b s) -> p b s", b=NB))\
                        .then_inc(S.xT_done, 1)
                if live(s, 3):
                    t, p = s - 3, 1 - q
                    act.wait_ge(k_done, t + 1)
                    if exists(t - 2):
                        act.wait_ge(k2_done, t - 1)
                    nc.scalar.activation(kr[p][:, :], psK[:, 0:P], ACT.Relu).then_inc(kr_done, 1)

            run_steps(act, step, LAG)

        @block.vector
        def _(dve):
            def step(s, q):
                if live(s, 2):
                    S.ln_norm(dve, s - 2, q)
                if live(s, 5):
                    t, p = s - 5, 1 - q
                    dve.wait_ge(S.o_done, t + 1)
                    dve.wait_ge(thr_done, t + 1)
                    if exists(t - 2):
                        dve.wait_ge(S.res_done, t - 1)
                    nc.vector.scalar_tensor_tensor(mixed[p][:, :], thr[p][:, :], 1.0, psO[:, 0:P], ALU.add, ALU.mult)\
                        .then_inc(mixed_done, 1)
                if live(s, 1):
                    S.bn_first(dve, s - 1, 1 - q)
                if live(s, 4):
                    t, p = s - 4, q
                    dve.wait_ge(kr_done, t + 1)
                    if exists(t - 2):
                        dve.wait_ge(S.o_done, t - 1)
                    nc.vector.tensor_tensor(k2[p][:, :], kr[p][:, :], kr[p][:, :], ALU.mult).then_inc(k2_done, 1)
                if live(s, 1):
                    S.bn_second(dve, s - 1, 1 - q)
                if live(s, 5):
                    dve.wait_ge(mixed_done, s - 4)
                    S.add_residual(dve, s - 5, 1 - q, mixed[1 - q], k["half_gate"][:, 6:7])
                if live(s, 1):
                    S.bn_third(dve, s - 1, 1 - q)

            run_steps(dve, step, LAG)


def layer3_ffn(nc, k, src, dst):
    with ExitStack() as c:
        S = Stream(nc, c, "f3", src, dst)
        lead = S.two("lead", [P, 32])
        t1 = S.two("t1", [P, P])
        t2 = S.two("t2", [P, P])
        down_rows = S.two("down_rows", [P, P])
        Hd = S.two("Hd", [P, HID])
        psX, psA, psB, psH, psD, psO = (S.bank(n) for n in ("psX", "psA", "psB", "psH", "psD", "psO"))
        ready, ab_done, t1_done, up_done, rows_done, h_done, gelu_done, d_done, t2_done, copied = (S.sem(n) for n in (
            "ready", "ab_done", "t1_done", "up_done", "rows_done", "h_done", "gelu_done", "d_done", "t2_done", "copied"))
        block = c.enter_context(nc.Block())

        @block.sync
        def _(sp):
            S.sp_program(sp)

        @block.gpsimd
        def _(pool):
            for p in range(2):
                nc.gpsimd.memset(t1[p][:, :], 0.0).then_inc(ready, 1)
                pool.wait_ge(ready, 2 * p + 1)
                nc.gpsimd.memset(t1[p][32:33, :], 1.0).then_inc(ready, 1)
                pool.wait_ge(ready, 2 * p + 2)

            def step(s, q):
                if live(s, 1):
                    S.ln_pow(pool, s - 1, 1 - q, k["minus_half"])

            run_steps(pool, step)

        @block.tensor
        def _(pe):
            pe.wait_ge(ready, 4)

            def rank(t, p):
                pe.wait_ge(S.xT_done, t + 1)
                pe.wait_ge(copied, t + 1)
                if exists(t - 1):
                    pe.wait_ge(t1_done, t)
                if exists(t - 1):
                    pe.wait_ge(up_done, t)
                if exists(t - 1):
                    pe.wait_ge(rows_done, t)
                nc.tensor.matmul(psA[0:32, 0:P], lead[p][:, :], S.xT[p][:, :], start=True, stop=True)
                nc.tensor.matmul(psA[0:32, P:2 * P], k["sel_token"][:, :], S.xh[p][:, :], start=True, stop=True)
                xs = S.xh[p][:, :].rearrange("p (r j) -> p j r", j=CH)
                for j in range(CH):
                    last = nc.tensor.matmul(psB[32 * j:32 * j + 32, 0:32], k["sel_token"][:, :], xs[:, j, :],
                                            start=True, stop=True)
                last.then_inc(ab_done, 1)

            def hidden(t, p):
                pe.wait_ge(t1_done, t + 1)
                pe.wait_ge(up_done, t + 1)
                if exists(t - 1):
                    pe.wait_ge(gelu_done, t)
                for i in range(CH):
                    nc.tensor.matmul(psH[:, i * P:(i + 1) * P], k["l3_w1T"][:, i * P:(i + 1) * P], S.xT[p][:, :],
                                     start=True, stop=False)
                    last = nc.tensor.matmul(psH[:, i * P:(i + 1) * P], k["lora_up"][p][:, i * P:(i + 1) * P],
                                            t1[p][:, :], start=False, stop=True)
                last.then_inc(h_done, 1)

            def down_rank(t, p):
                pe.wait_ge(gelu_done, t + 1)
                if exists(t - 1):
                    pe.wait_ge(t2_done, t)
                for j in range(CH):
                    last = nc.tensor.matmul(psD[32 * j:32 * j + 32, 0:P], lead[p][:, :], Hd[p][:, j * P:(j + 1) * P],
                                            start=True, stop=True)
                last.then_inc(d_done, 1)

            def down(t, p):
                if exists(t - 1):
                    pe.wait_ge(S.res_done, t)
                for i in range(CH):
                    nc.tensor.matmul(psO[:, 0:P], Hd[p][:, i * P:(i + 1) * P], k["l3_w2T"][:, i, :],
                                     start=(i == 0), stop=False)
                nc.tensor.matmul(psO[:, 0:P], k["ones_bf"][:, :], k["bias3"][:, HID + P:HID + 2 * P],
                                 start=False, stop=False)

            def down_last(t, p):
                pe.wait_ge(t2_done, t + 1)
                pe.wait_ge(rows_done, t + 1)
                nc.tensor.matmul(psO[:, 0:P], t2[p][:, :], down_rows[p][:, :], start=False, stop=True)\
                    .then_inc(S.o_done, 1)

            def step(s, q):
                if live(s, 3):
                    rank(s - 3, 1 - q)
                if live(s, 4):
                    down_rank(s - 4, q)
                    down(s - 4, q)
                if live(s, 2):
                    S.x_transpose(pe, s - 2, q, psX, k["ident"])
                if live(s, 3):
                    hidden(s - 3, 1 - q)
                if live(s, 4):
                    down_last(s - 4, q)

            run_steps(pe, step)

        @block.scalar
        def _(act):
            def step(s, q):
                if live(s, 2):
                    t, p = s - 2, q
                    act.wait_ge(S.xtr_done, t + 1)
                    if exists(t - 2):
                        act.wait_ge(h_done, t - 1)
                    nc.scalar.copy(S.xT[p][:, :], psX[:, 0:P]).then_inc(copied, 1)
                    if exists(t - 2):
                        act.wait_ge(d_done, t - 1)
                    nc.scalar.copy(lead[p][:, :].rearrange("p (b s) -> p b s", b=NB),
                                   psX[:, 0:P].rearrange("p (b s) -> p b s", b=NB)[:, :, 1:17])\
                        .then_inc(S.xT_done, 1)
                if live(s, 3):
                    t, p = s - 3, 1 - q
                    act.wait_ge(h_done, t + 1)
                    if exists(t - 2):
                        act.wait_ge(S.o_done, t - 1)
                    nc.scalar.activation(Hd[p][:, :], psH[:, :], ACT.Gelu).then_inc(gelu_done, 1)

            run_steps(act, step)

        @block.vector
        def _(dve):
            def step(s, q):
                if live(s, 3):
                    t, p = s - 3, 1 - q
                    dve.wait_ge(ab_done, t + 1)
                    if exists(t - 2):
                        dve.wait_ge(h_done, t - 1)
                    nc.vector.tensor_tensor(t1[p][0:32, :], psA[0:32, 0:P], k["mask_up"][:, :], ALU.mult)\
                        .then_inc(t1_done, 1)
                    nc.vector.tensor_tensor(
                        k["lora_up"][p][0:32, :].rearrange("p (i c) -> p i c", i=CH),
                        psA[0:32, P:2 * P].unsqueeze(1).broadcast_to([32, CH, P]), k["sel_up"][:, :, :], ALU.mult)\
                        .then_inc(up_done, 1)
                if live(s, 2):
                    if exists(s - 4):
                        dve.wait_ge(ab_done, s - 3)
                    S.ln_norm(dve, s - 2, q)
                if live(s, 4):
                    t, p = s - 4, q
                    dve.wait_ge(d_done, t + 1)
                    if exists(t - 2):
                        dve.wait_ge(S.o_done, t - 1)
                    nc.vector.tensor_tensor(t2[p][:, :], psD[:, 0:P], k["mask_down"][:, :], ALU.mult)\
                        .then_inc(t2_done, 1)
                if live(s, 1):
                    S.bn_first(dve, s - 1, 1 - q)
                if live(s, 3):
                    t, p = s - 3, 1 - q
                    if exists(t - 2):
                        dve.wait_ge(S.o_done, t - 1)
                    nc.vector.tensor_tensor(
                        down_rows[p][:, :].rearrange("p (i r) -> p i r", i=CH),
                        psB[:, 0:32].unsqueeze(1).broadcast_to([P, CH, 32]), k["sel_down"][:, :, :], ALU.mult)\
                        .then_inc(rows_done, 1)
                if live(s, 1):
                    S.bn_second(dve, s - 1, 1 - q)
                    S.bn_third(dve, s - 1, 1 - q)
                if live(s, 4):
                    S.add_residual(dve, s - 4, q, psO, load_gate(k, 7))

            run_steps(dve, step)


def build(nc, w, out):
    with ExitStack() as c:
        X = c.enter_context(nc.sbuf_tensor("residual", [P, NT * P], F32))
        k = prepare(nc, c, w)

        def x_tile(row):
            return w["x"][bass.ds(row, P), :]

        def resident(row):
            return X[:, bass.ds(row, P)]

        def ctx_tile(row):
            return w["ctxT"][:, bass.ds(row, P)]

        def out_tile(row):
            return out[bass.ds(row, P), :]

        layer0_attention(nc, k, x_tile, resident, ctx_tile)
        layer0_ffn(nc, k, resident, resident)
        layer1_attention(nc, k, resident, resident, ctx_tile)
        layer1_ffn(nc, k, resident, resident)
        small_head_attention(nc, k, "a2", resident, resident, ctx_tile, "l2_", False, 2)
        layer2_ffn(nc, k, resident, resident)
        small_head_attention(nc, k, "a3", resident, resident, ctx_tile, "l3_", True, 3)
        layer3_ffn(nc, k, resident, out_tile)


def shape_constants():
    c = {}
    tok, seq = np.arange(P), np.arange(P) // SEQ
    c["ident"] = np.eye(P, dtype=np.float32)
    seen = (seq[:, None] == seq[None, :]) & (tok[None, :] <= tok[:, None])
    c["causal"] = np.where(seen, 0.0, -1e30).astype(np.float32)
    c["desc"] = np.broadcast_to(np.arange(NE, 0, -1, dtype=np.float32), (P, NE)).copy()
    row = np.arange(P)
    c["jmask"] = ((row // 8 % 4)[:, None] == np.arange(4)[None, :]).astype(np.float32)
    inv = (1.0 / 10000.0 ** (np.arange(0, 8, 2, dtype=np.float32) / 8)).astype(np.float32)
    angle = (tok % SEQ).astype(np.float32)[None, :] * inv[row % 4][:, None]
    sign = np.where(row % 8 < 4, -1.0, 1.0)[:, None]
    cos, sin = np.cos(angle), np.sin(angle) * sign
    q = 8.0 ** -0.5
    c["rope"] = np.stack([np.stack([cos * q, cos], 1), np.stack([sin * q, sin], 1)], 1).astype(np.float32)
    b32, n32 = np.arange(32) // 16, np.arange(32) % 16
    c["mask_up"] = ((b32[:, None] == seq[None, :]) & (n32 % 2 == 1)[:, None] & (n32 < 8)[:, None]).astype(np.float32)
    down = (b32[:, None] == seq[None, :]) & (n32 % 2 == 1)[:, None] & (n32 > 8)[:, None]
    c["mask_down"] = np.tile(down, (4, 1)).astype(np.float32)
    c["sel_token"] = (tok[:, None] == (SEQ * b32 + n32)[None, :]).astype(np.float32)
    i = np.arange(CH)
    c["sel_up"] = np.broadcast_to((n32[:, None] == 2 * i + 1)[:, :, None], (32, CH, P)).astype(np.float32)
    c["sel_down"] = np.broadcast_to(np.tile(n32[:, None] == 2 * i + 9, (4, 1))[:, :, None], (P, CH, 32))\
        .astype(np.float32)
    return c


def lay_out(v):
    def t(a):
        return np.ascontiguousarray(np.asarray(a).T)

    def rows(a):
        a = np.asarray(a)
        return np.ascontiguousarray(a.reshape(-1, P, a.shape[-1]).transpose(1, 0, 2))

    def parity(a):
        a = t(a).reshape(P, PAIRS, 2, 8)
        z = np.zeros((P, 2, PAIRS, 2, 8), a.dtype)
        for j in range(2):
            z[:, j, :, j, :] = a[:, :, j, :]
        return z.reshape(P, 2, P)

    swap = np.arange(P) ^ 4
    d = shape_constants()
    d["x"] = np.asarray(v["x"]).reshape(NT * P, P)
    d["ctxT"] = t(np.asarray(v["ctx_1024"]).reshape(NT * P, P))
    g = np.concatenate([np.asarray(v["g_xattn"]), np.asarray(v["g_ffn"])])
    d["gates"] = np.broadcast_to(g, (P, 8)).copy()
    d["l0_wqT"], d["l0_wkT"], d["l0_wv"] = t(v["L0_xattn_w_q"]), t(v["L0_xattn_w_k"]), np.asarray(v["L0_xattn_w_v"])
    d["l0_w1T"] = t(v["L0_ffn_w1"]).reshape(P, CH, P)
    d["l0_convw"] = np.broadcast_to(t(np.asarray(v["L0_ffn_conv_w"])[:, 0, :]), (P, 3, HID)).copy()
    d["row_biases"] = np.concatenate([np.asarray(v[n]) for n in ("L0_ffn_conv_b", "L2_xattn_bo", "L3_ffn_b2")])[None]
    d["l0_w2T"] = rows(t(v["L0_ffn_w2"]))
    for n in "qkv":
        d[f"l1_w{n}T"] = rows(t(np.asarray(v[f"L1_xattn_W{n}"]).reshape(P, -1)))
    d["l1_wo"] = rows(np.asarray(v["L1_xattn_Wo"]).reshape(-1, P))
    d["l1_gateT"] = t(v["L1_ffn_gate_w"])
    d["l1_wgT"] = t(np.asarray(v["L1_ffn_w_gate"]).reshape(HID, P))
    d["l1_wuT"] = t(np.asarray(v["L1_ffn_w_up"]).reshape(HID, P))
    d["l1_wdT"] = rows(np.asarray(v["L1_ffn_w_down"]).transpose(0, 2, 1).reshape(HID, P))
    for n in ("2", "3"):
        a = f"L{n}_xattn_W"
        d[f"l{n}_wqT"], d[f"l{n}_wkT"], d[f"l{n}_woT"] = t(v[a + "q"]), t(v[a + "k"]), t(v[a + "o"])
        d[f"l{n}_wvT2"] = parity(v[a + "v"])
    d["l3_wqrT"], d["l3_wkrT"] = t(np.asarray(v["L3_xattn_Wq"])[swap]), t(np.asarray(v["L3_xattn_Wk"])[swap])
    for n in "qkv":
        d["l2_b" + n] = np.asarray(v["L2_xattn_b" + n]).reshape(P, 1)
    d["l2_wrT"], d["l2_wkfT"], d["l2_wvfT"] = t(v["L2_ffn_W_r"]), t(v["L2_ffn_W_k"]), t(v["L2_ffn_W_v"])
    d["l2_mur"], d["l2_muk"] = np.asarray(v["L2_ffn_mu_r"]).reshape(P, 1), np.asarray(v["L2_ffn_mu_k"]).reshape(P, 1)
    d["l3_w1T"], d["l3_w2T"] = t(v["L3_ffn_W1"]), rows(t(v["L3_ffn_W2"]))
    d["l3_b1"] = np.pad(np.asarray(v["L3_ffn_b1"]).reshape(1, HID), ((0, P - 33), (0, 0)))
    d["l3_scale"] = np.broadcast_to(np.asarray(v["L3_ffn_scale"]).reshape(1, 1), (P, 1)).copy()
    return {n: np.ascontiguousarray(a) for n, a in d.items()}


def kernel(**inputs):
    import concourse.bacc as bacc
    from concourse.bass_utils import run_bass_kernel_spmd

    nc = bacc.Bacc("TRN2", target_bir_lowering=False, num_devices=1)
    arrays, w = {}, {}
    for name, a in lay_out(inputs).items():
        arrays[f"in_{name}"] = a
        w[name] = nc.dram_tensor(f"in_{name}", a.shape, mybir.dt.from_np(a.dtype), kind="ExternalInput").ap()
    out = nc.dram_tensor("out_x", (NT * P, P), F32, kind="ExternalOutput").ap()
    build(nc, w, out)
    r = run_bass_kernel_spmd(nc, [arrays], core_ids=[0])
    return r.results[0]["out_x"].reshape(NT * P // SEQ, SEQ, P)
```

```python
from contextlib import ExitStack

import numpy as np

import concourse.bass as bass
from concourse import mybir

F32 = mybir.dt.float32
BF16 = mybir.dt.bfloat16
ALU = mybir.AluOpType
ACT = mybir.ActivationFunctionType
AX = mybir.AxisListType

P = 128
SEQ = 64
NB = P // SEQ
NT = 32
SLOTS = 4
UNROLL = SLOTS
NH = 16
PAIRS = NH // 2
HID = 512
CH = HID // P
NE = 8
EPS = 1e-5
MAGIC = 12582912.0


def live(s, lag):
    return not isinstance(s, int) or 0 <= s - lag < NT


def exists(t):
    return not isinstance(t, int) or t >= 0


def moved(t, n):
    return t * (16 // SLOTS) + (16 - n * (16 // SLOTS))


def run_steps(eng, step, last_lag):
    peel = -(-(last_lag + SLOTS) // UNROLL) * UNROLL
    for s in range(peel):
        step(s, s % SLOTS)
    with eng.Fori(peel, NT - UNROLL + 1, UNROLL) as s:
        for n in range(UNROLL):
            step(s + n, n)
    for s in range(NT, NT + last_lag + 1):
        step(s, s % SLOTS)


def semaphores(nc, c):
    taken = []

    def close():
        nc.clear_and_free_semaphores(taken)
        nc.all_engine_barrier()

    def allocate(name):
        taken.append(nc.alloc_semaphore(name=name))
        return taken[-1]

    c.callback(close)
    return allocate


class Stream:

    def __init__(self, nc, c, name, src, dst, ctx=None):
        self.nc, self.c, self.name, self.src, self.dst, self.ctx_src = nc, c, name, src, dst, ctx
        self.allocate = semaphores(nc, c)
        self.xin = self.sb("xin", [P, SLOTS, P])
        self.xres = self.sb("xres", [P, SLOTS, P])
        self.xout = self.sb("xout", [P, SLOTS, P])
        self.xh = self.two("xh", [P, P])
        self.xT = self.two("xT", [P, P])
        self.bn = self.two("bn", [P, 6])
        self.mv = self.two("mv", [P, 2])
        self.var = self.two("var", [P, 1])
        self.rstd = self.two("rstd", [P, 1])
        self.x_loaded = self.sems("x_loaded")
        self.res_loaded = self.sems("res_loaded")
        self.stored = self.sems("stored")
        if ctx is not None:
            self.ctxT = self.sb("ctxT", [P, SLOTS, P])
            self.ctx_loaded = self.sems("ctx_loaded")
            self.ctx_used = None
        self.bn_done = self.sem("bn_done")
        self.bn_waited = self.sem("bn_waited")
        self.mv_done = self.sem("mv_done")
        self.var_done = self.sem("var_done")
        self.rstd_done = self.sem("rstd_done")
        self.xh_done = self.sem("xh_done")
        self.xtr_done = self.sem("xtr_done")
        self.xT_done = self.sem("xT_done")
        self.o_done = self.sem("o_done")
        self.res_done = self.sem("res_done")

    def sem(self, n):
        return self.allocate(f"{self.name}_{n}")

    def sems(self, n):
        return [self.sem(f"{n}{i}") for i in range(2)]

    def sb(self, n, shape, dt=F32):
        return self.c.enter_context(self.nc.sbuf_tensor(f"{self.name}_{n}", shape, dt))

    def two(self, n, shape, dt=F32):
        return [self.sb(f"{n}{i}", shape, dt) for i in range(2)]

    def bank(self, n, dt=F32):
        return self.c.enter_context(
            self.nc.psum_tensor(f"{self.name}_{n}", [P, 512 if dt == F32 else 1024], dt))

    def own_wait(self, eng, t):
        if not isinstance(t, int):
            eng.wait_ge(self.x_loaded[0], 16)

    def load(self, sp, t, n, row):
        self.own_wait(sp, t)
        if exists(t - SLOTS):
            sp.wait_ge(self.xh_done, t + 2 - SLOTS)
        sp.dma_start(self.xin[:, n:n + 2, :], self.src(row)).then_inc(self.x_loaded[n // 2], 16)

    def load_ctx(self, sp, t, n, row):
        self.own_wait(sp, t)
        if exists(t - SLOTS):
            sp.wait_ge(self.ctx_used[0], self.ctx_used[1] * (t + 2 - SLOTS))
        sp.dma_start(self.ctxT[:, n:n + 2, :], self.ctx_src(row)).then_inc(self.ctx_loaded[n // 2], 16)

    def load_res(self, sp, t, n, row):
        self.own_wait(sp, t)
        if exists(t - SLOTS):
            sp.wait_ge(self.res_done, t + 2 - SLOTS)
        sp.dma_start(self.xres[:, n:n + 2, :], self.src(row)).then_inc(self.res_loaded[n // 2], 16)

    def store(self, sp, t, n, row):
        self.own_wait(sp, t)
        sp.wait_ge(self.res_done, t + 2)
        sp.dma_start(self.dst(row), self.xout[:, n:n + 2, :]).then_inc(self.stored[n // 2], 16)

    def sp_program(self, sp, add_lag):
        res_lag = (add_lag - 1) // 2 * 2
        store_lag = add_lag // 2 * 2 + 2

        def step(s, n):
            if n % 2:
                return
            row = {lag: (s - lag) * P if isinstance(s, int) else sp.snap((s - lag) * P)
                   for lag in {0, 2, res_lag, store_lag}}
            if live(s, 0):
                self.load(sp, s, n, row[0])
            if self.ctx_src is not None:
                if live(s, 2):
                    self.load_ctx(sp, s - 2, (n - 2) % SLOTS, row[2])
            if live(s, res_lag):
                self.load_res(sp, s - res_lag, (n - res_lag) % SLOTS, row[res_lag])
            if live(s, store_lag):
                self.store(sp, s - store_lag, (n - store_lag) % SLOTS, row[store_lag])

        run_steps(sp, step, store_lag)
        for h in range(2):
            sp.wait_ge(self.stored[h], moved(NT - SLOTS + 2 * h, 2 * h))

    def bn_first(self, dve, t, n):
        if n % 2 == 0:
            dve.wait_ge(self.x_loaded[n // 2], moved(t, n))
        self.nc.vector.bn_stats(self.bn[n % 2][:, :], self.xin[:, n, :]).then_inc(self.bn_done, 1)

    def bn_second(self, dve, t, p):
        dve.wait_ge(self.bn_done, t + 1)
        dve.sem_inc(self.bn_waited, 1)
        self.nc.vector.bn_aggr(self.mv[p][:, :], self.bn[p][:, :]).then_inc(self.mv_done, 1)

    def bn_third(self, dve, t, p):
        dve.wait_ge(self.mv_done, t + 1)
        if exists(t - 2):
            dve.wait_ge(self.rstd_done, t - 1)
        self.nc.vector.tensor_scalar_add(self.var[p][:, :], self.mv[p][:, 1:2], EPS).then_inc(self.var_done, 1)

    def ln_pow(self, pool, t, p, minus_half):
        pool.wait_ge(self.var_done, t + 1)
        if exists(t - 2):
            pool.wait_ge(self.xh_done, t - 1)
        self.nc.gpsimd.tensor_tensor(self.rstd[p][:, :], self.var[p][:, :], minus_half[:, :],
                                     ALU.pow).then_inc(self.rstd_done, 1)

    def ln_norm(self, dve, t, n):
        p = n % 2
        dve.wait_ge(self.rstd_done, t + 1)
        if exists(t - 2):
            dve.wait_ge(self.xtr_done, t - 1)
        self.nc.vector.tensor_scalar(self.xh[p][:, :], self.xin[:, n, :], self.mv[p][:, 0:1],
                                     self.rstd[p][:, :], ALU.subtract, ALU.mult).then_inc(self.xh_done, 1)

    def x_transpose(self, pe, t, p, psX, ident, ready=None, src=None):
        pe.wait_ge(ready or self.xh_done, t + 1)
        if exists(t - 1):
            pe.wait_ge(self.xT_done, t)
        self.nc.tensor.transpose(psX[:, 0:P], (src or self.xh)[p][:, :], ident[:, :]).then_inc(self.xtr_done, 1)

    def x_copy(self, act, t, p, psX, used, per):
        act.wait_ge(self.xtr_done, t + 1)
        if exists(t - 2):
            act.wait_ge(used, per * (t - 1))
        self.nc.scalar.copy(self.xT[p][:, :], psX[:, 0:P]).then_inc(self.xT_done, 1)

    def add_residual(self, dve, t, n, psO, coef):
        dve.wait_ge(self.o_done, t + 1)
        if n % 2 == 0:
            dve.wait_ge(self.res_loaded[n // 2], moved(t, n))
            if exists(t - SLOTS):
                dve.wait_ge(self.stored[n // 2], moved(t - SLOTS, n))
        self.nc.vector.scalar_tensor_tensor(self.xout[:, n, :], psO[:, 0:P], coef, self.xres[:, n, :],
                                            ALU.mult, ALU.add).then_inc(self.res_done, 1)


FIRST = {"ident": [P, P], "l0_wqT": [P, P], "l0_wkT": [P, P], "l0_wv": [P, P], "causal": [P, P], "gates": [P, 8]}
L0_FFN = {"l0_w1T": [P, CH, P], "l0_w2T": [P, CH, P], "l0_convw": [P, 3, HID]}
L1_ATT = {"l1_" + n: [P, PAIRS, P] for n in ("wqT", "wkT", "wvT", "wo")}
OTHERS = {"l1_gateT": [P, NE], "l1_wgT": [P, HID], "l1_wuT": [P, HID], "l1_wdT": [P, CH, P], "desc": [P, NE],
          "l2_wqT": [P, P], "l2_wkT": [P, P], "l2_wvT2": [P, 2, P], "l2_woT": [P, P],
          "l2_bq": [P, 1], "l2_bk": [P, 1], "l2_bv": [P, 1],
          "l2_wrT": [P, P], "l2_wkfT": [P, P], "l2_wvfT": [P, P], "l2_mur": [P, 1], "l2_muk": [P, 1],
          "l3_wqT": [P, P], "l3_wkT": [P, P], "l3_wqrT": [P, P], "l3_wkrT": [P, P],
          "l3_wvT2": [P, 2, P], "l3_woT": [P, P], "rope": [P, 2, 2, P], "jmask": [P, 4],
          "l3_w1T": [P, HID], "l3_w2T": [P, CH, P], "l3_scale": [P, 1],
          "lora_up0": [P, HID], "lora_up1": [P, HID],
          "mask_up": [32, P], "mask_down": [P, P], "sel_token": [P, 32], "sel_up": [32, CH, P],
          "sel_down": [P, CH, 32]}
PACKS = {"first": FIRST, "l0_ffn": L0_FFN, "l1_att": L1_ATT, "others": OTHERS}


def columns(shapes):
    at, where = 0, {}
    for name, shape in shapes.items():
        n = int(np.prod(shape[1:]))
        where[name] = at, at + n
        at += n
    return where


def pack_tile(nc, c, pack):
    where = columns(PACKS[pack])
    tile = c.enter_context(nc.sbuf_tensor("pack_" + pack, [P, max(b for _, b in where.values())], F32))
    views = {}
    for name, shape in PACKS[pack].items():
        a, b = where[name]
        v = tile[0:shape[0], a:b]
        if len(shape) == 3:
            v = v.rearrange("p (a b) -> p a b", a=shape[1])
        elif len(shape) == 4:
            v = v.rearrange("p (a b c) -> p a b c", a=shape[1], b=shape[2])
        views[name] = v
    return tile, views


def prepare_first(nc, c, w):
    allocate = semaphores(nc, c)
    def sb(name, shape, dt=F32):
        return c.enter_context(nc.sbuf_tensor(name, shape, dt))

    first, k = pack_tile(nc, c, "first")
    others, views = pack_tile(nc, c, "others")
    k.update(views)
    k["others"] = others
    k["lora_up"] = k["lora_up0"], k["lora_up1"]
    k["tg"] = sb("tanh_gates", [P, 8])
    k["half_gate"] = sb("half_gate", [P, 8])
    k["A0"] = sb("A0", [P, P])
    k["AT"] = sb("AT", [P, NH, P])
    k["B"] = sb("B", [P, 2, PAIRS, P])
    k["WJ"] = sb("WJ", [P, 3, HID])
    k["tern2"] = sb("tern2", [P, CH, P], BF16)
    k["bias3"] = sb("bias3", [P, HID + 2 * P], BF16)
    k["ones_bf"] = sb("ones_bf", [P, P], BF16)
    k["onesf"] = sb("onesf", [P, P])
    k["minus_half"] = sb("minus_half", [P, 1])
    k["coef2"] = sb("coef2", [P, 1])
    for n in ("wr0", "wr1", "wk0", "wk1"):
        k[n] = sb("l2f_" + n, [P, P])

    k["row_biases"] = sb("row_biases", [1, HID + 2 * P])
    k["rows_loaded"], k["others_loaded"], k["a_loaded"] = (allocate(n) for n in (
        "rows_loaded", "others_loaded", "a_loaded"))

    with ExitStack() as pc:
        sem = semaphores(nc, pc)
        ps = pc.enter_context(nc.psum_tensor("prep_ps", [P, 512], F32))
        loaded, prod, copied, tanhed, filled = (sem("first_" + n) for n in (
            "loaded", "prod", "copied", "tanhed", "filled"))
        with nc.Block() as block:
            @block.sync
            def _(sp):
                sp.dma_start(first[:, :], w["first"]).then_inc(loaded, 16)
                sp.dma_start(k["row_biases"][:, :], w["row_biases"]).then_inc(k["rows_loaded"], 16)

            @block.tensor
            def _(pe):
                pe.wait_ge(loaded, 16)
                nc.tensor.matmul(ps[:, 0:P], k["l0_wqT"], k["l0_wkT"], start=True, stop=True).then_inc(prod, 1)

            @block.scalar
            def _(act):
                act.wait_ge(loaded, 16)
                nc.scalar.activation(k["tg"][:, :], k["gates"], ACT.Tanh).then_inc(tanhed, 1)
                act.wait_ge(prod, 1)
                nc.scalar.activation(k["A0"][:, :], ps[:, 0:P], ACT.Copy, scale=float(P) ** -0.5).then_inc(copied, 1)

            @block.vector
            def _(dve):
                nc.vector.memset(k["minus_half"][:, :], -0.5)
                nc.vector.memset(k["onesf"][:, :], 1.0)
                nc.vector.memset(k["ones_bf"][:, :], 1.0)
                nc.vector.memset(k["bias3"][:, :], 0.0).then_inc(filled, 1)
    return k


class QuantisedWeights:

    def __init__(self, nc, c, w, k, allocate):
        self.nc, self.w, self.k = nc, w, k
        self.pack, self.f = pack_tile(nc, c, "l0_ffn")
        self.asum, self.small = (c.enter_context(nc.sbuf_tensor(n, [P, 4], F32)) for n in ("asum", "small"))
        self.left = c.enter_context(nc.sbuf_tensor("bias_left", [1, 2, HID + 2 * P], F32))
        self.mid = c.enter_context(nc.sbuf_tensor("bias_mid", [1, HID + 2 * P], BF16))
        self.bias_chain = allocate("bias_chain")
        self.wr = [c.enter_context(nc.sbuf_tensor(f"wrounded{i}", [P, CH, P], F32)) for i in range(2)]
        self.ps = c.enter_context(nc.psum_tensor("asum_ps", [P, 512], F32))
        self.loaded, self.sums_ready, self.summed, self.chain, self.chain2 = (allocate("quant_" + n) for n in (
            "loaded", "sums_ready", "summed", "chain", "chain2"))

    def load(self, act):
        act.dma_start(self.pack[:, :], self.w["l0_ffn"]).then_inc(self.loaded, 16)

    def split_biases(self, dve):
        nc, chain, rows, left, mid, bias3 = (
            self.nc, self.bias_chain, self.k["row_biases"], self.left, self.mid, self.k["bias3"])
        dve.wait_ge(self.k["rows_loaded"], 16)
        nc.vector.tensor_copy(bias3[0:1, :], rows[:, :]).then_inc(chain, 1)
        dve.wait_ge(chain, 1)
        nc.vector.tensor_tensor(left[:, 0, :], rows[:, :], bias3[0:1, :], ALU.subtract).then_inc(chain, 1)
        dve.wait_ge(chain, 2)
        nc.vector.tensor_copy(mid[:, :], left[:, 0, :]).then_inc(chain, 1)
        dve.wait_ge(chain, 3)
        nc.vector.tensor_copy(bias3[32:33, :], mid[:, :]).then_inc(chain, 1)
        nc.vector.tensor_tensor(left[:, 1, :], left[:, 0, :], mid[:, :], ALU.subtract).then_inc(chain, 1)
        dve.wait_ge(chain, 5)
        nc.vector.tensor_copy(bias3[64:65, :], left[:, 1, :])

    def sums(self, dve):
        dve.wait_ge(self.loaded, 16)
        for i, n in enumerate(("l0_w1T", "l0_w2T")):
            self.nc.vector.tensor_reduce(self.asum[:, i:i + 1], self.f[n], AX.XY, ALU.add,
                                         apply_absolute_value=True).then_inc(self.sums_ready, 1)

    def total(self, pe):
        pe.wait_ge(self.sums_ready, 2)
        self.nc.tensor.matmul(self.ps[:, 0:2], self.k["onesf"][:, :], self.asum[:, 0:2], start=True, stop=True)\
            .then_inc(self.summed, 1)

    def scales(self, dve):
        nc, small = self.nc, self.small
        dve.wait_ge(self.summed, 1)
        nc.vector.tensor_scalar(small[:, 0:2], self.ps[:, 0:2], 1.0 / (HID * P), 1e-5, ALU.mult, ALU.max)\
            .then_inc(self.chain, 1)
        dve.wait_ge(self.chain, 1)
        nc.vector.reciprocal(small[:, 2:4], small[:, 0:2]).then_inc(self.chain, 1)
        nc.vector.tensor_scalar(self.k["coef2"][:, :], small[:, 1:2], self.k["tg"][:, 4:5], 0.5, ALU.mult, ALU.mult)

    def first(self, pool):
        nc, k, wr = self.nc, self.k, self.wr[0][:, :, :].rearrange("p a b -> p (a b)")
        pool.wait_ge(self.chain, 2)
        nc.gpsimd.tensor_scalar(wr, self.f["l0_w1T"].rearrange("p a b -> p (a b)"), self.small[:, 2:3], 1.0,
                                ALU.mult, ALU.min).then_inc(self.chain, 1)
        pool.wait_ge(self.chain, 3)
        nc.gpsimd.tensor_scalar(wr, wr, -1.0, MAGIC, ALU.max, ALU.add).then_inc(self.chain, 1)
        pool.wait_ge(self.chain, 4)
        nc.gpsimd.tensor_scalar(wr, wr, -MAGIC, self.small[:, 0:1], ALU.add, ALU.mult).then_inc(self.chain, 1)
        pool.wait_ge(self.chain, 5)
        for j in range(3):
            nc.gpsimd.tensor_tensor(k["WJ"][:, j, :], wr, self.f["l0_convw"][:, j, :], ALU.mult)

    def second(self, dve):
        nc, wr = self.nc, self.wr[1]
        dve.wait_ge(self.chain, 2)
        nc.vector.tensor_scalar(wr[:, :, :], self.f["l0_w2T"], self.small[:, 3:4], 1.0, ALU.mult, ALU.min)\
            .then_inc(self.chain2, 1)
        dve.wait_ge(self.chain2, 1)
        nc.vector.tensor_scalar(wr[:, :, :], wr[:, :, :], -1.0, MAGIC, ALU.max, ALU.add).then_inc(self.chain2, 1)
        dve.wait_ge(self.chain2, 2)
        nc.vector.tensor_scalar_add(self.k["tern2"][:, :, :], wr[:, :, :], -MAGIC)


class LaterWeights:
    CHUNKS = 8

    def __init__(self, nc, c, w, k, allocate):
        self.nc, self.w, self.k = nc, w, k
        self.l1_att, a = pack_tile(nc, c, "l1_att")
        self.small = c.enter_context(nc.sbuf_tensor("small2", [P, 2], F32))
        self.ps = [c.enter_context(nc.psum_tensor(f"later_ps{i}", [P, 512], F32)) for i in range(2)]
        self.prod, self.copied, self.chain = (allocate("later_" + n) for n in ("prod", "copied", "chain"))
        self.groups = []
        for j in range(2):
            for q in range(0, PAIRS, 4):
                r = slice(64 * j, 64 * j + 64)
                part = [(a["l1_wkT"][r, i, :], a["l1_wqT"][r, i, :]) for i in range(q, q + 4)]
                self.groups.append(
                    (part, k["AT"][:, :, :].rearrange("p (a j) b -> p a j b", j=2)[:, q:q + 4, j, :], 0.125))
                part = [(a["l1_wvT"][r, i, :], a["l1_wo"][r, i, :]) for i in range(q, q + 4)]
                self.groups.append((part, k["B"][:, j, q:q + 4, :], 1.0))

    def load(self, act, i):
        for tile, name, sem in ((self.l1_att, "l1_att", "a_loaded"), (self.k["others"], "others", "others_loaded")):
            n = tile.shape[1]
            cut = slice(i * n // self.CHUNKS, (i + 1) * n // self.CHUNKS)
            act.dma_start(tile[:, cut], self.w[name][:, cut]).then_inc(self.k[sem], 16)

    def multiply(self, pe, g):
        if g == 0:
            pe.wait_ge(self.k["a_loaded"], 16 * self.CHUNKS)
        if g >= 2:
            pe.wait_ge(self.copied, g - 1)
        for i, (lhsT, rhs) in enumerate(self.groups[g][0]):
            last = self.nc.tensor.matmul(self.ps[g % 2][:, i * P:(i + 1) * P], lhsT, rhs, start=True, stop=True)
        last.then_inc(self.prod, 1)

    def copy(self, act, g):
        _, out, scale = self.groups[g]
        act.wait_ge(self.prod, g + 1)
        self.nc.scalar.activation(out, self.ps[g % 2][:, :].rearrange("p (a b) -> p a b", a=4), ACT.Copy,
                                  scale=scale).then_inc(self.copied, 1)

    def scale(self, pool):
        nc, k, small, chain = self.nc, self.k, self.small, self.chain
        pool.wait_ge(k["others_loaded"], 16 * self.CHUNKS)
        nc.gpsimd.tensor_scalar_mul(k["half_gate"][:, :], k["tg"][:, :], 0.5)
        for i, (m, wx, a, b) in enumerate((("l2_mur", "l2_wrT", "wr0", "wr1"), ("l2_muk", "l2_wkfT", "wk0", "wk1"))):
            nc.gpsimd.tensor_scalar(small[:, i:i + 1], k[m], -1.0, 1.0, ALU.mult, ALU.add).then_inc(chain, 1)
            nc.gpsimd.tensor_scalar_mul(k[a][:, :], k[wx], k[m])
            pool.wait_ge(chain, i + 1)
            nc.gpsimd.tensor_scalar_mul(k[b][:, :], k[wx], small[:, i:i + 1])
        nc.gpsimd.tensor_scalar_mul(k["l2_bq"], k["l2_bq"], 8.0 ** -0.5)
        nc.gpsimd.tensor_scalar_mul(k["mask_down"], k["mask_down"], k["l3_scale"]).then_inc(chain, 1)
        pool.wait_ge(chain, 3)
        nc.gpsimd.tensor_scalar_mul(k["mask_up"], k["mask_up"], k["l3_scale"][0:32, :])


def load_gate(k, i):
    return k["tg"][:, i:i + 1]


def layer0_attention(nc, k, src, dst, ctx, w):
    LAG = 5
    with ExitStack() as c:
        S = Stream(nc, c, "a0", src, dst, ctx)
        qT, V, E, PT = (S.two(n, [P, P]) for n in ("qT", "V", "E", "PT"))
        nmax, ssum, rinv, coef = (S.two(n, [P, 1]) for n in ("nmax", "ssum", "rinv", "coef"))
        psX, psQ, psV, psS, psPT, psO = (S.bank(n) for n in ("psX", "psQ", "psV", "psS", "psPT", "psO"))
        q_done, q_copied, v_done, v_copied, s_done, masked, max_done, exp_done, rinv_done, coef_done, \
            ptr_done, pt_copied = (S.sem(n) for n in (
                "q_done", "q_copied", "v_done", "v_copied", "s_done", "masked", "max_done", "exp_done",
                "rinv_done", "coef_done", "ptr_done", "pt_copied"))
        S.ctx_used = s_done, 1
        quant = QuantisedWeights(nc, c, w, k, S.allocate)
        block = c.enter_context(nc.Block())

        @block.sync
        def _(sp):
            S.sp_program(sp, LAG)

        @block.gpsimd
        def _(pool):
            def step(s, n):
                q = n % 2
                if live(s, 1):
                    S.ln_pow(pool, s - 1, 1 - q, k["minus_half"])

            run_steps(pool, step, LAG)
            quant.first(pool)

        @block.tensor
        def _(pe):
            def project_q(t, p):
                pe.wait_ge(S.xT_done, t + 1)
                if exists(t - 1):
                    pe.wait_ge(q_copied, t)
                nc.tensor.matmul(psQ[:, 0:P], k["A0"][:, :], S.xT[p][:, :], start=True, stop=True).then_inc(q_done, 1)

            def project_v(t, n):
                if n % 2 == 0:
                    pe.wait_ge(S.ctx_loaded[n // 2], moved(t, n))
                if exists(t - 1):
                    pe.wait_ge(v_copied, t)
                nc.tensor.matmul(psV[:, 0:P], S.ctxT[:, n, :], k["l0_wv"][:, :], start=True, stop=True)\
                    .then_inc(v_done, 1)

            def scores(t, n):
                pe.wait_ge(q_copied, t + 1)
                if exists(t - 1):
                    pe.wait_ge(masked, t)
                nc.tensor.matmul(psS[:, 0:P], qT[n % 2][:, :], S.ctxT[:, n, :], start=True, stop=True)\
                    .then_inc(s_done, 1)

            def transpose_p(t, p):
                pe.wait_ge(exp_done, t + 1)
                if exists(t - 1):
                    pe.wait_ge(pt_copied, t)
                nc.tensor.transpose(psPT[:, 0:P], E[p][:, :], k["ident"][:, :]).then_inc(ptr_done, 1)

            def values(t, p):
                pe.wait_ge(pt_copied, t + 1)
                pe.wait_ge(v_copied, t + 1)
                if exists(t - 1):
                    pe.wait_ge(S.res_done, t)
                nc.tensor.matmul(psO[:, 0:P], PT[p][:, :], V[p][:, :], start=True, stop=True).then_inc(S.o_done, 1)

            def step(s, n):
                q = n % 2
                if isinstance(s, int) and s == NT + 1:
                    quant.total(pe)
                if live(s, 4):
                    scores(s - 4, n)
                if live(s, 5):
                    transpose_p(s - 5, 1 - q)
                if live(s, 3):
                    project_q(s - 3, 1 - q)
                if live(s, 5):
                    values(s - 5, 1 - q)
                if live(s, 3):
                    project_v(s - 3, (n - 3) % SLOTS)
                if live(s, 2):
                    S.x_transpose(pe, s - 2, q, psX, k["ident"])

            run_steps(pe, step, LAG)

        @block.scalar
        def _(act):
            def step(s, n):
                q = n % 2
                if live(s, 5):
                    t, p = s - 5, 1 - q
                    act.wait_ge(ptr_done, t + 1)
                    if exists(t - 2):
                        act.wait_ge(S.o_done, t - 1)
                    nc.scalar.copy(PT[p][:, :], psPT[:, 0:P]).then_inc(pt_copied, 1)
                if live(s, 3):
                    t, p = s - 3, 1 - q
                    act.wait_ge(q_done, t + 1)
                    if exists(t - 2):
                        act.wait_ge(s_done, t - 1)
                    nc.scalar.copy(qT[p][:, :], psQ[:, 0:P]).then_inc(q_copied, 1)
                if live(s, 4):
                    t, p = s - 4, q
                    act.wait_ge(max_done, t + 1)
                    if exists(t - 2):
                        act.wait_ge(rinv_done, t - 1)
                    nc.scalar.activation(E[p][:, :], E[p][:, :], ACT.Exp, bias=nmax[p][:, :],
                                         accum_out=ssum[p][:, :]).then_inc(exp_done, 1)
                if live(s, 3):
                    t, p = s - 3, 1 - q
                    act.wait_ge(v_done, t + 1)
                    if exists(t - 2):
                        act.wait_ge(S.o_done, t - 1)
                    nc.scalar.copy(V[p][:, :], psV[:, 0:P]).then_inc(v_copied, 1)
                if live(s, 2):
                    S.x_copy(act, s - 2, q, psX, q_done, 1)
                if isinstance(s, int) and s == 6:
                    quant.load(act)

            run_steps(act, step, LAG)

        @block.vector
        def _(dve):
            def step(s, n):
                q = n % 2
                if live(s, 2):
                    S.ln_norm(dve, s - 2, (n - 2) % SLOTS)
                if live(s, 4):
                    t, p = s - 4, q
                    dve.wait_ge(s_done, t + 1)
                    if exists(t - 2):
                        dve.wait_ge(ptr_done, t - 1)
                    nc.vector.tensor_tensor(E[p][:, :], psS[:, 0:P], k["causal"][:, :], ALU.add).then_inc(masked, 1)
                if live(s, 1):
                    S.bn_first(dve, s - 1, (n - 1) % SLOTS)
                if live(s, 4):
                    t, p = s - 4, q
                    dve.wait_ge(masked, t + 1)
                    if exists(t - 2):
                        dve.wait_ge(exp_done, t - 1)
                    nc.vector.tensor_reduce(nmax[p][:, :], E[p][:, :], AX.X, ALU.max, negate=True)\
                        .then_inc(max_done, 1)
                if live(s, 1):
                    S.bn_second(dve, s - 1, 1 - q)
                if live(s, 5):
                    t, p = s - 5, 1 - q
                    dve.wait_ge(exp_done, t + 1)
                    if exists(t - 2):
                        dve.wait_ge(coef_done, t - 1)
                    nc.vector.reciprocal(rinv[p][:, :], ssum[p][:, :]).then_inc(rinv_done, 1)
                if live(s, 1):
                    S.bn_third(dve, s - 1, 1 - q)
                if live(s, 5):
                    t, p = s - 5, 1 - q
                    dve.wait_ge(rinv_done, t + 1)
                    if exists(t - 2):
                        dve.wait_ge(S.res_done, t - 1)
                    nc.vector.tensor_scalar_mul(coef[p][:, :], rinv[p][:, :], load_gate(k, 0)).then_inc(coef_done, 1)
                if live(s, 5):
                    dve.wait_ge(coef_done, s - 4)
                    S.add_residual(dve, s - 5, (n - 5) % SLOTS, psO, coef[1 - q][:, :])
                if isinstance(s, int) and s == 0:
                    quant.split_biases(dve)
                if isinstance(s, int) and s == NT:
                    quant.sums(dve)
                if isinstance(s, int) and s == NT + 1:
                    quant.scales(dve)

            run_steps(dve, step, LAG)
            quant.second(dve)


def layer0_ffn(nc, k, src, dst, w):
    PADDED = SEQ + 2
    LAG = 6
    with ExitStack() as c:
        S = Stream(nc, c, "f0", src, dst)
        xpad = S.two("xpad", [P, NB, PADDED])
        xq, xd = S.two("xq", [P, P]), S.two("xd", [P, P])
        amax, step1, inv1, amax2, step2, inv2, coef = (
            S.two(n, [P, 1]) for n in ("amax", "step1", "inv1", "amax2", "step2", "inv2", "coef"))
        th, g, gm = (S.two(n, [P, HID]) for n in ("th", "g", "gm"))
        q2 = S.two("q2", [P, HID], BF16)
        q2T = S.two("q2T", [P, HID], BF16)
        magic, minus_magic = S.sb("magic", [P, 1]), S.sb("minus_magic", [P, 1])
        identb = S.sb("identb", [P, P], BF16)
        psX, psO = S.bank("psX"), S.bank("psO")
        psH = [S.bank(f"psH{i}") for i in range(2)]
        psT = S.bank("psT", BF16)
        xT_used = S.sem("xT_used")
        ready, amax_done, step_done, inv_done, round_done, xd_done, h_done, th_done, g_done, amax2_done, \
            step2_done, inv2_done, gm_done, q2_done, coef_done, qtr_done, qT_done = (S.sem(n) for n in (
                "ready", "amax_done", "step_done", "inv_done", "round_done", "xd_done", "h_done", "th_done",
                "g_done", "amax2_done", "step2_done", "inv2_done", "gm_done", "q2_done", "coef_done",
                "qtr_done", "qT_done"))
        later = LaterWeights(nc, c, w, k, S.allocate)
        block = c.enter_context(nc.Block())

        @block.sync
        def _(sp):
            S.sp_program(sp, LAG)

        @block.gpsimd
        def _(pool):
            nc.gpsimd.tensor_copy(identb[:, :], k["ident"][:, :]).then_inc(ready, 1)
            nc.gpsimd.memset(magic[:, :], MAGIC).then_inc(ready, 1)
            nc.gpsimd.memset(minus_magic[:, :], -MAGIC).then_inc(ready, 1)
            for p in range(2):
                nc.gpsimd.memset(xpad[p][:, :, :], 0.0).then_inc(ready, 1)

            def step(s, n):
                q = n % 2
                if live(s, 1):
                    S.ln_pow(pool, s - 1, 1 - q, k["minus_half"])

            run_steps(pool, step, LAG)
            later.scale(pool)

        @block.tensor
        def _(pe):
            def hidden_tap(t, p, j):
                if j == 0:
                    pe.wait_ge(S.xT_done, t + 1)
                    if exists(t - 2):
                        pe.wait_ge(g_done, t - 1)
                for b in range(NB):
                    last = nc.tensor.matmul(psH[p][64 * b:64 * b + 64, :], xpad[p][:, b, j:j + SEQ],
                                            k["WJ"][:, j, :], start=(j == 0), stop=False)
                if j == 2:
                    last.then_inc(xT_used, 1)

            def hidden_bias(t, p):
                for b in range(NB):
                    last = nc.tensor.matmul(psH[p][64 * b:64 * b + 64, :], k["ones_bf"][:, 0:64], k["bias3"][:, 0:HID],
                                            start=False, stop=True)
                last.then_inc(h_done, 1)

            def transpose_q(t, p):
                pe.wait_ge(q2_done, t + 1)
                if exists(t - 1):
                    pe.wait_ge(qT_done, t)
                for i in range(CH):
                    last = nc.tensor.transpose(psT[:, i * P:(i + 1) * P], q2[p][:, i * P:(i + 1) * P], identb[:, :])
                last.then_inc(qtr_done, 1)

            def down(t, p):
                pe.wait_ge(qT_done, t + 1)
                if exists(t - 1):
                    pe.wait_ge(S.res_done, t)
                for i in range(CH):
                    last = nc.tensor.matmul(psO[:, 0:P], q2T[p][:, i * P:(i + 1) * P], k["tern2"][:, i, :],
                                            start=(i == 0), stop=(i == CH - 1))
                last.then_inc(S.o_done, 1)

            pe.wait_ge(ready, 5)

            def step(s, n):
                q = n % 2
                if live(s, 3):
                    hidden_tap(s - 3, 1 - q, 0)
                if live(s, 6):
                    down(s - 6, q)
                if live(s, 3):
                    hidden_tap(s - 3, 1 - q, 1)
                if live(s, 2):
                    S.x_transpose(pe, s - 2, q, psX, k["ident"], ready=xd_done, src=xd)
                if live(s, 3):
                    hidden_tap(s - 3, 1 - q, 2)
                    hidden_bias(s - 3, 1 - q)
                if isinstance(s, int) and s >= NT:
                    later.multiply(pe, s - NT)
                if live(s, 5):
                    transpose_q(s - 5, 1 - q)

            run_steps(pe, step, LAG)
            later.multiply(pe, LAG + 1)

        @block.scalar
        def _(act):
            act.wait_ge(ready, 5)

            def step(s, n):
                q = n % 2
                if live(s, 5):
                    t, p = s - 5, 1 - q
                    act.wait_ge(gm_done, t + 1)
                    if exists(t - 2):
                        act.wait_ge(qtr_done, t - 1)
                    nc.scalar.activation(q2[p][:, :], gm[p][:, :], ACT.Identity, bias=minus_magic[:, :])\
                        .then_inc(q2_done, 1)
                if live(s, 2):
                    t, p = s - 2, q
                    act.wait_ge(S.xtr_done, t + 1)
                    if exists(t - 2):
                        act.wait_ge(xT_used, t - 1)
                    nc.scalar.copy(xpad[p][:, :, 1:1 + SEQ], psX[:, 0:P].rearrange("p (b s) -> p b s", b=NB))\
                        .then_inc(S.xT_done, 1)
                if live(s, 5):
                    t, p = s - 5, 1 - q
                    act.wait_ge(qtr_done, t + 1)
                    if exists(t - 2):
                        act.wait_ge(S.o_done, t - 1)
                    nc.scalar.copy(q2T[p][:, :], psT[:, 0:HID]).then_inc(qT_done, 1)
                if live(s, 4):
                    t, p = s - 4, q
                    act.wait_ge(inv2_done, t + 1)
                    if exists(t - 2):
                        act.wait_ge(q2_done, t - 1)
                    nc.scalar.activation(gm[p][:, :], g[p][:, :], ACT.Identity, bias=magic[:, :],
                                         scale=inv2[p][:, :]).then_inc(gm_done, 1)
                if live(s, 3):
                    t, p = s - 3, 1 - q
                    act.wait_ge(h_done, t + 1)
                    if exists(t - 2):
                        act.wait_ge(g_done, t - 1)
                    nc.scalar.activation(th[p][:, :], psH[p][:, :], ACT.Tanh, scale=0.5).then_inc(th_done, 1)
                if isinstance(s, int) and 2 <= s < 2 + later.CHUNKS:
                    later.load(act, s - 2)
                if isinstance(s, int) and s >= NT:
                    later.copy(act, s - NT)

            run_steps(act, step, LAG)
            later.copy(act, LAG + 1)

        @block.vector
        def _(dve):
            def step(s, n):
                q = n % 2
                ti, pi = s - 2, q
                tt, ph = s - 4, q
                if live(s, 2):
                    S.ln_norm(dve, ti, (n - 2) % SLOTS)
                if live(s, 1):
                    S.bn_first(dve, s - 1, (n - 1) % SLOTS)
                if live(s, 2):
                    dve.wait_ge(S.xh_done, ti + 1)
                    nc.vector.tensor_reduce(amax[pi][:, :], S.xh[pi][:, :], AX.X, ALU.max,
                                            apply_absolute_value=True).then_inc(amax_done, 1)
                if live(s, 1):
                    S.bn_second(dve, s - 1, 1 - q)
                if live(s, 2):
                    dve.wait_ge(amax_done, ti + 1)
                    nc.vector.tensor_scalar(step1[pi][:, :], amax[pi][:, :], 1e-5, 1.0 / 127.0, ALU.max, ALU.mult)\
                        .then_inc(step_done, 1)
                if live(s, 1):
                    S.bn_third(dve, s - 1, 1 - q)
                if live(s, 2):
                    dve.wait_ge(step_done, ti + 1)
                    nc.vector.reciprocal(inv1[pi][:, :], step1[pi][:, :]).then_inc(inv_done, 1)
                if live(s, 2):
                    dve.wait_ge(inv_done, ti + 1)
                    nc.vector.tensor_scalar(xq[pi][:, :], S.xh[pi][:, :], inv1[pi][:, :], MAGIC, ALU.mult, ALU.add)\
                        .then_inc(round_done, 1)
                if live(s, 6):
                    dve.wait_ge(coef_done, s - 5)
                    S.add_residual(dve, s - 6, (n - 6) % SLOTS, psO, coef[q][:, :])
                if live(s, 2):
                    dve.wait_ge(round_done, ti + 1)
                    if exists(ti - 2):
                        dve.wait_ge(S.xtr_done, ti - 1)
                    nc.vector.tensor_scalar(xd[pi][:, :], xq[pi][:, :], MAGIC, step1[pi][:, :],
                                            ALU.subtract, ALU.mult).then_inc(xd_done, 1)
                if live(s, 4):
                    dve.wait_ge(th_done, tt + 1)
                    if exists(tt - 2):
                        dve.wait_ge(gm_done, tt - 1)
                    nc.vector.scalar_tensor_tensor(g[ph][:, :], th[ph][:, :], 1.0, psH[ph][:, :], ALU.add, ALU.mult)\
                        .then_inc(g_done, 1)
                if live(s, 4):
                    dve.wait_ge(g_done, tt + 1)
                    nc.vector.tensor_reduce(amax2[ph][:, :], g[ph][:, :], AX.X, ALU.max,
                                            apply_absolute_value=True).then_inc(amax2_done, 1)
                if live(s, 4):
                    dve.wait_ge(amax2_done, tt + 1)
                    nc.vector.tensor_scalar(step2[ph][:, :], amax2[ph][:, :], 2e-5, 1.0 / 127.0, ALU.max, ALU.mult)\
                        .then_inc(step2_done, 1)
                if live(s, 4):
                    dve.wait_ge(step2_done, tt + 1)
                    nc.vector.reciprocal(inv2[ph][:, :], step2[ph][:, :]).then_inc(inv2_done, 1)
                if live(s, 4):
                    if exists(tt - 2):
                        dve.wait_ge(S.res_done, tt - 1)
                    nc.vector.tensor_scalar_mul(coef[ph][:, :], step2[ph][:, :], k["coef2"][:, :])\
                        .then_inc(coef_done, 1)

            run_steps(dve, step, LAG)


def softmax_max_sub(dve, nc, nmax, E, psS, t, p, s_done, max_done, sub_done, e_used):
    for hf in range(2):
        dve.wait_ge(s_done, 2 * t + hf + 1)
        if hf == 0:
            if exists(t - 2):
                dve.wait_ge(sub_done, 2 * t - 2)
        nc.vector.tensor_reduce(nmax[p][:, 8 * hf:8 * hf + 8], psS[hf][:, :].rearrange("p (h k) -> p h k", k=SEQ),
                                AX.X, ALU.max).then_inc(max_done, 1)
    for hf in range(2):
        dve.wait_ge(max_done, 2 * t + hf + 1)
        if hf == 0:
            if exists(t - 2):
                dve.wait_ge(e_used, 2 * t - 2)
        nc.vector.tensor_tensor(E[p][:, hf, :].rearrange("p (h k) -> p h k", k=SEQ),
                                psS[hf][:, :].rearrange("p (h k) -> p h k", k=SEQ),
                                nmax[p][:, 8 * hf:8 * hf + 8].unsqueeze(2).broadcast_to([P, 8, SEQ]),
                                ALU.subtract).then_inc(sub_done, 1)


def layer1_attention(nc, k, src, dst, ctx):
    LAG = 4
    with ExitStack() as c:
        S = Stream(nc, c, "a1", src, dst, ctx)
        T = S.two("T", [P, NB, NH, SEQ])
        U = S.two("U", [P, NB, PAIRS, P])
        E = S.two("E", [P, 2, 512])
        PT = S.two("PT", [P, PAIRS, P])
        rmax, ssum, rinv = (S.two(n, [P, NH]) for n in ("rmax", "ssum", "rinv"))
        psM = [S.bank(f"psM{i}") for i in range(2)]
        psS = [S.bank(f"psS{i}") for i in range(2)]
        psT = [S.bank(f"psT{i}") for i in range(2)]
        psX, psO = S.bank("psX"), S.bank("psO")
        proj_done, proj_copied, s_done, max_done, sub_done, exp_done, sum_done, rinv_done, p_done, \
            ptr_done, pt_copied = (S.sem(n) for n in (
                "proj_done", "proj_copied", "s_done", "max_done", "sub_done", "exp_done", "sum_done",
                "rinv_done", "p_done", "ptr_done", "pt_copied"))
        S.ctx_used = proj_done, 8
        block = c.enter_context(nc.Block())

        @block.sync
        def _(sp):
            S.sp_program(sp, LAG)

        @block.gpsimd
        def _(pool):
            def step(s, n):
                q = n % 2
                if live(s, 1):
                    S.ln_pow(pool, s - 1, 1 - q, k["minus_half"])
                if live(s, 3):
                    t, p = s - 3, 1 - q
                    for hf in range(2):
                        pool.wait_ge(rinv_done, 2 * t + hf + 1)
                        ev = E[p][:, hf, :].rearrange("p (h k) -> p h k", k=SEQ)
                        nc.gpsimd.tensor_tensor(
                            ev, ev, rinv[p][:, 8 * hf:8 * hf + 8].unsqueeze(2).broadcast_to([P, 8, SEQ]),
                            ALU.mult).then_inc(p_done, 1)

            run_steps(pool, step, LAG)

        @block.tensor
        def _(pe):
            def project_t(t, n):
                ctxT = S.ctxT[:, n, :]
                pe.wait_ge(S.xT_done, t + 1)
                if n % 2 == 0:
                    pe.wait_ge(S.ctx_loaded[n // 2], moved(t, n))
                for i in range(4):
                    if i < 2:
                        if exists(t - 1):
                            pe.wait_ge(proj_copied, 8 * t + i - 1)
                    else:
                        pe.wait_ge(proj_copied, 8 * t + i - 1)
                    for h in range(4):
                        last = nc.tensor.matmul(psM[i % 2][:, h * P:(h + 1) * P], k["AT"][:, 4 * i + h, :],
                                                ctxT, start=True, stop=True)
                    last.then_inc(proj_done, 1)

            def project_u(t, n):
                ctxT = S.ctxT[:, n, :]
                for i in range(4):
                    pe.wait_ge(proj_copied, 8 * t + i + 3)
                    b, q4 = i // 2, 4 * (i % 2)
                    for j in range(2):
                        last = nc.tensor.matmul(psM[i % 2][64 * j:64 * j + 64, :], ctxT[:, 64 * b:64 * b + 64],
                                                k["B"][:, j, q4:q4 + 4, :], start=True, stop=True)
                    last.then_inc(proj_done, 1)

            def scores(t, p):
                for hf in range(2):
                    pe.wait_ge(proj_copied, 8 * t + 4)
                    if exists(t - 1):
                        pe.wait_ge(sub_done, 2 * t + hf - 1)
                    for b in range(NB):
                        last = nc.tensor.matmul(psS[hf][64 * b:64 * b + 64, :], S.xT[p][:, 64 * b:64 * b + 64],
                                                T[p][:, b, 8 * hf:8 * hf + 8, :], start=True, stop=True)
                    last.then_inc(s_done, 1)

            def transpose_p(t, p):
                for hf in range(2):
                    pe.wait_ge(p_done, 2 * t + hf + 1)
                    if exists(t - 1):
                        pe.wait_ge(pt_copied, 2 * t + hf - 1)
                    for i in range(4):
                        last = nc.tensor.transpose(psT[hf][:, i * P:(i + 1) * P], E[p][:, hf, i * P:(i + 1) * P],
                                                   k["ident"][:, :])
                    last.then_inc(ptr_done, 1)

            def values(t, p):
                if exists(t - 1):
                    pe.wait_ge(S.res_done, t)
                for i in range(PAIRS):
                    if i % 4 == 0:
                        pe.wait_ge(pt_copied, 2 * t + i // 4 + 1)
                    for b in range(NB):
                        last = nc.tensor.matmul(psO[64 * b:64 * b + 64, 0:P], PT[p][:, i, 64 * b:64 * b + 64],
                                                U[p][:, b, i, :], start=(i == 0), stop=(i == PAIRS - 1))
                last.then_inc(S.o_done, 1)

            def step(s, n):
                q = n % 2
                if live(s, 3):
                    project_t(s - 3, (n - 3) % SLOTS)
                if live(s, 4):
                    transpose_p(s - 4, q)
                if live(s, 3):
                    project_u(s - 3, (n - 3) % SLOTS)
                    scores(s - 3, 1 - q)
                if live(s, 2):
                    S.x_transpose(pe, s - 2, q, psX, k["ident"])
                if live(s, 4):
                    values(s - 4, q)

            run_steps(pe, step, LAG)

        @block.scalar
        def _(act):
            def step(s, n):
                q = n % 2
                if live(s, 3):
                    t, p = s - 3, 1 - q
                    if exists(t - 2):
                        act.wait_ge(s_done, 2 * t - 2)
                    for i in range(4):
                        act.wait_ge(proj_done, 8 * t + i + 1)
                        nc.scalar.copy(T[p][:, :, 4 * i:4 * i + 4, :].rearrange("p b h k -> p h b k"),
                                       psM[i % 2][:, :].rearrange("p (h b k) -> p h b k", h=4, b=NB))\
                            .then_inc(proj_copied, 1)
                if live(s, 4):
                    t, p = s - 4, q
                    if exists(t - 2):
                        act.wait_ge(S.o_done, t - 1)
                    for hf in range(2):
                        act.wait_ge(ptr_done, 2 * t + hf + 1)
                        nc.scalar.copy(PT[p][:, 4 * hf:4 * hf + 4, :].rearrange("p a b -> p (a b)"), psT[hf][:, :])\
                            .then_inc(pt_copied, 1)
                if live(s, 3):
                    t, p = s - 3, 1 - q
                    if exists(t - 2):
                        act.wait_ge(S.o_done, t - 1)
                    for i in range(4):
                        act.wait_ge(proj_done, 8 * t + i + 5)
                        b, q4 = i // 2, 4 * (i % 2)
                        nc.scalar.copy(U[p][:, b, q4:q4 + 4, :].rearrange("p a b -> p (a b)"), psM[i % 2][:, :])\
                            .then_inc(proj_copied, 1)
                if live(s, 2):
                    S.x_copy(act, s - 2, q, psX, s_done, 2)
                if live(s, 3):
                    t, p = s - 3, 1 - q
                    for hf in range(2):
                        act.wait_ge(sub_done, 2 * t + hf + 1)
                        nc.scalar.activation(E[p][:, hf, :], E[p][:, hf, :], ACT.Exp).then_inc(exp_done, 1)

            run_steps(act, step, LAG)

        @block.vector
        def _(dve):
            def step(s, n):
                q = n % 2
                if live(s, 2):
                    S.ln_norm(dve, s - 2, (n - 2) % SLOTS)
                if live(s, 1):
                    S.bn_first(dve, s - 1, (n - 1) % SLOTS)
                    S.bn_second(dve, s - 1, 1 - q)
                    S.bn_third(dve, s - 1, 1 - q)
                if live(s, 3):
                    softmax_max_sub(dve, nc, rmax, E, psS, s - 3, 1 - q, s_done, max_done, sub_done, ptr_done)
                    t, p = s - 3, 1 - q
                    for hf in range(2):
                        h8 = slice(8 * hf, 8 * hf + 8)
                        dve.wait_ge(exp_done, 2 * t + hf + 1)
                        if hf == 0:
                            if exists(t - 2):
                                dve.wait_ge(rinv_done, 2 * t - 2)
                        nc.vector.tensor_reduce(ssum[p][:, h8], E[p][:, hf, :].rearrange("p (h k) -> p h k", k=SEQ),
                                                AX.X, ALU.add).then_inc(sum_done, 1)
                        dve.wait_ge(sum_done, 2 * t + hf + 1)
                        if hf == 0:
                            if exists(t - 2):
                                dve.wait_ge(p_done, 2 * t - 2)
                        nc.vector.reciprocal(rinv[p][:, h8], ssum[p][:, h8]).then_inc(rinv_done, 1)
                if live(s, 4):
                    S.add_residual(dve, s - 4, (n - 4) % SLOTS, psO, load_gate(k, 1))

            run_steps(dve, step, LAG)


def layer1_ffn(nc, k, src, dst):
    LAG = 7
    with ExitStack() as c:
        S = Stream(nc, c, "f1", src, dst)
        top, topw, th_top, rwh, coef = (S.two(n, [P, 1]) for n in ("top", "topw", "th_top", "rwh", "coef"))
        ranks, pick = (S.two(n, [P, NE]) for n in ("ranks", "pick"))
        TH, A, Hd = (S.two(n, [P, HID]) for n in ("TH", "A", "Hd"))
        HT = S.two("HT", [P, HID])
        gate2 = S.sb("gate2", [P, 1])
        psX, psL, psT, psO = (S.bank(n) for n in ("psX", "psL", "psT", "psO"))
        psG = [S.bank(f"psG{i}") for i in range(2)]
        psU = [S.bank(f"psU{i}") for i in range(2)]
        ready, l_done, g_done, u_done, top_done, ranks_done, topw_done, pick_done, thtop_done, rwh_done, \
            TH_done, A_done, H_done, picked, coef_done, htr_done, hT_done = (S.sem(n) for n in (
                "ready", "l_done", "g_done", "u_done", "top_done", "ranks_done", "topw_done", "pick_done",
                "thtop_done", "rwh_done", "TH_done", "A_done", "H_done", "picked", "coef_done", "htr_done",
                "hT_done"))
        block = c.enter_context(nc.Block())

        @block.sync
        def _(sp):
            S.sp_program(sp, LAG)

        @block.gpsimd
        def _(pool):
            def step(s, n):
                q = n % 2
                if live(s, 5):
                    t, p = s - 5, 1 - q
                    pool.wait_ge(H_done, t + 1)
                    pool.wait_ge(pick_done, t + 1)
                    hv = Hd[p][:, :].rearrange("p (e i) -> p e i", e=NE)
                    nc.gpsimd.tensor_tensor(hv, hv, pick[p][:, :].unsqueeze(2).broadcast_to([P, NE, HID // NE]),
                                            ALU.mult).then_inc(picked, 1)
                if live(s, 1):
                    S.ln_pow(pool, s - 1, 1 - q, k["minus_half"])

            run_steps(pool, step, LAG)

        @block.tensor
        def _(pe):
            def up(t, p):
                pe.wait_ge(S.xT_done, t + 1)
                if exists(t - 2):
                    pe.wait_ge(A_done, t - 1)
                nc.tensor.matmul(psG[p][:, :], S.xT[p][:, :], k["l1_wgT"][:, :], start=True, stop=True)\
                    .then_inc(g_done, 1)
                if exists(t - 2):
                    pe.wait_ge(H_done, t - 1)
                nc.tensor.matmul(psU[p][:, :], S.xT[p][:, :], k["l1_wuT"][:, :], start=True, stop=True)\
                    .then_inc(u_done, 1)
                if exists(t - 1):
                    pe.wait_ge(ranks_done, t)
                nc.tensor.matmul(psL[:, 0:NE], S.xT[p][:, :], k["l1_gateT"][:, :], start=True, stop=True)\
                    .then_inc(l_done, 1)

            def transpose_h(t, p):
                pe.wait_ge(picked, t + 1)
                if exists(t - 1):
                    pe.wait_ge(hT_done, t)
                for i in range(CH):
                    last = nc.tensor.transpose(psT[:, i * P:(i + 1) * P], Hd[p][:, i * P:(i + 1) * P], k["ident"][:, :])
                last.then_inc(htr_done, 1)

            def down(t, p):
                pe.wait_ge(hT_done, t + 1)
                if exists(t - 1):
                    pe.wait_ge(S.res_done, t)
                for i in range(CH):
                    last = nc.tensor.matmul(psO[:, 0:P], HT[p][:, i * P:(i + 1) * P], k["l1_wdT"][:, i, :],
                                            start=(i == 0), stop=(i == CH - 1))
                last.then_inc(S.o_done, 1)

            def step(s, n):
                q = n % 2
                if live(s, 7):
                    down(s - 7, 1 - q)
                if live(s, 6):
                    transpose_h(s - 6, q)
                if live(s, 2):
                    S.x_transpose(pe, s - 2, q, psX, k["ident"])
                if live(s, 3):
                    up(s - 3, 1 - q)

            run_steps(pe, step, LAG)

        @block.scalar
        def _(act):
            def step(s, n):
                q = n % 2
                if live(s, 6):
                    t, p = s - 6, q
                    act.wait_ge(htr_done, t + 1)
                    if exists(t - 2):
                        act.wait_ge(S.o_done, t - 1)
                    nc.scalar.copy(HT[p][:, :], psT[:, :]).then_inc(hT_done, 1)
                if live(s, 2):
                    S.x_copy(act, s - 2, q, psX, l_done, 1)
                if live(s, 4):
                    t, p = s - 4, q
                    act.wait_ge(top_done, t + 1)
                    if exists(t - 2):
                        act.wait_ge(rwh_done, t - 1)
                    nc.scalar.activation(th_top[p][:, :], top[p][:, :], ACT.Tanh, scale=0.5).then_inc(thtop_done, 1)
                    act.wait_ge(rwh_done, t + 1)
                    act.wait_ge(g_done, t + 1)
                    if exists(t - 2):
                        act.wait_ge(A_done, t - 1)
                    nc.scalar.activation(TH[p][:, :], psG[p][:, :], ACT.Tanh, scale=rwh[p][:, :]).then_inc(TH_done, 1)

            run_steps(act, step, LAG)

        @block.vector
        def _(dve):
            nc.vector.tensor_scalar_mul(gate2[:, :], load_gate(k, 5), 2.0).then_inc(ready, 1)
            dve.wait_ge(ready, 1)

            def step(s, n):
                q = n % 2
                t4, p4 = s - 4, q
                t5, p5 = s - 5, 1 - q
                if live(s, 5):
                    dve.wait_ge(TH_done, t5 + 1)
                    if exists(t5 - 2):
                        dve.wait_ge(H_done, t5 - 1)
                    nc.vector.scalar_tensor_tensor(A[p5][:, :], TH[p5][:, :], 1.0, psG[p5][:, :], ALU.add, ALU.mult)\
                        .then_inc(A_done, 1)
                if live(s, 2):
                    S.ln_norm(dve, s - 2, (n - 2) % SLOTS)
                if live(s, 4):
                    dve.wait_ge(l_done, t4 + 1)
                    if exists(t4 - 2):
                        dve.wait_ge(thtop_done, t4 - 1)
                    if exists(t4 - 2):
                        dve.wait_ge(ranks_done, t4 - 1)
                    nc.vector.tensor_reduce(top[p4][:, :], psL[:, 0:NE], AX.X, ALU.max).then_inc(top_done, 1)
                if live(s, 5):
                    dve.wait_ge(A_done, t5 + 1)
                    dve.wait_ge(u_done, t5 + 1)
                    if exists(t5 - 2):
                        dve.wait_ge(htr_done, t5 - 1)
                    nc.vector.tensor_tensor(Hd[p5][:, :], psU[p5][:, :], A[p5][:, :], ALU.mult).then_inc(H_done, 1)
                if live(s, 4):
                    dve.wait_ge(top_done, t4 + 1)
                    nc.vector.scalar_tensor_tensor(ranks[p4][:, :], psL[:, 0:NE], top[p4][:, :], k["desc"][:, :],
                                                   ALU.is_equal, ALU.mult).then_inc(ranks_done, 1)
                if live(s, 7):
                    dve.wait_ge(coef_done, s - 6)
                    S.add_residual(dve, s - 7, (n - 7) % SLOTS, psO, coef[1 - q][:, :])
                if live(s, 4):
                    dve.wait_ge(thtop_done, t4 + 1)
                    if exists(t4 - 2):
                        dve.wait_ge(TH_done, t4 - 1)
                    if exists(t4 - 2):
                        dve.wait_ge(coef_done, t4 - 1)
                    nc.vector.tensor_scalar(rwh[p4][:, :], th_top[p4][:, :], 1.0, 0.25, ALU.add, ALU.mult)\
                        .then_inc(rwh_done, 1)
                    dve.wait_ge(ranks_done, t4 + 1)
                    nc.vector.tensor_reduce(topw[p4][:, :], ranks[p4][:, :], AX.X, ALU.max).then_inc(topw_done, 1)
                if live(s, 1):
                    S.bn_first(dve, s - 1, (n - 1) % SLOTS)
                if live(s, 4):
                    dve.wait_ge(topw_done, t4 + 1)
                    if exists(t4 - 2):
                        dve.wait_ge(picked, t4 - 1)
                    nc.vector.tensor_scalar(pick[p4][:, :], ranks[p4][:, :], topw[p4][:, :], None, ALU.is_equal)\
                        .then_inc(pick_done, 1)
                if live(s, 1):
                    S.bn_second(dve, s - 1, 1 - q)
                if live(s, 1):
                    S.bn_third(dve, s - 1, 1 - q)
                if live(s, 5):
                    dve.wait_ge(rwh_done, t5 + 1)
                    if exists(t5 - 2):
                        dve.wait_ge(S.res_done, t5 - 1)
                    nc.vector.tensor_scalar(coef[p5][:, :], rwh[p5][:, :], rwh[p5][:, :], gate2[:, :],
                                            ALU.mult, ALU.mult).then_inc(coef_done, 1)

            run_steps(dve, step, LAG)


def small_head_attention(nc, k, name, src, dst, ctx, w, rotary, gate):
    LAG = 7
    G = NH // 4
    with ExitStack() as c:
        S = Stream(nc, c, name, src, dst, ctx)
        QK = S.two("QK", [P, 2, P] if rotary else [P, 1, P])
        Qj = S.two("Qj", [P, 4, P])
        Kg = S.two("Kg", [P, NB, G, SEQ])
        V = S.two("V", [P, NB, NH, 9])
        E = S.two("E", [P, 2, 512])
        PT = S.two("PT", [P, PAIRS, P])
        on, oT = S.two("on", [P, P]), S.two("oT", [P, P])
        rmax, rinv = S.two("rmax", [P, NH]), S.two("rinv", [P, NH])
        if rotary:
            rc, rs = S.two("rc", [P, 2, P]), S.two("rs", [P, 2, P])
        psX, psQK, psV, psO = S.bank("psX"), S.bank("psQK"), S.bank("psV"), S.bank("psO")
        psS = [S.bank(f"psS{i}") for i in range(2)]
        psT = [S.bank(f"psT{i}") for i in range(2)]
        o9 = psO[:, P:P + 9 * NH].rearrange("p (h e) -> p h e", e=9)
        ready, qk_done, qk_ready, qj_ready, kg_ready, v_done, v_copied, rc_done, rs_done, s_done, max_done, \
            sub_done, exp_done, ptr_done, pt_copied, pv_done, rinv_done, on_done, otr_done, oT_done = (
                S.sem(n) for n in (
                    "ready", "qk_done", "qk_ready", "qj_ready", "kg_ready", "v_done", "v_copied", "rc_done",
                    "rs_done", "s_done", "max_done", "sub_done", "exp_done", "ptr_done", "pt_copied", "pv_done",
                    "rinv_done", "on_done", "otr_done", "oT_done"))
        S.ctx_used = v_done, 1
        block = c.enter_context(nc.Block())

        @block.sync
        def _(sp):
            S.sp_program(sp, LAG)

        @block.gpsimd
        def _(pool):
            for p in range(2):
                nc.gpsimd.memset(Kg[p][:, :, :, :], 0.0).then_inc(ready, 1)
                for j in range(2):
                    r = slice(64 * j, 64 * j + 64)
                    pool.wait_ge(ready, 5 * p + 2 * j + 1)
                    nc.gpsimd.memset(V[p][r, :, j::2, 8:9], 1.0).then_inc(ready, 1)
                    pool.wait_ge(ready, 5 * p + 2 * j + 2)
                    nc.gpsimd.memset(V[p][r, :, 1 - j::2, 8:9], 0.0).then_inc(ready, 1)
                pool.wait_ge(ready, 5 * p + 5)

            def step(s, n):
                q = n % 2
                if live(s, 3):
                    t, p = s - 3, 1 - q
                    pool.wait_ge(qk_ready, t + 1)
                    if exists(t - 2):
                        pool.wait_ge(s_done, 2 * t - 2)
                    nc.gpsimd.tensor_tensor(Qj[p][:, :, :], QK[p][:, 0:1, :].broadcast_to([P, 4, P]),
                                            k["jmask"][:, :].unsqueeze(2).broadcast_to([P, 4, P]), ALU.mult)\
                        .then_inc(qj_ready, 1)
                if live(s, 1):
                    S.ln_pow(pool, s - 1, 1 - q, k["minus_half"])

            run_steps(pool, step, LAG)

        @block.tensor
        def _(pe):
            pe.wait_ge(ready, 10)

            def project_qk(t, n):
                p, ctxT = n % 2, S.ctxT[:, n, :]
                pe.wait_ge(S.xT_done, t + 1)
                if n % 2 == 0:
                    pe.wait_ge(S.ctx_loaded[n // 2], moved(t, n))
                if exists(t - 1):
                    pe.wait_ge(qk_ready, t)
                if not rotary:
                    if exists(t - 1):
                        pe.wait_ge(kg_ready, G * t)
                nc.tensor.matmul(psQK[:, 0:P], k[w + "wqT"][:, :], S.xT[p][:, :], start=True, stop=True)
                if rotary:
                    nc.tensor.matmul(psQK[:, 2 * P:3 * P], k[w + "wqrT"][:, :], S.xT[p][:, :], start=True, stop=True)
                    nc.tensor.matmul(psQK[:, 3 * P:4 * P], k[w + "wkrT"][:, :], ctxT, start=True, stop=True)
                nc.tensor.matmul(psQK[:, P:2 * P], k[w + "wkT"][:, :], ctxT, start=True, stop=True)\
                    .then_inc(qk_done, 1)

            def project_v(t, n):
                if exists(t - 1):
                    pe.wait_ge(v_copied, t)
                for b in range(NB):
                    for j in range(2):
                        last = nc.tensor.matmul(psV[64 * j:64 * j + 64, b * P:(b + 1) * P],
                                                S.ctxT[:, n, 64 * b:64 * b + 64], k[w + "wvT2"][:, j, :],
                                                start=True, stop=True)
                last.then_inc(v_done, 1)

            def scores(t, p):
                pe.wait_ge(kg_ready, G * t + G)
                pe.wait_ge(qj_ready, t + 1)
                for hf in range(2):
                    if exists(t - 1):
                        pe.wait_ge(sub_done, 2 * t + hf - 1)
                    sv = psS[hf][:, :].rearrange("p (g j k) -> p g j k", g=G, j=2)
                    for j in range(2):
                        for b in range(NB):
                            last = nc.tensor.matmul(sv[64 * b:64 * b + 64, :, j, :],
                                                    Qj[p][:, 2 * hf + j, 64 * b:64 * b + 64],
                                                    Kg[p][:, b, :, :], start=True, stop=True)
                    last.then_inc(s_done, 1)

            def transpose_p(t, p):
                for hf in range(2):
                    pe.wait_ge(exp_done, 2 * t + hf + 1)
                    if exists(t - 1):
                        pe.wait_ge(pt_copied, 2 * t + hf - 1)
                    for i in range(4):
                        last = nc.tensor.transpose(psT[hf][:, i * P:(i + 1) * P], E[p][:, hf, i * P:(i + 1) * P],
                                                   k["ident"][:, :])
                    last.then_inc(ptr_done, 1)

            def values(t, p):
                pe.wait_ge(v_copied, t + 1)
                if exists(t - 1):
                    pe.wait_ge(on_done, t)
                if exists(t - 2):
                    pe.wait_ge(S.res_done, t - 1)
                for hf in range(2):
                    pe.wait_ge(pt_copied, 2 * t + hf + 1)
                    for g in range(G):
                        h = 4 * g + 2 * hf
                        for b in range(NB):
                            last = nc.tensor.matmul(o9[64 * b:64 * b + 64, h:h + 2, :],
                                                    PT[p][:, G * hf + g, 64 * b:64 * b + 64], V[p][:, b, h:h + 2, :],
                                                    start=True, stop=True)
                last.then_inc(pv_done, 1)

            def out_transpose(t, p):
                pe.wait_ge(on_done, t + 1)
                if exists(t - 1):
                    pe.wait_ge(oT_done, t)
                last_normed = min(t + 3, NT - 1) if isinstance(t, int) else t + 3
                pe.wait_ge(S.xT_done, last_normed + 1)
                nc.tensor.transpose(psX[:, P:2 * P], on[p][:, :], k["ident"][:, :]).then_inc(otr_done, 1)

            def out_project(t, p):
                pe.wait_ge(oT_done, t + 1)
                if exists(t - 1):
                    pe.wait_ge(S.res_done, t)
                last = nc.tensor.matmul(psO[:, 0:P], oT[p][:, :], k[w + "woT"][:, :], start=True, stop=rotary)
                if not rotary:
                    last = nc.tensor.matmul(psO[:, 0:P], k["ones_bf"][:, :], k["bias3"][:, HID:HID + P],
                                            start=False, stop=True)
                last.then_inc(S.o_done, 1)

            def step(s, n):
                q = n % 2
                if live(s, 3):
                    project_qk(s - 3, (n - 3) % SLOTS)
                if live(s, 4):
                    scores(s - 4, q)
                if live(s, 5):
                    transpose_p(s - 5, 1 - q)
                if live(s, 6):
                    out_transpose(s - 6, q)
                if live(s, 2):
                    S.x_transpose(pe, s - 2, q, psX, k["ident"])
                if live(s, 3):
                    project_v(s - 3, (n - 3) % SLOTS)
                if live(s, 5):
                    values(s - 5, 1 - q)
                if live(s, 6):
                    out_project(s - 6, q)

            run_steps(pe, step, LAG)

        @block.scalar
        def _(act):
            act.wait_ge(ready, 10)

            def step(s, n):
                q = n % 2
                if live(s, 3) and not rotary:
                    t, p = s - 3, 1 - q
                    act.wait_ge(qk_done, t + 1)
                    if exists(t - 2):
                        act.wait_ge(qj_ready, t - 1)
                    nc.scalar.activation(QK[p][:, 0, :], psQK[:, 0:P], ACT.Identity, bias=k[w + "bq"][:, :],
                                         scale=8.0 ** -0.5).then_inc(qk_ready, 1)
                    if exists(t - 2):
                        act.wait_ge(s_done, 2 * t - 2)
                    for g in range(G):
                        r = slice(32 * g, 32 * g + 32)
                        nc.scalar.activation(Kg[p][r, :, g, :],
                                             psQK[r, P:2 * P].rearrange("p (b k) -> p b k", b=NB),
                                             ACT.Identity, bias=k[w + "bk"][r, :]).then_inc(kg_ready, 1)
                if live(s, 5):
                    t, p = s - 5, 1 - q
                    if exists(t - 2):
                        act.wait_ge(pv_done, t - 1)
                    for hf in range(2):
                        act.wait_ge(ptr_done, 2 * t + hf + 1)
                        nc.scalar.copy(PT[p][:, 4 * hf:4 * hf + 4, :].rearrange("p a b -> p (a b)"), psT[hf][:, :])\
                            .then_inc(pt_copied, 1)
                if live(s, 6):
                    t, p = s - 6, q
                    act.wait_ge(otr_done, t + 1)
                    if live(s, 2):
                        act.wait_ge(S.xtr_done, s - 1)
                    if exists(t - 2):
                        act.wait_ge(S.o_done, t - 1)
                    if rotary:
                        nc.scalar.copy(oT[p][:, :], psX[:, P:2 * P]).then_inc(oT_done, 1)
                    else:
                        nc.scalar.activation(oT[p][:, :], psX[:, P:2 * P], ACT.Identity, bias=k[w + "bv"][:, :])\
                            .then_inc(oT_done, 1)
                if live(s, 2):
                    t, p = s - 2, q
                    act.wait_ge(S.xtr_done, t + 1)
                    if exists(t - 2):
                        act.wait_ge(qk_done, t - 1)
                    nc.scalar.copy(S.xT[p][:, :], psX[:, 0:P]).then_inc(S.xT_done, 1)
                if live(s, 3) and rotary:
                    t, p = s - 3, 1 - q
                    act.wait_ge(qk_ready, t + 1)
                    if exists(t - 2):
                        act.wait_ge(s_done, 2 * t - 2)
                    for g in range(G):
                        r = slice(32 * g, 32 * g + 32)
                        nc.scalar.copy(Kg[p][r, :, g, :], QK[p][r, 1, :].rearrange("p (b k) -> p b k", b=NB))\
                            .then_inc(kg_ready, 1)
                if live(s, 4):
                    t, p = s - 4, q
                    act.wait_ge(sub_done, 2 * t + 1)
                    nc.scalar.activation(E[p][:, 0, :], E[p][:, 0, :], ACT.Exp).then_inc(exp_done, 1)
                    act.wait_ge(sub_done, 2 * t + 2)
                    nc.scalar.activation(E[p][:, 1, :], E[p][:, 1, :], ACT.Exp).then_inc(exp_done, 1)
                if live(s, 3):
                    t, p = s - 3, 1 - q
                    act.wait_ge(v_done, t + 1)
                    if exists(t - 2):
                        act.wait_ge(pv_done, t - 1)
                    nc.scalar.copy(V[p][:, :, :, 0:8], psV[:, 0:2 * P].rearrange("p (b h e) -> p b h e", b=NB, e=8))\
                        .then_inc(v_copied, 1)

            run_steps(act, step, LAG)

        @block.vector
        def _(dve):
            dve.wait_ge(ready, 10)

            def rotate(t, p):
                qk = psQK[:, 0:2 * P].rearrange("p (a s) -> p a s", a=2)
                qk_swapped = psQK[:, 2 * P:4 * P].rearrange("p (a s) -> p a s", a=2)
                dve.wait_ge(qk_done, t + 1)
                if exists(t - 2):
                    dve.wait_ge(qk_ready, t - 1)
                nc.vector.tensor_tensor(rc[p][:, :, :], qk, k["rope"][:, 0, :, :], ALU.mult).then_inc(rc_done, 1)
                nc.vector.tensor_tensor(rs[p][:, :, :], qk_swapped, k["rope"][:, 1, :, :], ALU.mult).then_inc(rs_done, 1)
                dve.wait_ge(rc_done, t + 1)
                dve.wait_ge(rs_done, t + 1)
                if exists(t - 2):
                    dve.wait_ge(qj_ready, t - 1)
                if exists(t - 2):
                    dve.wait_ge(kg_ready, G * (t - 1))
                nc.vector.tensor_tensor(QK[p][:, :, :], rc[p][:, :, :], rs[p][:, :, :], ALU.add).then_inc(qk_ready, 1)

            def step(s, n):
                q = n % 2
                if live(s, 2):
                    S.ln_norm(dve, s - 2, (n - 2) % SLOTS)
                if live(s, 7):
                    S.add_residual(dve, s - 7, (n - 7) % SLOTS, psO, load_gate(k, gate))
                t, p = s - 6, q
                if live(s, 6):
                    dve.wait_ge(pv_done, t + 1)
                    if exists(t - 2):
                        dve.wait_ge(on_done, t - 1)
                    nc.vector.reciprocal(rinv[p][:, :].unsqueeze(2), o9[:, :, 8:9]).then_inc(rinv_done, 1)
                if live(s, 1):
                    S.bn_first(dve, s - 1, (n - 1) % SLOTS)
                if live(s, 6):
                    dve.wait_ge(rinv_done, t + 1)
                    if exists(t - 2):
                        dve.wait_ge(otr_done, t - 1)
                    nc.vector.tensor_tensor(on[p][:, :].rearrange("p (h e) -> p h e", e=8), o9[:, :, 0:8],
                                            rinv[p][:, :].unsqueeze(2).broadcast_to([P, NH, 8]), ALU.mult)\
                        .then_inc(on_done, 1)
                if live(s, 3) and rotary:
                    rotate(s - 3, 1 - q)
                if live(s, 1):
                    S.bn_second(dve, s - 1, 1 - q)
                if live(s, 4):
                    softmax_max_sub(dve, nc, rmax, E, psS, s - 4, q, s_done, max_done, sub_done, ptr_done)
                if live(s, 1):
                    S.bn_third(dve, s - 1, 1 - q)

            run_steps(dve, step, LAG)


def layer2_ffn(nc, k, src, dst):
    LAG = 5
    with ExitStack() as c:
        S = Stream(nc, c, "f2", src, dst)
        xpad = S.two("xpad", [P, NB, SEQ + 1])
        thr, kr, k2, mixed = (S.two(n, [P, P]) for n in ("thr", "kr", "k2", "mixed"))
        psX, psR, psK, psO = (S.bank(n) for n in ("psX", "psR", "psK", "psO"))
        ready, r_done, k_done, thr_done, kr_done, k2_done, mixed_done = (S.sem(n) for n in (
            "ready", "r_done", "k_done", "thr_done", "kr_done", "k2_done", "mixed_done"))
        block = c.enter_context(nc.Block())

        @block.sync
        def _(sp):
            S.sp_program(sp, LAG)

        @block.gpsimd
        def _(pool):
            for p in range(2):
                nc.gpsimd.memset(xpad[p][:, :, :], 0.0).then_inc(ready, 1)

            def step(s, n):
                q = n % 2
                if live(s, 1):
                    S.ln_pow(pool, s - 1, 1 - q, k["minus_half"])

            run_steps(pool, step, LAG)

        @block.tensor
        def _(pe):
            pe.wait_ge(ready, 2)

            def hidden(t, p):
                now, before = xpad[p][:, :, 1:1 + SEQ], xpad[p][:, :, 0:SEQ]
                pe.wait_ge(S.xT_done, t + 1)
                if exists(t - 1):
                    pe.wait_ge(thr_done, t)
                for x, wx, first in ((now, "wr0", True), (before, "wr1", False)):
                    for b in range(NB):
                        last = nc.tensor.matmul(psR[64 * b:64 * b + 64, 0:P], x[:, b, :], k[wx][:, :],
                                                start=first, stop=not first)
                last.then_inc(r_done, 1)
                if exists(t - 1):
                    pe.wait_ge(kr_done, t)
                psk = psK[:, 0:P].rearrange("p (b s) -> p b s", b=NB)
                nc.tensor.matmul(psk, k["wk0"][:, :], now, start=True, stop=False)
                nc.tensor.matmul(psk, k["wk1"][:, :], before, start=False, stop=True).then_inc(k_done, 1)

            def step(s, n):
                q = n % 2
                if live(s, 5):
                    t, p = s - 5, 1 - q
                    pe.wait_ge(k2_done, t + 1)
                    if exists(t - 1):
                        pe.wait_ge(mixed_done, t)
                    nc.tensor.matmul(psO[:, 0:P], k2[p][:, :], k["l2_wvfT"][:, :], start=True, stop=True)\
                        .then_inc(S.o_done, 1)
                if live(s, 3):
                    hidden(s - 3, 1 - q)
                if live(s, 2):
                    S.x_transpose(pe, s - 2, q, psX, k["ident"])

            run_steps(pe, step, LAG)

        @block.scalar
        def _(act):
            act.wait_ge(ready, 2)

            def step(s, n):
                q = n % 2
                if live(s, 3):
                    t, p = s - 3, 1 - q
                    act.wait_ge(r_done, t + 1)
                    if exists(t - 2):
                        act.wait_ge(mixed_done, t - 1)
                    nc.scalar.activation(thr[p][:, :], psR[:, 0:P], ACT.Tanh, scale=0.5).then_inc(thr_done, 1)
                if live(s, 2):
                    t, p = s - 2, q
                    act.wait_ge(S.xtr_done, t + 1)
                    if exists(t - 2):
                        act.wait_ge(k_done, t - 1)
                    nc.scalar.copy(xpad[p][:, :, 1:1 + SEQ], psX[:, 0:P].rearrange("p (b s) -> p b s", b=NB))\
                        .then_inc(S.xT_done, 1)
                if live(s, 3):
                    t, p = s - 3, 1 - q
                    act.wait_ge(k_done, t + 1)
                    if exists(t - 2):
                        act.wait_ge(k2_done, t - 1)
                    nc.scalar.activation(kr[p][:, :], psK[:, 0:P], ACT.Relu).then_inc(kr_done, 1)

            run_steps(act, step, LAG)

        @block.vector
        def _(dve):
            def step(s, n):
                q = n % 2
                if live(s, 1):
                    S.bn_first(dve, s - 1, (n - 1) % SLOTS)
                if live(s, 5):
                    t, p = s - 5, 1 - q
                    dve.wait_ge(S.o_done, t + 1)
                    dve.wait_ge(thr_done, t + 1)
                    if exists(t - 2):
                        dve.wait_ge(S.res_done, t - 1)
                    nc.vector.scalar_tensor_tensor(mixed[p][:, :], thr[p][:, :], 1.0, psO[:, 0:P], ALU.add, ALU.mult)\
                        .then_inc(mixed_done, 1)
                if live(s, 2):
                    S.ln_norm(dve, s - 2, (n - 2) % SLOTS)
                if live(s, 1):
                    S.bn_second(dve, s - 1, 1 - q)
                if live(s, 4):
                    t, p = s - 4, q
                    dve.wait_ge(kr_done, t + 1)
                    if exists(t - 2):
                        dve.wait_ge(S.o_done, t - 1)
                    nc.vector.tensor_tensor(k2[p][:, :], kr[p][:, :], kr[p][:, :], ALU.mult).then_inc(k2_done, 1)
                if live(s, 1):
                    S.bn_third(dve, s - 1, 1 - q)
                if live(s, 5):
                    dve.wait_ge(mixed_done, s - 4)
                    S.add_residual(dve, s - 5, (n - 5) % SLOTS, mixed[1 - q], k["half_gate"][:, 6:7])

            run_steps(dve, step, LAG)


def layer3_ffn(nc, k, src, dst):
    LAG = 4
    with ExitStack() as c:
        S = Stream(nc, c, "f3", src, dst)
        lead = S.two("lead", [P, 32])
        t1 = S.two("t1", [P, P])
        t2 = S.two("t2", [P, P])
        down_rows = S.two("down_rows", [P, P])
        Hd = S.two("Hd", [P, HID])
        psX, psA, psB, psH, psD, psO = (S.bank(n) for n in ("psX", "psA", "psB", "psH", "psD", "psO"))
        ready, ab_done, t1_done, up_done, rows_done, h_done, gelu_done, d_done, t2_done, copied = (S.sem(n) for n in (
            "ready", "ab_done", "t1_done", "up_done", "rows_done", "h_done", "gelu_done", "d_done", "t2_done", "copied"))
        block = c.enter_context(nc.Block())

        @block.sync
        def _(sp):
            S.sp_program(sp, LAG)

        @block.gpsimd
        def _(pool):
            for p in range(2):
                nc.gpsimd.memset(t1[p][:, :], 0.0).then_inc(ready, 1)
                pool.wait_ge(ready, 2 * p + 1)
                nc.gpsimd.memset(t1[p][32:33, :], 1.0).then_inc(ready, 1)
                pool.wait_ge(ready, 2 * p + 2)

            def step(s, n):
                q = n % 2
                if live(s, 1):
                    S.ln_pow(pool, s - 1, 1 - q, k["minus_half"])

            run_steps(pool, step, LAG)

        @block.tensor
        def _(pe):
            pe.wait_ge(ready, 4)

            def rank(t, p):
                pe.wait_ge(S.xT_done, t + 1)
                pe.wait_ge(copied, t + 1)
                if exists(t - 1):
                    pe.wait_ge(t1_done, t)
                if exists(t - 1):
                    pe.wait_ge(up_done, t)
                if exists(t - 1):
                    pe.wait_ge(rows_done, t)
                nc.tensor.matmul(psA[0:32, 0:P], lead[p][:, :], S.xT[p][:, :], start=True, stop=True)
                nc.tensor.matmul(psA[0:32, P:2 * P], k["sel_token"][:, :], S.xh[p][:, :], start=True, stop=True)
                xs = S.xh[p][:, :].rearrange("p (r j) -> p j r", j=CH)
                for j in range(CH):
                    last = nc.tensor.matmul(psB[32 * j:32 * j + 32, 0:32], k["sel_token"][:, :], xs[:, j, :],
                                            start=True, stop=True)
                last.then_inc(ab_done, 1)

            def hidden(t, p):
                pe.wait_ge(t1_done, t + 1)
                pe.wait_ge(up_done, t + 1)
                if exists(t - 1):
                    pe.wait_ge(gelu_done, t)
                for i in range(CH):
                    nc.tensor.matmul(psH[:, i * P:(i + 1) * P], k["l3_w1T"][:, i * P:(i + 1) * P], S.xT[p][:, :],
                                     start=True, stop=False)
                    last = nc.tensor.matmul(psH[:, i * P:(i + 1) * P], k["lora_up"][p][:, i * P:(i + 1) * P],
                                            t1[p][:, :], start=False, stop=True)
                last.then_inc(h_done, 1)

            def down_rank(t, p):
                pe.wait_ge(gelu_done, t + 1)
                if exists(t - 1):
                    pe.wait_ge(t2_done, t)
                for j in range(CH):
                    last = nc.tensor.matmul(psD[32 * j:32 * j + 32, 0:P], lead[p][:, :], Hd[p][:, j * P:(j + 1) * P],
                                            start=True, stop=True)
                last.then_inc(d_done, 1)

            def down(t, p):
                if exists(t - 1):
                    pe.wait_ge(S.res_done, t)
                for i in range(CH):
                    nc.tensor.matmul(psO[:, 0:P], Hd[p][:, i * P:(i + 1) * P], k["l3_w2T"][:, i, :],
                                     start=(i == 0), stop=False)
                nc.tensor.matmul(psO[:, 0:P], k["ones_bf"][:, :], k["bias3"][:, HID + P:HID + 2 * P],
                                 start=False, stop=False)

            def down_last(t, p):
                pe.wait_ge(t2_done, t + 1)
                pe.wait_ge(rows_done, t + 1)
                nc.tensor.matmul(psO[:, 0:P], t2[p][:, :], down_rows[p][:, :], start=False, stop=True)\
                    .then_inc(S.o_done, 1)

            def step(s, n):
                q = n % 2
                if live(s, 3):
                    rank(s - 3, 1 - q)
                if live(s, 4):
                    down_rank(s - 4, q)
                    down(s - 4, q)
                if live(s, 2):
                    S.x_transpose(pe, s - 2, q, psX, k["ident"])
                if live(s, 3):
                    hidden(s - 3, 1 - q)
                if live(s, 4):
                    down_last(s - 4, q)

            run_steps(pe, step, LAG)

        @block.scalar
        def _(act):
            def step(s, n):
                q = n % 2
                if live(s, 2):
                    t, p = s - 2, q
                    act.wait_ge(S.xtr_done, t + 1)
                    if exists(t - 2):
                        act.wait_ge(h_done, t - 1)
                    nc.scalar.copy(S.xT[p][:, :], psX[:, 0:P]).then_inc(copied, 1)
                    if exists(t - 2):
                        act.wait_ge(d_done, t - 1)
                    nc.scalar.copy(lead[p][:, :].rearrange("p (b s) -> p b s", b=NB),
                                   psX[:, 0:P].rearrange("p (b s) -> p b s", b=NB)[:, :, 1:17])\
                        .then_inc(S.xT_done, 1)
                if live(s, 3):
                    t, p = s - 3, 1 - q
                    act.wait_ge(h_done, t + 1)
                    if exists(t - 2):
                        act.wait_ge(S.o_done, t - 1)
                    nc.scalar.activation(Hd[p][:, :], psH[:, :], ACT.Gelu).then_inc(gelu_done, 1)

            run_steps(act, step, LAG)

        @block.vector
        def _(dve):
            def step(s, n):
                q = n % 2
                if live(s, 2):
                    if exists(s - 4):
                        dve.wait_ge(ab_done, s - 3)
                    S.ln_norm(dve, s - 2, (n - 2) % SLOTS)
                if live(s, 3):
                    t, p = s - 3, 1 - q
                    dve.wait_ge(ab_done, t + 1)
                    if exists(t - 2):
                        dve.wait_ge(h_done, t - 1)
                    nc.vector.tensor_tensor(t1[p][0:32, :], psA[0:32, 0:P], k["mask_up"][:, :], ALU.mult)\
                        .then_inc(t1_done, 1)
                    nc.vector.tensor_tensor(
                        k["lora_up"][p][0:32, :].rearrange("p (i c) -> p i c", i=CH),
                        psA[0:32, P:2 * P].unsqueeze(1).broadcast_to([32, CH, P]), k["sel_up"][:, :, :], ALU.mult)\
                        .then_inc(up_done, 1)
                if live(s, 1):
                    S.bn_first(dve, s - 1, (n - 1) % SLOTS)
                if live(s, 4):
                    t, p = s - 4, q
                    dve.wait_ge(d_done, t + 1)
                    if exists(t - 2):
                        dve.wait_ge(S.o_done, t - 1)
                    nc.vector.tensor_tensor(t2[p][:, :], psD[:, 0:P], k["mask_down"][:, :], ALU.mult)\
                        .then_inc(t2_done, 1)
                if live(s, 3):
                    t, p = s - 3, 1 - q
                    if exists(t - 2):
                        dve.wait_ge(S.o_done, t - 1)
                    nc.vector.tensor_tensor(
                        down_rows[p][:, :].rearrange("p (i r) -> p i r", i=CH),
                        psB[:, 0:32].unsqueeze(1).broadcast_to([P, CH, 32]), k["sel_down"][:, :, :], ALU.mult)\
                        .then_inc(rows_done, 1)
                if live(s, 1):
                    S.bn_second(dve, s - 1, 1 - q)
                    S.bn_third(dve, s - 1, 1 - q)
                if live(s, 4):
                    S.add_residual(dve, s - 4, (n - 4) % SLOTS, psO, load_gate(k, 7))

            run_steps(dve, step, LAG)


def build(nc, w, out):
    with ExitStack() as c:
        X = c.enter_context(nc.sbuf_tensor("residual", [P, NT * P], F32))
        k = prepare_first(nc, c, w)

        def x_tiles(row):
            return w["x"][bass.ds(row, 2 * P), :].rearrange("(a p) d -> p a d", a=2)

        def resident(row):
            return X[:, bass.ds(row, 2 * P)].rearrange("p (a d) -> p a d", a=2)

        def ctx_tiles(row):
            return w["ctxT"][:, bass.ds(row, 2 * P)].rearrange("p (a s) -> p a s", a=2)

        def out_tiles(row):
            return out[bass.ds(row, 2 * P), :].rearrange("(a p) d -> p a d", a=2)

        layer0_attention(nc, k, x_tiles, resident, ctx_tiles, w)
        layer0_ffn(nc, k, resident, resident, w)
        layer1_attention(nc, k, resident, resident, ctx_tiles)
        layer1_ffn(nc, k, resident, resident)
        small_head_attention(nc, k, "a2", resident, resident, ctx_tiles, "l2_", False, 2)
        layer2_ffn(nc, k, resident, resident)
        small_head_attention(nc, k, "a3", resident, resident, ctx_tiles, "l3_", True, 3)
        layer3_ffn(nc, k, resident, out_tiles)


def shape_constants():
    c = {}
    tok, seq = np.arange(P), np.arange(P) // SEQ
    c["ident"] = np.eye(P, dtype=np.float32)
    seen = (seq[:, None] == seq[None, :]) & (tok[None, :] <= tok[:, None])
    c["causal"] = np.where(seen, 0.0, -1e30).astype(np.float32)
    c["desc"] = np.broadcast_to(np.arange(NE, 0, -1, dtype=np.float32), (P, NE)).copy()
    row = np.arange(P)
    c["jmask"] = ((row // 8 % 4)[:, None] == np.arange(4)[None, :]).astype(np.float32)
    inv = (1.0 / 10000.0 ** (np.arange(0, 8, 2, dtype=np.float32) / 8)).astype(np.float32)
    angle = (tok % SEQ).astype(np.float32)[None, :] * inv[row % 4][:, None]
    sign = np.where(row % 8 < 4, -1.0, 1.0)[:, None]
    cos, sin = np.cos(angle), np.sin(angle) * sign
    q = 8.0 ** -0.5
    c["rope"] = np.stack([np.stack([cos * q, cos], 1), np.stack([sin * q, sin], 1)], 1).astype(np.float32)
    b32, n32 = np.arange(32) // 16, np.arange(32) % 16
    c["mask_up"] = ((b32[:, None] == seq[None, :]) & (n32 % 2 == 1)[:, None] & (n32 < 8)[:, None]).astype(np.float32)
    down = (b32[:, None] == seq[None, :]) & (n32 % 2 == 1)[:, None] & (n32 > 8)[:, None]
    c["mask_down"] = np.tile(down, (4, 1)).astype(np.float32)
    c["sel_token"] = (tok[:, None] == (SEQ * b32 + n32)[None, :]).astype(np.float32)
    i = np.arange(CH)
    c["sel_up"] = np.broadcast_to((n32[:, None] == 2 * i + 1)[:, :, None], (32, CH, P)).astype(np.float32)
    c["sel_down"] = np.broadcast_to(np.tile(n32[:, None] == 2 * i + 9, (4, 1))[:, :, None], (P, CH, 32))\
        .astype(np.float32)
    return c


def lay_out(v):
    def t(a):
        return np.ascontiguousarray(np.asarray(a).T)

    def rows(a):
        a = np.asarray(a)
        return np.ascontiguousarray(a.reshape(-1, P, a.shape[-1]).transpose(1, 0, 2))

    def parity(a):
        a = t(a).reshape(P, PAIRS, 2, 8)
        z = np.zeros((P, 2, PAIRS, 2, 8), a.dtype)
        for j in range(2):
            z[:, j, :, j, :] = a[:, :, j, :]
        return z.reshape(P, 2, P)

    swap = np.arange(P) ^ 4
    d = shape_constants()
    d["x"] = np.asarray(v["x"]).reshape(NT * P, P)
    d["ctxT"] = t(np.asarray(v["ctx_1024"]).reshape(NT * P, P))
    g = np.concatenate([np.asarray(v["g_xattn"]), np.asarray(v["g_ffn"])])
    d["gates"] = np.broadcast_to(g, (P, 8)).copy()
    d["l0_wqT"], d["l0_wkT"], d["l0_wv"] = t(v["L0_xattn_w_q"]), t(v["L0_xattn_w_k"]), np.asarray(v["L0_xattn_w_v"])
    d["l0_w1T"] = t(v["L0_ffn_w1"]).reshape(P, CH, P)
    d["l0_convw"] = np.broadcast_to(t(np.asarray(v["L0_ffn_conv_w"])[:, 0, :]), (P, 3, HID)).copy()
    d["row_biases"] = np.concatenate([np.asarray(v[n]) for n in ("L0_ffn_conv_b", "L2_xattn_bo", "L3_ffn_b2")])[None]
    d["l0_w2T"] = rows(t(v["L0_ffn_w2"]))
    for n in "qkv":
        d[f"l1_w{n}T"] = rows(t(np.asarray(v[f"L1_xattn_W{n}"]).reshape(P, -1)))
    d["l1_wo"] = rows(np.asarray(v["L1_xattn_Wo"]).reshape(-1, P))
    d["l1_gateT"] = t(v["L1_ffn_gate_w"])
    d["l1_wgT"] = t(np.asarray(v["L1_ffn_w_gate"]).reshape(HID, P))
    d["l1_wuT"] = t(np.asarray(v["L1_ffn_w_up"]).reshape(HID, P))
    d["l1_wdT"] = rows(np.asarray(v["L1_ffn_w_down"]).transpose(0, 2, 1).reshape(HID, P))
    for n in ("2", "3"):
        a = f"L{n}_xattn_W"
        d[f"l{n}_wqT"], d[f"l{n}_wkT"], d[f"l{n}_woT"] = t(v[a + "q"]), t(v[a + "k"]), t(v[a + "o"])
        d[f"l{n}_wvT2"] = parity(v[a + "v"])
    d["l3_wqrT"], d["l3_wkrT"] = t(np.asarray(v["L3_xattn_Wq"])[swap]), t(np.asarray(v["L3_xattn_Wk"])[swap])
    for n in "qkv":
        d["l2_b" + n] = np.asarray(v["L2_xattn_b" + n]).reshape(P, 1)
    d["l2_wrT"], d["l2_wkfT"], d["l2_wvfT"] = t(v["L2_ffn_W_r"]), t(v["L2_ffn_W_k"]), t(v["L2_ffn_W_v"])
    d["l2_mur"], d["l2_muk"] = np.asarray(v["L2_ffn_mu_r"]).reshape(P, 1), np.asarray(v["L2_ffn_mu_k"]).reshape(P, 1)
    d["l3_w1T"], d["l3_w2T"] = t(v["L3_ffn_W1"]), rows(t(v["L3_ffn_W2"]))
    d["l3_scale"] = np.broadcast_to(np.asarray(v["L3_ffn_scale"]).reshape(1, 1), (P, 1)).copy()
    for b in range(2):
        d[f"lora_up{b}"] = np.pad(np.asarray(v["L3_ffn_b1"])[None], ((32, P - 33), (0, 0)))

    def padded(name, shape):
        return np.pad(np.asarray(d[name]).reshape(shape[0], -1), ((0, P - shape[0]), (0, 0)))

    out = {pack: np.concatenate([padded(n, shape) for n, shape in shapes.items()], 1)
           for pack, shapes in PACKS.items()}
    for n in ("x", "ctxT", "row_biases"):
        out[n] = d[n]
    return {n: np.ascontiguousarray(a) for n, a in out.items()}


def kernel(**inputs):
    import concourse.bacc as bacc
    from concourse.bass_utils import run_bass_kernel_spmd

    nc = bacc.Bacc("TRN2", target_bir_lowering=False, num_devices=1)
    arrays, w = {}, {}
    for name, a in lay_out(inputs).items():
        arrays[f"in_{name}"] = a
        w[name] = nc.dram_tensor(f"in_{name}", a.shape, mybir.dt.from_np(a.dtype), kind="ExternalInput").ap()
    out = nc.dram_tensor("out_x", (NT * P, P), F32, kind="ExternalOutput").ap()
    build(nc, w, out)
    r = run_bass_kernel_spmd(nc, [arrays], core_ids=[0])
    return r.results[0]["out_x"].reshape(NT * P // SEQ, SEQ, P)
```
